# Optimizing a Trainium2 kernel written in Bass

```python
import numpy as np
import jax
import jax.numpy as jnp

def _softmax(x, axis=-1):
    return jax.nn.softmax(x, axis=axis)

def _gelu(x):
    return jax.nn.gelu(x, approximate=True)

def _silu(x):
    return jax.nn.silu(x)

def _sigmoid(x):
    return jax.nn.sigmoid(x)

def _layernorm(x, axis=-1, eps=1e-05):
    m = jnp.mean(x, axis=axis, keepdims=True)
    v = jnp.var(x, axis=axis, keepdims=True)
    return (x - m) / jnp.sqrt(v + eps)

def _scatter_add(tgt, idx, src, axis=0):
    return tgt.at[idx].add(src)

def _segment_sum(src, seg, n):
    return jax.ops.segment_sum(src, seg, n)
kernel_name = 'mk_gnn_preln_d4_gnn_r32_7243da'

def setup_inputs(seed: int=0):
    np.random.seed(seed)
    _w = jnp.asarray

    def _rec_inputs():
        import jax
        import jax.numpy as jnp
        _gk = jax.random.key(seed)
        x = -2.705e-05 + 0.03247 * jax.random.normal(jax.random.fold_in(_gk, 1), (3125, 128), jnp.float32)
        src = jax.random.randint(jax.random.fold_in(_gk, 2), (50000,), 0, 3125, jnp.int32)
        dst = jax.random.randint(jax.random.fold_in(_gk, 3), (50000,), 0, 3125, jnp.int32)
        _o = jnp.argsort(dst, stable=True)
        src = src[_o]
        dst = dst[_o]
        edge_weight1 = jax.random.uniform(jax.random.fold_in(_gk, 12), (50000, 1), jnp.float32, 0.0, 0.999998)
        return (x, src, dst, edge_weight1)
    x, src, dst, edge_weight1 = _rec_inputs()

    def _L0_gnn_setup():
        import jax, jax.numpy as jnp
        import numpy as np
        EPS = 1e-07
        N_NODES, N_EDGES, D = (10000, 5000, 128)

        def mobius_add(x, y):
            x2 = jnp.sum(x * x, axis=-1, keepdims=True)
            y2 = jnp.sum(y * y, axis=-1, keepdims=True)
            xy = jnp.sum(x * y, axis=-1, keepdims=True)
            num = (1.0 + 2.0 * xy + y2) * x + (1.0 - x2) * y
            den = 1.0 + 2.0 * xy + x2 * y2
            return num / jnp.maximum(den, EPS)

        def mobius_scalar_mul(r, x):
            nrm = jnp.sqrt(jnp.sum(x * x, axis=-1, keepdims=True))
            nrm_c = jnp.clip(nrm, EPS, 1.0 - EPS)
            scaled = jnp.tanh(r * jnp.arctanh(nrm_c)) * (x / nrm_c)
            return jnp.where(nrm > EPS, scaled, jnp.zeros_like(x))
        key = jax.random.key(seed)
        kx, ke = jax.random.split(key)
        raw = jax.random.normal(kx, (N_NODES, D), dtype=jnp.float32)
        x = 0.4 * raw / (1.0 + jnp.linalg.norm(raw, axis=-1, keepdims=True))
        edge_index = jax.random.randint(ke, (2, N_EDGES), 0, N_NODES, dtype=jnp.int64)
        return {'x': x, 'edge_index': edge_index}
    _L0_gnn_all = _L0_gnn_setup()
    _L0_gnn_in = {k: v for k, v in _L0_gnn_all.items() if k in ()}
    del _L0_gnn_all

    def _L1_gnn_setup():
        import jax, jax.numpy as jnp
        import numpy as np
        N = 50000
        E = 18750
        DIM = 128
        H = 4
        C = DIM // H
        NEG_SLOPE = 0.2
        LN_EPS = 1e-05
        key = jax.random.key(seed)
        ks = jax.random.split(key, 6)
        s = 1.0 / np.sqrt(DIM)
        x = jax.random.normal(ks[0], (N, DIM), jnp.float32)
        edge_index = jax.random.randint(ks[1], (2, E), 0, N, dtype=jnp.int64)
        W = jax.random.normal(ks[2], (DIM, H * C), jnp.float32) * s
        att_src = jax.random.normal(ks[3], (H, C), jnp.float32) * s
        att_dst = jax.random.normal(ks[4], (H, C), jnp.float32) * s
        bias = jnp.zeros((H * C,), jnp.float32)
        gamma = jnp.ones((DIM,), jnp.float32)
        beta = jnp.zeros((DIM,), jnp.float32)
        return {'x': x, 'W': W, 'att_src': att_src, 'att_dst': att_dst, 'bias': bias, 'gamma': gamma, 'beta': beta, 'edge_index': edge_index}
    _L1_gnn_all = _L1_gnn_setup()
    _L1_gnn_in = {k: v for k, v in _L1_gnn_all.items() if k in ('W', 'att_src', 'att_dst', 'bias', 'gamma', 'beta')}
    del _L1_gnn_all

    def _L2_gnn_setup():
        import jax, jax.numpy as jnp
        import numpy as np
        N, E, IN_DIM, HID, HEADS, LAYERS = (50000, 10000, 128, 128, 4, 2)
        C = HID // HEADS
        EPS = 1e-05

        def _init(key, shape, fan_in):
            return jax.random.normal(key, shape, dtype=jnp.float32) / np.sqrt(fan_in)

        def _transformer_conv(h, src, tgt, edge_attr, Wq, bq, Wk, bk, Wv, bv, We, Wskip, bskip, Wbeta):
            n = h.shape[0]
            q = (h @ Wq + bq).reshape(n, HEADS, C)
            k = (h @ Wk + bk).reshape(n, HEADS, C)
            v = (h @ Wv + bv).reshape(n, HEADS, C)
            e = (edge_attr @ We).reshape(-1, HEADS, C)
            k_j = k[src] + e
            alpha = jnp.einsum('ehc,ehc->eh', q[tgt], k_j) / jnp.sqrt(jnp.float32(C))
            amax = jax.ops.segment_max(alpha, tgt, num_segments=n)
            ex = jnp.exp(alpha - amax[tgt])
            denom = jax.ops.segment_sum(ex, tgt, num_segments=n)
            a = ex / denom[tgt]
            msg = (v[src] + e) * a[..., None]
            out = jax.ops.segment_sum(msg, tgt, num_segments=n).reshape(n, HID)
            x_r = h @ Wskip + bskip
            beta = jax.nn.sigmoid(jnp.concatenate([out, x_r, out - x_r], axis=-1) @ Wbeta)
            return beta * x_r + (1.0 - beta) * out

        def _batchnorm(h, gamma, beta):
            mu = h.mean(axis=0)
            var = h.var(axis=0)
            return gamma * (h - mu) * jax.lax.rsqrt(var + EPS) + beta
        key = jax.random.key(seed)
        ks = jax.random.split(key, 20)
        x = jax.random.normal(ks[0], (N, IN_DIM), dtype=jnp.float32)
        edge_index = jax.random.randint(ks[1], (2, E), 0, N, dtype=jnp.int64)
        edge_attr = jax.random.uniform(ks[2], (E, 1), dtype=jnp.float32)
        inp = {'x': x, 'edge_index': edge_index, 'edge_attr': edge_attr, 'W_in': _init(ks[3], (IN_DIM, HID), IN_DIM), 'b_in': jnp.zeros((HID,), jnp.float32), 'Wq': _init(ks[4], (LAYERS, HID, HID), HID), 'bq': jnp.zeros((LAYERS, HID), jnp.float32), 'Wk': _init(ks[5], (LAYERS, HID, HID), HID), 'bk': jnp.zeros((LAYERS, HID), jnp.float32), 'Wv': _init(ks[6], (LAYERS, HID, HID), HID), 'bv': jnp.zeros((LAYERS, HID), jnp.float32), 'We': _init(ks[7], (LAYERS, 1, HID), 1), 'Wskip': _init(ks[8], (LAYERS, HID, HID), HID), 'bskip': jnp.zeros((LAYERS, HID), jnp.float32), 'Wbeta': _init(ks[9], (LAYERS, 3 * HID, 1), 3 * HID), 'bn_gamma': jnp.ones((LAYERS, HID), jnp.float32), 'bn_beta': jnp.zeros((LAYERS, HID), jnp.float32)}
        return inp
    _L2_gnn_all = _L2_gnn_setup()
    _L2_gnn_in = {k: v for k, v in _L2_gnn_all.items() if k in ('W_in', 'b_in', 'Wq', 'bq', 'Wk', 'bk', 'Wv', 'bv', 'We', 'Wskip', 'bskip', 'Wbeta', 'bn_gamma', 'bn_beta')}
    del _L2_gnn_all

    def _L3_gnn_setup():
        import jax, jax.numpy as jnp
        import numpy as np
        N_NODES = 3125
        N_EDGES = 50000
        NODE_DIM = 128
        HIDDEN = 128
        N_LAYERS = 4
        LN_EPS = 1e-05

        def _layernorm(x, g, b):
            mu = jnp.mean(x, axis=-1, keepdims=True)
            var = jnp.mean(jnp.square(x - mu), axis=-1, keepdims=True)
            return (x - mu) * jax.lax.rsqrt(var + LN_EPS) * g + b
        key = jax.random.key(seed)
        ks = jax.random.split(key, 16)
        s = 1.0 / np.sqrt(HIDDEN)
        inp = {'x': jax.random.normal(ks[0], (N_NODES, NODE_DIM), dtype=jnp.float32), 'edge_index': jax.random.randint(ks[1], (2, N_EDGES), 0, N_NODES, dtype=jnp.int64), 'Wn': jax.random.normal(ks[2], (NODE_DIM, HIDDEN), dtype=jnp.float32) / np.sqrt(NODE_DIM), 'bn': jnp.zeros((HIDDEN,), dtype=jnp.float32), 'WQ': jax.random.normal(ks[3], (N_LAYERS, HIDDEN, HIDDEN), dtype=jnp.float32) * s, 'bQ': jnp.zeros((N_LAYERS, HIDDEN), dtype=jnp.float32), 'WK': jax.random.normal(ks[4], (N_LAYERS, HIDDEN, HIDDEN), dtype=jnp.float32) * s, 'bK': jnp.zeros((N_LAYERS, HIDDEN), dtype=jnp.float32), 'WV': jax.random.normal(ks[5], (N_LAYERS, HIDDEN, HIDDEN), dtype=jnp.float32) * s, 'bV': jnp.zeros((N_LAYERS, HIDDEN), dtype=jnp.float32), 'WO': jax.random.normal(ks[6], (N_LAYERS, HIDDEN, HIDDEN), dtype=jnp.float32) * s, 'bO': jnp.zeros((N_LAYERS, HIDDEN), dtype=jnp.float32), 'ln_g': jnp.ones((N_LAYERS, HIDDEN), dtype=jnp.float32), 'ln_b': jnp.zeros((N_LAYERS, HIDDEN), dtype=jnp.float32), 'Wout': jax.random.normal(ks[7], (HIDDEN, NODE_DIM), dtype=jnp.float32) * s, 'bout': jnp.zeros((NODE_DIM,), dtype=jnp.float32)}
        return inp
    _L3_gnn_all = _L3_gnn_setup()
    _L3_gnn_in = {k: v for k, v in _L3_gnn_all.items() if k in ('Wn', 'bn', 'WQ', 'bQ', 'WK', 'bK', 'WV', 'bV', 'WO', 'bO', 'ln_g', 'ln_b', 'Wout', 'bout')}
    del _L3_gnn_all
    return {'x': x, 'src': src, 'dst': dst, 'edge_weight1': edge_weight1, 'L1_gnn_W': _L1_gnn_in['W'], 'L1_gnn_att_src': _L1_gnn_in['att_src'], 'L1_gnn_att_dst': _L1_gnn_in['att_dst'], 'L1_gnn_bias': _L1_gnn_in['bias'], 'L1_gnn_gamma': _L1_gnn_in['gamma'], 'L1_gnn_beta': _L1_gnn_in['beta'], 'L2_gnn_W_in': _L2_gnn_in['W_in'], 'L2_gnn_b_in': _L2_gnn_in['b_in'], 'L2_gnn_Wq': _L2_gnn_in['Wq'], 'L2_gnn_bq': _L2_gnn_in['bq'], 'L2_gnn_Wk': _L2_gnn_in['Wk'], 'L2_gnn_bk': _L2_gnn_in['bk'], 'L2_gnn_Wv': _L2_gnn_in['Wv'], 'L2_gnn_bv': _L2_gnn_in['bv'], 'L2_gnn_We': _L2_gnn_in['We'], 'L2_gnn_Wskip': _L2_gnn_in['Wskip'], 'L2_gnn_bskip': _L2_gnn_in['bskip'], 'L2_gnn_Wbeta': _L2_gnn_in['Wbeta'], 'L2_gnn_bn_gamma': _L2_gnn_in['bn_gamma'], 'L2_gnn_bn_beta': _L2_gnn_in['bn_beta'], 'L3_gnn_Wn': _L3_gnn_in['Wn'], 'L3_gnn_bn': _L3_gnn_in['bn'], 'L3_gnn_WQ': _L3_gnn_in['WQ'], 'L3_gnn_bQ': _L3_gnn_in['bQ'], 'L3_gnn_WK': _L3_gnn_in['WK'], 'L3_gnn_bK': _L3_gnn_in['bK'], 'L3_gnn_WV': _L3_gnn_in['WV'], 'L3_gnn_bV': _L3_gnn_in['bV'], 'L3_gnn_WO': _L3_gnn_in['WO'], 'L3_gnn_bO': _L3_gnn_in['bO'], 'L3_gnn_ln_g': _L3_gnn_in['ln_g'], 'L3_gnn_ln_b': _L3_gnn_in['ln_b'], 'L3_gnn_Wout': _L3_gnn_in['Wout'], 'L3_gnn_bout': _L3_gnn_in['bout']}

def reference(x, src, dst, edge_weight1, L1_gnn_W, L1_gnn_att_src, L1_gnn_att_dst, L1_gnn_bias, L1_gnn_gamma, L1_gnn_beta, L2_gnn_W_in, L2_gnn_b_in, L2_gnn_Wq, L2_gnn_bq, L2_gnn_Wk, L2_gnn_bk, L2_gnn_Wv, L2_gnn_bv, L2_gnn_We, L2_gnn_Wskip, L2_gnn_bskip, L2_gnn_Wbeta, L2_gnn_bn_gamma, L2_gnn_bn_beta, L3_gnn_Wn, L3_gnn_bn, L3_gnn_WQ, L3_gnn_bQ, L3_gnn_WK, L3_gnn_bK, L3_gnn_WV, L3_gnn_bV, L3_gnn_WO, L3_gnn_bO, L3_gnn_ln_g, L3_gnn_ln_b, L3_gnn_Wout, L3_gnn_bout):
    import jax
    import jax.numpy as jnp

    def _L0_gnn_ref(x, edge_index):
        import jax, jax.numpy as jnp
        import numpy as np
        EPS = 1e-07
        N_NODES, N_EDGES, D = (10000, 5000, 128)

        def mobius_add(x, y):
            x2 = jnp.sum(x * x, axis=-1, keepdims=True)
            y2 = jnp.sum(y * y, axis=-1, keepdims=True)
            xy = jnp.sum(x * y, axis=-1, keepdims=True)
            num = (1.0 + 2.0 * xy + y2) * x + (1.0 - x2) * y
            den = 1.0 + 2.0 * xy + x2 * y2
            return num / jnp.maximum(den, EPS)

        def mobius_scalar_mul(r, x):
            nrm = jnp.sqrt(jnp.sum(x * x, axis=-1, keepdims=True))
            nrm_c = jnp.clip(nrm, EPS, 1.0 - EPS)
            scaled = jnp.tanh(r * jnp.arctanh(nrm_c)) * (x / nrm_c)
            return jnp.where(nrm > EPS, scaled, jnp.zeros_like(x))
        src, dst = (edge_index[0], edge_index[1])
        n, d = x.shape
        messages = mobius_add(x[src], -x[dst])

        def body(out, em):
            m, idx = em
            return (out.at[idx].set(mobius_add(out[idx], m)), None)
        out0 = jnp.zeros((n, d), dtype=x.dtype)
        total, _ = jax.lax.scan(body, out0, (messages, dst))
        count = jnp.zeros((n,), dtype=x.dtype).at[dst].add(1.0)
        scale = 1.0 / jnp.maximum(count, 1.0)
        aggr = mobius_scalar_mul(scale[:, None], total)
        return mobius_add(x, aggr)

    def _L1_gnn_ref(x, W, att_src, att_dst, bias, gamma, beta, edge_index):
        import jax, jax.numpy as jnp
        import numpy as np
        N = 50000
        E = 18750
        DIM = 128
        H = 4
        C = DIM // H
        NEG_SLOPE = 0.2
        LN_EPS = 1e-05
        n = x.shape[0]
        loop = jnp.arange(n, dtype=edge_index.dtype)
        src = jnp.concatenate([edge_index[0], loop])
        dst = jnp.concatenate([edge_index[1], loop])
        h = (x @ W).reshape(n, H, C)
        a_src = jnp.einsum('nhc,hc->nh', h, att_src)
        a_dst = jnp.einsum('nhc,hc->nh', h, att_dst)
        e = jax.nn.leaky_relu(a_src[src] + a_dst[dst], NEG_SLOPE)
        m = jax.ops.segment_max(e, dst, num_segments=n)
        p = jnp.exp(e - m[dst])
        denom = jax.ops.segment_sum(p, dst, num_segments=n)
        alpha = p / (denom[dst] + 1e-16)
        out = jax.ops.segment_sum(alpha[:, :, None] * h[src], dst, num_segments=n)
        out = out.reshape(n, H * C) + bias
        y = x + out
        mu = jnp.mean(y, axis=-1, keepdims=True)
        var = jnp.var(y, axis=-1, keepdims=True)
        return gamma * (y - mu) * jax.lax.rsqrt(var + LN_EPS) + beta

    def _L2_gnn_ref(x, edge_index, edge_attr, W_in, b_in, Wq, bq, Wk, bk, Wv, bv, We, Wskip, bskip, Wbeta, bn_gamma, bn_beta):
        import jax, jax.numpy as jnp
        import numpy as np
        N, E, IN_DIM, HID, HEADS, LAYERS = (50000, 10000, 128, 128, 4, 2)
        C = HID // HEADS
        EPS = 1e-05

        def _init(key, shape, fan_in):
            return jax.random.normal(key, shape, dtype=jnp.float32) / np.sqrt(fan_in)

        def _transformer_conv(h, src, tgt, edge_attr, Wq, bq, Wk, bk, Wv, bv, We, Wskip, bskip, Wbeta):
            n = h.shape[0]
            q = (h @ Wq + bq).reshape(n, HEADS, C)
            k = (h @ Wk + bk).reshape(n, HEADS, C)
            v = (h @ Wv + bv).reshape(n, HEADS, C)
            e = (edge_attr @ We).reshape(-1, HEADS, C)
            k_j = k[src] + e
            alpha = jnp.einsum('ehc,ehc->eh', q[tgt], k_j) / jnp.sqrt(jnp.float32(C))
            amax = jax.ops.segment_max(alpha, tgt, num_segments=n)
            ex = jnp.exp(alpha - amax[tgt])
            denom = jax.ops.segment_sum(ex, tgt, num_segments=n)
            a = ex / denom[tgt]
            msg = (v[src] + e) * a[..., None]
            out = jax.ops.segment_sum(msg, tgt, num_segments=n).reshape(n, HID)
            x_r = h @ Wskip + bskip
            beta = jax.nn.sigmoid(jnp.concatenate([out, x_r, out - x_r], axis=-1) @ Wbeta)
            return beta * x_r + (1.0 - beta) * out

        def _batchnorm(h, gamma, beta):
            mu = h.mean(axis=0)
            var = h.var(axis=0)
            return gamma * (h - mu) * jax.lax.rsqrt(var + EPS) + beta
        src, tgt = (edge_index[0], edge_index[1])
        h = jax.nn.relu(x @ W_in + b_in)
        for l in range(LAYERS):
            h_res = h
            h = _transformer_conv(h, src, tgt, edge_attr, Wq[l], bq[l], Wk[l], bk[l], Wv[l], bv[l], We[l], Wskip[l], bskip[l], Wbeta[l])
            h = jax.nn.relu(_batchnorm(h, bn_gamma[l], bn_beta[l]))
            h = h + h_res
        return h

    def _L3_gnn_ref(x, edge_index, Wn, bn, WQ, bQ, WK, bK, WV, bV, WO, bO, ln_g, ln_b, Wout, bout):
        import jax, jax.numpy as jnp
        import numpy as np
        N_NODES = 3125
        N_EDGES = 50000
        NODE_DIM = 128
        HIDDEN = 128
        N_LAYERS = 4
        LN_EPS = 1e-05

        def _layernorm(x, g, b):
            mu = jnp.mean(x, axis=-1, keepdims=True)
            var = jnp.mean(jnp.square(x - mu), axis=-1, keepdims=True)
            return (x - mu) * jax.lax.rsqrt(var + LN_EPS) * g + b
        n = x.shape[0]
        src, dst = (edge_index[0], edge_index[1])
        scale = 1.0 / np.sqrt(HIDDEN)
        h = x @ Wn + bn
        for l in range(N_LAYERS):
            Q = h @ WQ[l] + bQ[l]
            K = h @ WK[l] + bK[l]
            V = h @ WV[l] + bV[l]
            scores = jnp.sum(Q[dst] * K[src], axis=-1) * scale
            seg_max = jax.ops.segment_max(scores, dst, num_segments=n)
            e = jnp.exp(scores - seg_max[dst])
            seg_sum = jax.ops.segment_sum(e, dst, num_segments=n)
            attn = e / seg_sum[dst]
            messages = jax.ops.segment_sum(attn[:, None] * V[src], dst, num_segments=n)
            out = messages @ WO[l] + bO[l]
            h = _layernorm(h + out, ln_g[l], ln_b[l])
        return h @ Wout + bout
    edge_index = jnp.stack([src, dst])
    h = jnp.maximum(_layernorm(x, axis=-1), 0.0)
    x = x + _L0_gnn_ref(h, edge_index)
    h = jnp.maximum(_layernorm(x, axis=-1), 0.0)
    x = x + _L1_gnn_ref(h, L1_gnn_W, L1_gnn_att_src, L1_gnn_att_dst, L1_gnn_bias, L1_gnn_gamma, L1_gnn_beta, edge_index)
    h = jnp.maximum(_layernorm(x, axis=-1), 0.0)
    x = x + _L2_gnn_ref(h, edge_index, edge_weight1, L2_gnn_W_in, L2_gnn_b_in, L2_gnn_Wq, L2_gnn_bq, L2_gnn_Wk, L2_gnn_bk, L2_gnn_Wv, L2_gnn_bv, L2_gnn_We, L2_gnn_Wskip, L2_gnn_bskip, L2_gnn_Wbeta, L2_gnn_bn_gamma, L2_gnn_bn_beta)
    h = jnp.maximum(_layernorm(x, axis=-1), 0.0)
    x = x + _L3_gnn_ref(h, edge_index, L3_gnn_Wn, L3_gnn_bn, L3_gnn_WQ, L3_gnn_bQ, L3_gnn_WK, L3_gnn_bK, L3_gnn_WV, L3_gnn_bV, L3_gnn_WO, L3_gnn_bO, L3_gnn_ln_g, L3_gnn_ln_b, L3_gnn_Wout, L3_gnn_bout)
    return x

_drawn_inputs = setup_inputs


def setup_inputs(seed=0):
    import zlib

    import numpy as np

    out = dict(_drawn_inputs(seed))
    spreads = {'L1_gnn_bias': (0.0, 0.1),
     'L1_gnn_gamma': (1.0, 0.2),
     'L1_gnn_beta': (0.0, 0.1),
     'L2_gnn_b_in': (0.0, 0.1),
     'L2_gnn_bq': (0.0, 0.579),
     'L2_gnn_bk': (0.0, 0.8),
     'L2_gnn_bv': (0.0, 0.295),
     'L2_gnn_bskip': (0.0, 0.332),
     'L2_gnn_bn_gamma': (1.0, 0.2),
     'L2_gnn_bn_beta': (0.0, 0.1),
     'L3_gnn_bn': (0.0, 0.1),
     'L3_gnn_bQ': (0.0, 0.8),
     'L3_gnn_bK': (0.0, 0.8),
     'L3_gnn_bV': (0.0, 0.1),
     'L3_gnn_bO': (0.0, 0.1),
     'L3_gnn_ln_g': (1.0, 0.2),
     'L3_gnn_ln_b': (0.0, 0.1),
     'L3_gnn_bout': (0.0, 0.1)}
    factors = {'L1_gnn_att_dst': 4.874}
    for name, (base, spread) in spreads.items():
        noise = np.random.default_rng([zlib.crc32(name.encode()), seed]).standard_normal(out[name].shape)
        drawn = base * np.exp(spread * noise) if base else spread * noise
        out[name] = jnp.asarray(drawn.astype(out[name].dtype))
    for name, factor in factors.items():
        out[name] = (out[name] * factor).astype(out[name].dtype)
    return out
```

```python
from contextlib import ExitStack

import concourse.bass as bass
from concourse import mybir

ALU = mybir.AluOpType
ACT = mybir.ActivationFunctionType
X = mybir.AxisListType.X
F32 = mybir.dt.float32
I32 = mybir.dt.int32
BF16 = mybir.dt.bfloat16
U8 = mybir.dt.uint8

P = 128
D = 128
HEADS = 4
RANKS = 4
RING = 4
GROUP = 5
L1_LAYERS, L2_LAYERS, L3_LAYERS = 1, 2, 4
STEPS = 16
MASKED = 1e30
UNSET = -1e29
EPS_BALL = 1e-7
EPS_LN = 1e-5
SLOT = 16
NULL_KEY = 4095


class Count:

    def __init__(self, sem, base=0):
        self.sem, self.base, self.n = sem, base, 0

    def did(self, instruction, by=1):
        instruction.then_inc(self.sem, by)
        self.n += by
        return self.n

    def need(self, engine, mark):
        if isinstance(self.base, int) and self.base + mark == 0:
            return
        engine.wait_ge(self.sem, self.base + mark)


def spread(ap, axis, n):
    shape = list(ap.shape)
    return ap.unsqueeze(axis).to_broadcast(shape[:axis] + [n] + shape[axis:])


def program(nc, a, out):
    N = a["x"].shape[0]
    E = a["src"].shape[0]
    T = -(-N // P)
    NP = T * P
    LAST = N - (T - 1) * P
    GROUPS = T // GROUP
    EC = 8 * -(-E // (8 * P))
    EROWS = P * EC
    CHUNK = EC // 14
    IC = -(-(E // RANKS + T + E // (RANKS * P) + 3 * RING) // P)
    ITEMS = P * IC
    C = D // HEADS
    EF = E % EC
    EL = E // EC
    assert T % GROUP == 0 and EC % 14 == 0 and EL == P - 1 and NP < 4096 and E > RANKS

    with ExitStack() as ctx:
        def sb(name, shape, dt=F32):
            return ctx.enter_context(nc.sbuf_tensor(name, shape, dt))

        def sem(name):
            return ctx.enter_context(nc.semaphore(name))

        edge_rows = nc.dram_tensor("edge_rows", [EROWS, 2 * RANKS], F32).ap()
        key_row = nc.dram_tensor("key_row", [T, P], F32).ap()
        ranked = nc.dram_tensor("ranked", [NP, 4], I32).ap()
        tile_of_item = nc.dram_tensor("tile_of_item", [P, IC], U8).ap()
        group_of_step = nc.dram_tensor("group_of_step", [P, IC], U8).ap()
        step_items = nc.dram_tensor("step_items", [ITEMS, 8], I32).ap()
        slots = nc.dram_tensor("slots", [ITEMS, P, SLOT], F32).ap()
        row_width = [132, 132] + [256] * (L2_LAYERS + L3_LAYERS)
        tables = [nc.dram_tensor(f"table{n}", [NP, w], F32).ap() for n, w in enumerate(row_width)]

        x_all = sb("x_all", [P, T, D])
        h_all = sb("h_all", [P, T, D])
        stage = sb("stage", [P, T * 512])
        acc = sb("acc", [P, T * HEADS * (C + 2)])
        ta = sb("ta", [P, T, D])
        tb = sb("tb", [P, T, D])
        rows = sb("rows", [P, RING, RANKS, 256])
        prod = sb("prod", [P, RANKS, D])
        pv = sb("pv", [P, RING, RANKS, HEADS * (C + 2)])
        slot = sb("slot", [P, RING, SLOT])
        ident = sb("ident", [P, P])
        onesf = sb("onesf", [P, P])
        tile_row = sb("tile_row", [1, ITEMS], U8)
        counts = sb("counts", [1, 4], I32)
        node_id = sb("node_id", [P, T], I32)
        node_start = sb("node_start", [P, T])
        node_deg = sb("node_deg", [P, T])
        x_id = sb("x_id", [P, T], I32)
        run_max = sb("run_max", [P, T, HEADS])
        qe = sb("qe", [P, T, HEADS])
        s = sb("s", [P, RANKS, HEADS])
        s_w = sb("s_w", [P, RANKS, HEADS])
        mx = sb("mx", [P, HEADS])
        new_max = sb("new_max", [P, HEADS])
        dif = sb("dif", [P, RING, RANKS + 1, HEADS])
        alpha = sb("alpha", [P, RING, HEADS])
        htile = sb("htile", [P, GROUP, D])
        hT = sb("hT", [P, GROUP, D])
        sm = sb("sm", [P, 12, T])
        eps_ln = sb("eps_ln", [P, 1])
        left = sb("left", [P, T])
        n_blk = sb("n_blk", [1, 4, T])
        n_blk_i = sb("n_blk_i", [1, 2, T], I32)
        maxT = sb("maxT", [T, 1])
        per_tile = sb("per_tile", [P, 4, T])
        step_grid = sb("step_grid", [P, T])
        item_i = sb("item_i", [P, IC], I32)
        item_f = sb("item_f", [P, IC])
        tile_f = sb("tile_f", [P, IC])
        tile_u = sb("tile_u", [P, IC], U8)
        group_u = sb("group_u", [P, IC], U8)
        step_b = sb("step_b", [P, IC])
        step_off = ta[:, :, :].rearrange("p t d -> p (t d)")[:, 0:2 * IC * GROUP].rearrange("p (k n) -> p k n", k=2)
        step_off_i = tb[:, :, :].rearrange("p t d -> p (t d)")[:, 0:IC * 8].bitcast(I32).rearrange("p (i k) -> p i k", k=8)
        big = stage[:, 0:IC * T]
        big2 = stage[:, IC * T:2 * IC * T]
        group_row = acc[:, :].bitcast(U8)[0:1, 0:ITEMS]
        ps = ctx.enter_context(nc.psum_tensor("ps", [P, 8, 512], F32))

        w = {}
        vec = {}
        weight_parts = [("L1", [a["L1_gnn_W"]]), ("Win", [a["L2_gnn_W_in"]]), ("Wn", [a["L3_gnn_Wn"]]),
                        ("Wout", [a["L3_gnn_Wout"]])]
        vector_parts = [("att_src", [a["L1_gnn_att_src"].rearrange("h c -> (h c)")]),
                        ("att_dst", [a["L1_gnn_att_dst"].rearrange("h c -> (h c)")]),
                        ("L1_bias", [a["L1_gnn_bias"]]), ("L1_gamma", [a["L1_gnn_gamma"]]),
                        ("L1_beta", [a["L1_gnn_beta"]]), ("bin", [a["L2_gnn_b_in"]]),
                        ("bn", [a["L3_gnn_bn"]]), ("bout", [a["L3_gnn_bout"]])]
        for l in range(L2_LAYERS):
            vector_parts.append((f"We_{l}", [a["L2_gnn_We"][l, 0]]))
        for name, parts in weight_parts:
            w[name] = sb("w_" + name, [P, sum(p.shape[1] for p in parts)])
        for name, parts in vector_parts:
            vec[name] = sb("v_" + name, [P, sum(p.shape[0] for p in parts)])
        w_in = sb("w_in", [P, 4 * D])
        b_in = sb("b_in", [P, 4 * D])
        w_out = sb("w_out", [P, D])
        v_out = sb("v_out", [P, 5 * D])

        def into_layer(weights, biases):
            return [(w_in[:, k * D:(k + 1) * D], p) for k, p in enumerate(weights)] + [
                (b_in[:, k * D:(k + 1) * D], p.partition_broadcast(P)) for k, p in enumerate(biases)]

        def into_L2(l):
            return into_layer([a[f"L2_gnn_W{k}"][l] for k in ("k", "v", "q", "skip")],
                              [a[f"L2_gnn_b{k}"][l] for k in ("k", "v", "q", "skip")])

        def into_L3(l):
            return into_layer([a[f"L3_gnn_W{k}"][l] for k in ("K", "V", "Q")],
                              [a[f"L3_gnn_b{k}"][l] for k in ("K", "V", "Q")])

        def out_of_L2(l):
            return [(v_out[:, 0:3 * D], a["L2_gnn_Wbeta"][l].rearrange("k o -> (k o)").partition_broadcast(P)),
                    (v_out[:, 3 * D:4 * D], a["L2_gnn_bn_gamma"][l].partition_broadcast(P)),
                    (v_out[:, 4 * D:5 * D], a["L2_gnn_bn_beta"][l].partition_broadcast(P))]

        def out_of_L3(l):
            return [(w_out[:, :], a["L3_gnn_WO"][l])] + [
                (v_out[:, k * D:(k + 1) * D], a[f"L3_gnn_{n}"][l].partition_broadcast(P))
                for k, n in enumerate(("bO", "ln_g", "ln_b"))]

        params_in = Count(sem("params_in"))
        loaded = Count(sem("loaded"))
        x_gathered = Count(sem("x_gathered"))
        out_stored = Count(sem("out_stored"))
        stored = Count(sem("stored"))
        scattered = Count(sem("scattered"))
        vector_did = Count(sem("vector_did"))
        scalar_did = Count(sem("scalar_did"))
        tensor_did = Count(sem("tensor_did"))
        pool_did = Count(sem("pool_did"))
        hots_ready, hots_used = sem("hots_ready"), sem("hots_used")
        transposed, turned, staged_tile = sem("transposed"), sem("turned"), sem("staged_tile")
        projected, evacuated = sem("projected"), sem("evacuated")

        record_stored = [sem(f"record_stored{j}") for j in range(RING)]
        record_gathered = [sem(f"record_gathered{j}") for j in range(RING)]
        scan_slots_in = [sem(f"scan_slots_in{j}") for j in range(2)]
        scan_gathered = [sem(f"scan_gathered{j}") for j in range(2)]
        scan_did, scan_free, record_did = sem("scan_did"), sem("scan_free"), sem("record_did")
        slot_loaded = [sem(f"slot_loaded{j}") for j in range(RING)]
        rows_gathered = [sem(f"rows_gathered{j}") for j in range(RING)]
        pool_go, sync_go = sem("pool_go"), sem("sync_go")
        step_did = sem("step_did")
        shifted, exp_did, summed, ring_free = sem("shifted"), sem("exp_did"), sem("summed"), sem("ring_free")

        V, A, G, Q = nc.vector, nc.scalar, nc.gpsimd, nc.sync

        def vec_op(ins):
            vector_did.need(V, vector_did.did(ins))

        def act_op(ins):
            scalar_did.need(A, scalar_did.did(ins))

        flat = lambda t3: t3.rearrange("p t d -> p (t d)")

        ones_col = sb("ones_col", [P, 1])
        iota_i = sb("iota_i", [P, P], I32)
        iota_f = sb("iota_f", [P, P])
        part_i = sb("part_i", [P, 1], I32)
        part_f = sb("part_f", [P, 1])
        below = sb("below", [P, P])
        valid = sb("valid", [P, P])
        iota_b = sb("iota_b", [P, P], BF16)
        rank_f = iota_f[:, 0:RANKS]

        at = [0]

        def scratch(n, dt=F32):
            size = n if dt in (F32, I32) else -(-n // 2)
            v = stage[:, at[0]:at[0] + size]
            at[0] += size + size % 2
            return v if dt == F32 else v.bitcast(dt)

        src_e, w_e, dst_e = scratch(EC + RANKS, I32), scratch(EC + RANKS), scratch(EC, I32)
        lo_i, hi_i = scratch(EC, I32), scratch(EC, I32)
        lo_b, hi_b = scratch(EC, BF16), scratch(EC, BF16)
        ebs = scratch(EC * 2 * RANKS).rearrange("p (e k) -> p e k", k=2 * RANKS)
        lo_hot = [scratch(CHUNK * P, BF16).rearrange("p (c n) -> p c n", n=P) for _ in range(2)]
        hi_hot = [scratch(CHUNK * T, BF16).rearrange("p (c n) -> p c n", n=T) for _ in range(2)]
        zero_b = scratch(P, BF16)

        with nc.Block() as block:
            @block.sync
            def _(sp):
                pool_did.need(sp, 3)
                params_in_now = [(src_e, a["src"]), (w_e, a["edge_weight1"].rearrange("e o -> (e o)"))]
                for dst, arr in params_in_now:
                    body = bass.AP(arr.tensor, arr.offset, [[EC, P - 1], [1, EC + RANKS]])
                    loaded.did(sp.dma_start(dst[0:P - 1, :], body), 16)
                    loaded.did(sp.dma_start(dst[P - 1:P, 0:EF], arr[EL * EC:E].rearrange("(o e) -> o e", o=1)), 16)
                arr = a["dst"]
                loaded.did(sp.dma_start(dst_e[0:P - 1, :], arr[0:EL * EC].rearrange("(p e) -> p e", e=EC)), 16)
                loaded.did(sp.dma_start(dst_e[P - 1:P, 0:EF], arr[EL * EC:E].rearrange("(o e) -> o e", o=1)), 16)
                for name, parts in weight_parts:
                    c = 0
                    for p in parts:
                        params_in.did(sp.dma_start(w[name][:, c:c + p.shape[1]], p), 16)
                        c += p.shape[1]
                for name, parts in vector_parts:
                    c = 0
                    for p in parts:
                        params_in.did(sp.dma_start(vec[name][:, c:c + p.shape[0]], p.partition_broadcast(P)), 16)
                        c += p.shape[0]
                loaded.need(sp, loaded.n)

            @block.gpsimd
            def _(pool):
                pool_did.did(G.memset(src_e, 0))
                pool_did.did(G.memset(w_e, 0.0))
                pool_did.did(G.memset(dst_e, NULL_KEY))
                pool_did.did(G.iota(iota_i[:, :], [[1, P]], 0, 0))
                pool_did.did(G.iota(part_i[:, :], [[0, 1]], 0, 1))
                pool_did.did(G.memset(onesf[:, :], 1.0))

            @block.vector
            def _(dve):
                pool_did.need(dve, 6)
                vec_op(V.tensor_copy(iota_f[:, :], iota_i[:, :]))
                vec_op(V.tensor_copy(iota_b[:, :], iota_i[:, :]))
                vec_op(V.tensor_copy(part_f[:, :], part_i[:, :]))
                vec_op(V.tensor_scalar(ident[:, :], iota_f[:, :], part_f[:, 0:1], None, ALU.is_equal))
                vec_op(V.tensor_scalar(below[:, :], iota_f[:, :], part_f[:, 0:1], None, ALU.is_gt))
                vec_op(V.tensor_scalar(part_f[:, 0:1], part_f[:, 0:1], float(LAST), None, ALU.is_lt))
                vec_op(V.tensor_scalar(valid[:, :], onesf[:, :], part_f[:, 0:1], None, ALU.mult))
                vec_op(V.memset(eps_ln[:, :], EPS_LN))
                vec_op(V.memset(zero_b, 0.0))

        hist = ps[:, 0, 0:T]
        cnt = sm[:, 0, :]
        start = sm[:, 1, :]
        with nc.Block() as block:
            @block.vector
            def _(dve):
                vec_op(V.tensor_scalar(lo_i, dst_e, P - 1, None, ALU.bitwise_and))
                vec_op(V.tensor_scalar(hi_i, dst_e, 7, None, ALU.logical_shift_right))
                vec_op(V.tensor_copy(lo_b, lo_i))
                vec_op(V.tensor_copy(hi_b, hi_i))
                with dve.Fori(0, EC // CHUNK // 2) as q:
                    for b in range(2):
                        dve.wait_ge(hots_used, 2 * q + b + 1)
                        cols = bass.ds(q * (2 * CHUNK) + b * CHUNK, CHUNK)
                        V.tensor_tensor(lo_hot[b], spread(lo_b[:, cols], 2, P), spread(iota_b[:, :], 1, CHUNK),
                                        ALU.is_equal).then_inc(hots_ready, 1)
                        V.tensor_tensor(hi_hot[b], spread(hi_b[:, cols], 2, T), spread(iota_b[:, 0:T], 1, CHUNK),
                                        ALU.is_equal).then_inc(hots_ready, 1)

            @block.tensor
            def _(pe):
                nc.tensor.matmul(hist, zero_b, zero_b[:, 0:T], start=True, stop=False,
                                 skip_group_check=True).then_inc(hots_used, 2)
                with pe.Fori(0, EC // CHUNK // 2) as q:
                    for b in range(2):
                        pe.wait_ge(hots_ready, 4 * q + 2 * b + 2)
                        for c in range(CHUNK):
                            mm = nc.tensor.matmul(hist, lo_hot[b][:, c, :], hi_hot[b][:, c, :],
                                                  start=False, stop=False, skip_group_check=True)
                        mm.then_inc(hots_used, 1)
                tensor_did.did(nc.tensor.matmul(hist, zero_b, zero_b[:, 0:T], start=False, stop=True,
                                                skip_group_check=True))

            @block.gpsimd
            def _(pool):
                for k in range(RANKS):
                    pool_did.did(G.tensor_copy(ebs.bitcast(I32)[:, :, k], src_e[:, k:k + EC]))
                    pool_did.did(G.tensor_copy(ebs[:, :, RANKS + k], w_e[:, k:k + EC]))

            @block.sync
            def _(sp):
                pool_did.need(sp, pool_did.n)
                stored.did(sp.dma_start(edge_rows.rearrange("(p e) k -> p (e k)", p=P),
                                        ebs.rearrange("p e k -> p (e k)")), 16)
                stored.need(sp, stored.n)

        key = sm[:, 2, :]
        pos = sm[:, 3, :]
        n_rev = sm[:, 4, :]
        pos_i = sb("pos_i", [P, T], I32)
        n_i = sb("n_i", [P, T], I32)
        rec = sb("rec", [P, T, 4], I32)
        keyT = sb("keyT", [T, P])
        with nc.Block() as block:
            @block.gpsimd
            def _(pool):
                pool_did.did(G.iota(n_i[:, :], [[P, T]], 0, 1))

            @block.vector
            def _(dve):
                vec_op(V.tensor_copy(cnt, hist))
                pool_did.need(dve, pool_did.n)
                vec_op(V.tensor_copy(n_rev, n_i[:, :]))
                vec_op(V.tensor_scalar(n_rev, n_rev, -1.0, 4095.0, ALU.mult, ALU.add))
                vec_op(V.tensor_scalar(key, cnt, 4095.0, 4096.0, ALU.min, ALU.mult))
                vec_op(V.tensor_tensor(key, key, n_rev, ALU.add))

            @block.tensor
            def _(pe):
                vector_did.need(pe, vector_did.n)
                nc.tensor.matmul(ps[:, 1, 0:T], below[:, :], cnt, start=True, stop=True)
                nc.tensor.matmul(ps[:, 2, 0:T], onesf[:, :], cnt, start=True, stop=True)
                tensor_did.did(nc.tensor.transpose(ps[0:T, 3, 0:P], key, ident[:, :]))

            @block.scalar
            def _(act):
                tensor_did.need(act, tensor_did.n)
                scalar_did.did(A.copy(keyT[:, :], ps[0:T, 3, 0:P]))

            @block.sync
            def _(sp):
                scalar_did.need(sp, scalar_did.n)
                stored.did(sp.dma_start(key_row, keyT[:, :]), 16)
                stored.need(sp, stored.n)
                loaded.did(sp.dma_start(flat(ta[:, :, :]), key_row.rearrange("t p -> (t p)").partition_broadcast(P)), 16)
                loaded.need(sp, loaded.n)

        with nc.Block() as block:
            @block.vector
            def _(dve):
                vec_op(V.tensor_copy(sm[:, 5, :], ps[:, 2, 0:T]))
                vec_op(V.tensor_tensor_scan(sm[:, 6, :], onesf[:, 0:T], sm[:, 5, :], 0.0, ALU.mult, ALU.add))
                vec_op(V.tensor_tensor(start, sm[:, 6, :], sm[:, 5, :], ALU.subtract))
                vec_op(V.tensor_tensor(start, start, ps[:, 1, 0:T], ALU.add))
                for t in range(T):
                    vec_op(V.tensor_scalar(flat(tb[:, :, :]), flat(ta[:, :, :]), key[:, t:t + 1], 0.0,
                                           ALU.is_gt, ALU.add, accum_out=pos[:, t:t + 1]))
                vec_op(V.tensor_copy(pos_i[:, :], pos))
                vec_op(V.tensor_copy(rec[:, :, 0], n_i[:, :]))
                vec_op(V.tensor_copy(rec[:, :, 1], start))
                vec_op(V.tensor_copy(rec[:, :, 2], cnt))
                vec_op(V.memset(rec[:, :, 3], 0))

            @block.gpsimd
            def _(pool):
                vector_did.need(pool, vector_did.n)
                for t in range(T):
                    scattered.did(G.indirect_dma_start(
                        out=ranked, out_offset=bass.IndirectOffsetOnAxis(ap=pos_i[:, t:t + 1], axis=0),
                        in_=rec[:, t, :], in_offset=None), 16)

            @block.sync
            def _(sp):
                scattered.need(sp, scattered.n)
                loaded.did(sp.dma_start(rec[:, :, :], ranked.rearrange("(t p) c -> p t c", p=P)), 16)
                loaded.need(sp, loaded.n)

        def vector_block(*steps):
            with nc.Block() as block:
                @block.vector
                def _(dve):
                    for step in steps:
                        vec_op(step())

        def load_and_wait(*copies):
            with nc.Block() as block:
                @block.sync
                def _(sp):
                    for dst, src in copies:
                        loaded.did(sp.dma_start(dst, src), 16)
                    loaded.need(sp, loaded.n)

        vector_block(
            lambda: V.tensor_scalar(x_id[:, :], rec[:, :, 0], float(N - 1), None, ALU.min),
            lambda: V.tensor_copy(node_id[:, :], rec[:, :, 0]),
            lambda: V.tensor_copy(node_start[:, :], rec[:, :, 1]),
            lambda: V.tensor_copy(node_deg[:, :], rec[:, :, 2]),
            lambda: V.tensor_copy(left[:, :], rec[:, :, 2]))

        with nc.Block() as block:
            @block.tensor
            def _(pe):
                tensor_did.did(nc.tensor.transpose(ps[0:T, 0, 0:P], node_deg[:, :], ident[:, :]))

            @block.vector
            def _(dve):
                tensor_did.need(dve, tensor_did.n)
                vec_op(V.tensor_reduce(maxT[:, :], ps[0:T, 0, 0:P], X, ALU.max))

        with nc.Block() as block:
            @block.tensor
            def _(pe):
                tensor_did.did(nc.tensor.transpose(ps[0:1, 1, 0:T], maxT[:, :], ident[0:T, 0:T]))

            @block.vector
            def _(dve):
                tensor_did.need(dve, tensor_did.n)
                row = lambda k: n_blk[:, k, :]
                vec_op(V.tensor_scalar(row(0), ps[0:1, 1, 0:T], float(RANKS - 1), None, ALU.add))
                vec_op(V.tensor_copy(n_blk_i[:, 0, :], row(0)))
                vec_op(V.tensor_scalar(n_blk_i[:, 1, :], n_blk_i[:, 0, :], 2, None, ALU.arith_shift_right))
                vec_op(V.tensor_copy(row(0), n_blk_i[:, 1, :]))
                vec_op(V.tensor_tensor_scan(row(2), onesf[0:1, 0:T], row(0), 0.0, ALU.mult, ALU.add))
                vec_op(V.tensor_tensor(row(1), row(2), row(0), ALU.subtract))
                vec_op(V.memset(row(3), 0.0))
                vec_op(V.tensor_reduce(n_blk[:, 3, 0:GROUPS], row(0).rearrange("p (g k) -> p g k", k=GROUP), X, ALU.max))
                vec_op(V.tensor_tensor_scan(n_blk[:, 3, GROUPS:2 * GROUPS], onesf[0:1, 0:GROUPS],
                                            n_blk[:, 3, 0:GROUPS], 0.0, ALU.mult, ALU.add))
                vec_op(V.tensor_copy(n_blk_i[:, 0, 0:1], n_blk[:, 2, T - 1:T]))
                vec_op(V.tensor_scalar(n_blk_i[:, 0, 1:2], n_blk[:, 2, T - 1:T], float(RING - 1), None, ALU.add))
                vec_op(V.tensor_scalar(n_blk_i[:, 0, 2:3], n_blk[:, 3, 2 * GROUPS - 1:2 * GROUPS], 1.0, None, ALU.add))
                vec_op(V.tensor_scalar(counts[:, 0:1], n_blk_i[:, 0, 1:2], 2, None, ALU.arith_shift_right))
                vec_op(V.tensor_scalar(counts[:, 1:2], n_blk_i[:, 0, 0:1], 2, None, ALU.arith_shift_right))
                vec_op(V.tensor_scalar(counts[:, 0:1], counts[:, 0:1], 2.0, None, ALU.max))
                vec_op(V.tensor_scalar(counts[:, 1:2], counts[:, 1:2], 1.0, 2.0, ALU.add, ALU.max))
                vec_op(V.tensor_scalar(counts[:, 3:4], counts[:, 0:1], -1.0, None, ALU.add))
                vec_op(V.tensor_scalar(counts[:, 2:3], n_blk_i[:, 0, 2:3], 1, None, ALU.arith_shift_right))

            @block.gpsimd
            def _(pool):
                pool_did.did(G.iota(item_i[:, :], [[1, IC]], 0, IC))
                for t in range(T):
                    x_gathered.did(G.indirect_dma_start(
                        out=x_all[:, t, :], out_offset=None, in_=a["x"],
                        in_offset=bass.IndirectOffsetOnAxis(ap=x_id[:, t:t + 1], axis=0)), 16)
                x_gathered.need(pool, x_gathered.n)

        with nc.Block() as block:
            @block.tensor
            def _(pe):
                tensor_did.did(nc.tensor.matmul(ps[:, 2, 0:4 * T], onesf[0:1, :], n_blk[:, :, :].rearrange("p k t -> p (k t)"),
                                                start=True, stop=True))

            @block.vector
            def _(dve):
                tensor_did.need(dve, tensor_did.n)
                vec_op(V.tensor_copy(per_tile[:, :, :].rearrange("p k t -> p (k t)"), ps[:, 2, 0:4 * T]))
                vec_op(V.tensor_copy(item_f[:, :], item_i[:, :]))
                blocks, before, upto = per_tile[:, 0, :], per_tile[:, 1, :], per_tile[:, 2, :]
                g_blocks, g_upto = per_tile[:, 3, 0:GROUPS], per_tile[:, 3, GROUPS:2 * GROUPS]
                all_items = per_tile[:, 2, T - 1:T]
                by_tile = big.rearrange("p (i t) -> p i t", t=T)
                by_group = big2[:, 0:IC * GROUPS].rearrange("p (i g) -> p i g", g=GROUPS)
                by_both = big.rearrange("p (i k g) -> p i k g", k=GROUP, g=GROUPS)
                vec_op(V.tensor_tensor(by_tile, spread(item_f[:, :], 2, T), spread(upto, 1, IC), ALU.is_ge))
                vec_op(V.tensor_reduce(tile_f[:, :], by_tile, X, ALU.add))
                vec_op(V.tensor_scalar(tile_f[:, :], tile_f[:, :], float(T - 1), None, ALU.min))
                vec_op(V.tensor_copy(tile_u[:, :], tile_f[:, :]))
                vec_op(V.tensor_tensor(by_group, spread(item_f[:, :], 2, GROUPS), spread(g_upto, 1, IC), ALU.is_ge))
                vec_op(V.tensor_reduce(tile_f[:, :], by_group, X, ALU.add))
                vec_op(V.tensor_scalar(tile_f[:, :], tile_f[:, :], float(GROUPS - 1), None, ALU.min))
                vec_op(V.tensor_copy(group_u[:, :], tile_f[:, :]))
                vec_op(V.tensor_tensor(by_group, by_group, spread(g_blocks, 1, IC), ALU.mult))
                vec_op(V.tensor_reduce(step_b[:, :], by_group[:, :, 0:GROUPS - 1], X, ALU.add))
                vec_op(V.tensor_tensor(step_b[:, :], item_f[:, :], step_b[:, :], ALU.subtract))
                vec_op(V.tensor_tensor(by_group, spread(tile_f[:, :], 2, GROUPS), spread(iota_f[:, 0:GROUPS], 1, IC), ALU.is_equal))
                for k, what in ((0, blocks), (1, before)):
                    grid = what.rearrange("p (g k) -> p k g", k=GROUP)
                    vec_op(V.tensor_copy(step_grid[:, :], grid))
                    vec_op(V.tensor_tensor(by_both, spread(by_group, 2, GROUP),
                                           spread(step_grid[:, :].rearrange("p (k g) -> p k g", g=GROUPS), 1, IC), ALU.mult))
                    vec_op(V.tensor_reduce(step_off[:, k, :], by_both, X, ALU.add))
                off = lambda k: step_off[:, k, :].rearrange("p (i k) -> p i k", k=GROUP)
                vec_op(V.tensor_tensor(off(0), off(0), spread(step_b[:, :], 2, GROUP), ALU.is_gt))
                vec_op(V.tensor_tensor(off(1), off(1), spread(step_b[:, :], 2, GROUP), ALU.add))
                vec_op(V.tensor_scalar(off(1), off(1), all_items, None, ALU.subtract))
                vec_op(V.tensor_tensor(off(1), off(1), off(0), ALU.mult))
                vec_op(V.tensor_scalar(off(1), off(1), all_items, None, ALU.add))
                vec_op(V.memset(step_off_i[:, :, :], 0))
                vec_op(V.tensor_copy(step_off_i[:, :, 0:GROUP], off(1)))

            @block.sync
            def _(sp):
                vector_did.need(sp, vector_did.n)
                stored.did(sp.dma_start(tile_of_item, tile_u[:, :]), 16)
                stored.did(sp.dma_start(group_of_step, group_u[:, :]), 16)
                stored.did(sp.dma_start(step_items.rearrange("(p i) k -> p (i k)", p=P),
                                        step_off_i[:, :, :].rearrange("p i k -> p (i k)")), 16)
                stored.need(sp, stored.n)
                loaded.did(sp.dma_start(tile_row[:, :], tile_of_item.rearrange("(o p) i -> o (p i)", o=1)), 16)
                loaded.did(sp.dma_start(group_row, group_of_step.rearrange("(o p) i -> o (p i)", o=1)), 16)
                loaded.need(sp, loaded.n)

        index_of = sb("index_of", [P, RING], I32)
        with nc.Block() as block:
            @block.vector
            def _(dve):
                for first, credit in ((record_did, 1), (scan_did, 1), (step_did, 1), (ring_free, RING), (scan_free, 2)):
                    V.sem_inc(first, credit)

            @block.tensor
            def _(pe):
                nc.tensor.sem_inc(evacuated, GROUP)
                nc.tensor.sem_inc(projected, 1)

            @block.sync
            def _(sp):
                for j in range(RING):
                    sp.sem_inc(record_stored[j], 16)

        with nc.Block() as block:
            @block.vector
            def _(dve):
                n = dve.value_load(counts[0:1, 1:2], min_val=2, max_val=ITEMS // RING - 2)
                with dve.Fori(0, n) as q:
                    for j in range(RING):
                        did = Count(record_did, q * (5 * RING) + (5 * j + 1))
                        t = dve.value_load(tile_row[0:1, bass.ds(q * RING + j, 1)], min_val=0, max_val=T - 1)
                        dve.wait_ge(record_stored[j], q * 16 + 16)
                        dve.wait_ge(record_did, q * (5 * RING) + (5 * j + 1))
                        node = node_start[:, bass.ds(t, 1)]
                        rest = left[:, bass.ds(t, 1)]
                        did.did(V.tensor_scalar(index_of[:, j:j + 1], node, float(E), None, ALU.min))
                        did.did(V.tensor_scalar(slot[:, j, 3 * RANKS:4 * RANKS], rank_f, rest, None, ALU.is_lt))
                        did.need(dve, 2)
                        did.did(V.tensor_scalar(node, node, float(RANKS), None, ALU.add))
                        did.did(V.tensor_scalar(rest, rest, -float(RANKS), None, ALU.add))
                        did.did(V.tensor_scalar(slot[:, j, 2 * RANKS:3 * RANKS], slot[:, j, 3 * RANKS:4 * RANKS],
                                                MASKED, -MASKED, ALU.mult, ALU.add))

            @block.gpsimd
            def _(pool):
                n = pool.value_load(counts[0:1, 1:2], min_val=2, max_val=ITEMS // RING - 2)
                with pool.Fori(0, n) as q:
                    for j in range(RING):
                        pool.wait_ge(record_did, q * (5 * RING) + (5 * j + 2))
                        pool.sem_inc(pool_go, 1)
                        G.indirect_dma_start(
                            out=slot[:, j, 0:2 * RANKS], out_offset=None, in_=edge_rows,
                            in_offset=bass.IndirectOffsetOnAxis(ap=index_of[:, j:j + 1], axis=0)
                        ).then_inc(record_gathered[j], 16)

            @block.sync
            def _(sp):
                n = sp.value_load(counts[0:1, 1:2], min_val=2, max_val=ITEMS // RING - 2)
                with sp.Fori(0, n) as q:
                    for j in range(RING):
                        sp.wait_ge(record_did, q * (5 * RING) + (5 * j + 6))
                        sp.wait_ge(record_gathered[j], q * 16 + 16)
                        sp.dma_start(slots[bass.ds(q * RING + j, 1), :, :].rearrange("o p k -> p (o k)"),
                                     slot[:, j, :]).then_inc(record_stored[j], 16)
                for j in range(RING):
                    sp.wait_ge(record_stored[j], n * 16 + 16)
                    sp.sem_inc(sync_go, 1)

        def copy_all(dst, src):
            vector_block(lambda: V.tensor_copy(dst, src))

        def layer_norm(dst, src, relu=False, gamma=None, beta=None):
            mean, var = sm[:, 0, :], sm[:, 1, :]
            vector_block(
                lambda: V.tensor_reduce(mean, src, X, ALU.add),
                lambda: V.tensor_scalar(mean, mean, 1.0 / D, None, ALU.mult),
                lambda: V.tensor_tensor(ta[:, :, :], src, spread(mean, 2, D), ALU.subtract),
                lambda: V.tensor_tensor(tb[:, :, :], ta[:, :, :], ta[:, :, :], ALU.mult),
                lambda: V.tensor_reduce(var, tb[:, :, :], X, ALU.add))
            with nc.Block() as block:
                @block.scalar
                def _(act):
                    scalar_did.did(A.activation(var, var, ACT.Sqrt, bias=eps_ln[:, 0:1], scale=1.0 / D))

                @block.vector
                def _(dve):
                    scalar_did.need(dve, scalar_did.n)
                    vec_op(V.reciprocal(var, var))
                    if gamma is None:
                        vec_op(V.tensor_tensor(dst, ta[:, :, :], spread(var, 2, D), ALU.mult))
                    else:
                        vec_op(V.tensor_tensor(ta[:, :, :], ta[:, :, :], spread(var, 2, D), ALU.mult))
                        vec_op(V.tensor_tensor(ta[:, :, :], ta[:, :, :], spread(gamma, 1, T), ALU.mult))
                        vec_op(V.tensor_tensor(dst, ta[:, :, :], spread(beta, 1, T), ALU.add))
                    if relu:
                        vec_op(V.tensor_scalar(flat(dst), flat(dst), 0.0, None, ALU.max))

        projections = [0]

        def project(src, weight, bias, dst_of, cols, table=None, width=0):
            base = projections[0] * T
            projections[0] += 1
            with nc.Block() as block:
                @block.scalar
                def _(act):
                    with act.Fori(0, T // GROUP) as q:
                        A.copy(htile[:, :, :].rearrange("p k d -> p (k d)"),
                               src[:, bass.ds(q * (GROUP * D), GROUP * D)]).then_inc(staged_tile, 1)
                        act.wait_ge(transposed, q + (base // GROUP + 1))
                        act.wait_ge(projected, q * GROUP + (base + 1))
                        hT_flat = hT[:, :, :].rearrange("p k d -> p (k d)")
                        A.copy(hT_flat[:, 0:4 * D], ps[:, 5, :])
                        A.copy(hT_flat[:, 4 * D:GROUP * D], ps[:, 6, 0:D]).then_inc(turned, 1)

                @block.tensor
                def _(pe):
                    with pe.Fori(0, T // GROUP) as q:
                        pe.wait_ge(staged_tile, q + (base // GROUP + 1))
                        for k in range(GROUP):
                            mm = nc.tensor.transpose(ps[:, 5 + k // 4, (k % 4) * D:(k % 4) * D + D], htile[:, k, :], ident[:, :])
                        mm.then_inc(transposed, 1)
                        pe.wait_ge(turned, q + (base // GROUP + 1))
                        for k in range(GROUP):
                            pe.wait_ge(evacuated, q * GROUP + (base + k + 1))
                            nc.tensor.matmul(ps[:, k, 0:cols], hT[:, k, :], weight, start=True,
                                             stop=True).then_inc(projected, 1)

                @block.vector
                def _(dve):
                    with dve.Fori(0, T // GROUP) as q:
                        for k in range(GROUP):
                            dve.wait_ge(projected, q * GROUP + (base + k + 2))
                            if bias is None:
                                V.tensor_scalar(dst_of(q * GROUP + k), ps[:, k, 0:cols], 1.0, None, ALU.mult
                                                ).then_inc(evacuated, 1)
                            else:
                                V.tensor_tensor(dst_of(q * GROUP + k), ps[:, k, 0:cols], bias, ALU.add
                                                ).then_inc(evacuated, 1)

                if table is not None:
                    @block.gpsimd
                    def _(pool):
                        for t in range(T):
                            pool.wait_ge(evacuated, base + GROUP + t + 1)
                            scattered.did(G.indirect_dma_start(
                                out=table, out_offset=bass.IndirectOffsetOnAxis(ap=node_id[:, t:t + 1], axis=0),
                                in_=stage[:, t * width:t * width + table.shape[1]], in_offset=None), 16)
                        scattered.need(pool, scattered.n)

        def scatter(table, width):
            with nc.Block() as block:
                @block.gpsimd
                def _(pool):
                    for t in range(T):
                        scattered.did(G.indirect_dma_start(
                            out=table, out_offset=bass.IndirectOffsetOnAxis(ap=node_id[:, t:t + 1], axis=0),
                            in_=stage[:, t * width:t * width + table.shape[1]], in_offset=None), 16)
                    scattered.need(pool, scattered.n)

        layer_norm(h_all[:, :, :], x_all[:, :, :], relu=True)
        TW = row_width[0]
        table_rows = stage[:, 0:T * TW].rearrange("p (t d) -> p t d", d=TW)
        u_all = stage[:, T * TW:T * TW + T * D]
        ring0 = stage[:, T * (TW + D):T * (TW + D) + 2 * RANKS * GROUP * TW].rearrange(
            "p (j r k d) -> p j r k d", j=2, r=RANKS, k=GROUP)
        slot0 = sb("slot0", [P, 2, GROUP, SLOT])
        y2_all = sb("y2_all", [P, T])
        state = sb("state", [P, GROUPS * 4 * GROUP])
        RG = RANKS * GROUP
        e_c, e_a, e_al, e_den, e_t, e_t2 = (sb(f"edge_{n}", [P, RG]) for n in ("c", "a", "al", "den", "t", "t2"))
        e_ac = sb("edge_ac", [P, RANKS, 2, GROUP])
        e_v = sb("edge_v", [P, RANKS, 4, GROUP])
        r_s = {n: sb("r_" + n, [P, GROUP]) for n in ("ts", "om", "rest", "hu", "xy", "den", "num", "ba")}
        r_t = sb("r_t", [P, 2, GROUP])
        r_ab = sb("r_ab", [P, 2, GROUP])
        r_v1 = sb("r_v1", [P, 4, GROUP])
        r_v2 = sb("r_v2", [P, 4, GROUP])
        PRE, PER = 24, 26
        vector_block(
            lambda: V.tensor_tensor(ta[:, :, :], h_all[:, :, :], h_all[:, :, :], ALU.mult),
            lambda: V.tensor_reduce(y2_all[:, :], ta[:, :, :], X, ALU.add),
            lambda: V.memset(table_rows[:, :, D:TW], 0.0),
            lambda: V.tensor_copy(table_rows[:, :, D], y2_all[:, :]),
            lambda: V.tensor_copy(table_rows[:, :, 0:D], h_all[:, :, :]),
            lambda: V.memset(u_all, 0.0),
            lambda: V.memset(state[:, :], 0.0))
        scatter(tables[0], TW)

        with nc.Block() as block:
            @block.sync
            def _(sp):
                n = sp.value_load(counts[0:1, 2:3], min_val=1, max_val=ITEMS // 2 - 1)
                with sp.Fori(0, n) as q:
                    for j in range(2):
                        sp.wait_ge(scan_free, q * 2 + (j + 1))
                        sp.sem_inc(sync_go, 1)
                        for k in range(GROUP):
                            item = sp.value_load(step_items[bass.ds(q * 2 + j, 1), k:k + 1], min_val=0, max_val=ITEMS - 1)
                            sp.dma_start(slot0[:, j, k, :], slots[bass.ds(item, 1), :, :].rearrange("o p k -> p (o k)")
                                         ).then_inc(scan_slots_in[j], 16)

            @block.gpsimd
            def _(pool):
                n = pool.value_load(counts[0:1, 2:3], min_val=1, max_val=ITEMS // 2 - 1)
                with pool.Fori(0, n) as q:
                    for j in range(2):
                        pool.wait_ge(scan_slots_in[j], q * (16 * GROUP) + 16 * GROUP)
                        pool.sem_inc(pool_go, 1)
                        for r in range(RANKS):
                            for k in range(GROUP):
                                G.indirect_dma_start(
                                    out=ring0[:, j, r, k, :], out_offset=None, in_=tables[0],
                                    in_offset=bass.IndirectOffsetOnAxis(ap=slot0[:, j, k, r:r + 1].bitcast(I32), axis=0)
                                ).then_inc(scan_gathered[j], 16)

            @block.vector
            def _(dve):
                K = PRE + RANKS * PER
                n = dve.value_load(counts[0:1, 2:3], min_val=1, max_val=ITEMS // 2 - 1)
                with dve.Fori(0, n) as q:
                    for j in range(2):
                        base = dve.snap(q * (2 * K) + (j * K + 1))
                        did = Count(scan_did, base)
                        g = dve.value_load(group_row[0:1, bass.ds(q * 2 + j, 1)], min_val=0, max_val=GROUPS - 1)
                        h_g = flat(h_all[:, :, :])[:, bass.ds(g * (GROUP * D), GROUP * D)].rearrange("p (k d) -> p k d", k=GROUP)
                        u_g = u_all[:, bass.ds(g * (GROUP * D), GROUP * D)].rearrange("p (k d) -> p k d", k=GROUP)
                        y2 = y2_all[:, bass.ds(g * GROUP, GROUP)]
                        st = lambda a0, a1: state[:, bass.ds(g * (4 * GROUP) + a0 * GROUP, (a1 - a0) * GROUP)].rearrange(
                            "p (c k) -> p c k", k=GROUP)
                        st1 = lambda a0: state[:, bass.ds(g * (4 * GROUP) + a0 * GROUP, GROUP)]
                        rk = lambda t: t[:, :].rearrange("p (r k) -> p r k", k=GROUP)
                        src_h = ring0[:, j, :, :, 0:D]
                        x2 = ring0[:, j, :, :, D]
                        mask = slot0[:, j, :, 3 * RANKS:4 * RANKS].rearrange("p k r -> p r k")
                        tmp = flat(ta[:, :, :])[:, 0:RG * D].rearrange("p (r k d) -> p r k d", r=RANKS, k=GROUP)
                        y2r = spread(y2, 1, RANKS)

                        def op(ins, by=1):
                            did.need(dve, did.did(ins, by))

                        dve.wait_ge(scan_gathered[j], q * (16 * RG) + 16 * RG)
                        dve.wait_ge(scan_did, base)
                        op(V.tensor_tensor(tmp, src_h, spread(h_g, 1, RANKS), ALU.mult))
                        op(V.tensor_reduce(rk(e_c), tmp, X, ALU.add))
                        op(V.tensor_scalar(e_a[:, :], e_c[:, :], -2.0, 1.0, ALU.mult, ALU.add))
                        op(V.tensor_tensor(rk(e_den), x2, y2r, ALU.mult))
                        op(V.tensor_tensor(e_den[:, :], e_den[:, :], e_a[:, :], ALU.add))
                        op(V.tensor_scalar(e_den[:, :], e_den[:, :], EPS_BALL, None, ALU.max))
                        op(V.reciprocal(e_den[:, :], e_den[:, :]))
                        op(V.tensor_tensor(rk(e_den), rk(e_den), mask, ALU.mult))
                        op(V.tensor_tensor(rk(e_a), rk(e_a), y2r, ALU.add))
                        op(V.tensor_tensor(e_al[:, :], e_a[:, :], e_den[:, :], ALU.mult))
                        op(V.tensor_scalar(rk(e_t), x2, -1.0, None, ALU.add))
                        op(V.tensor_tensor(e_ac[:, :, 1, :], rk(e_t), rk(e_den), ALU.mult))
                        op(V.tensor_copy(e_v[:, :, 0, :], e_ac[:, :, 1, :]))
                        op(V.tensor_tensor(e_ac[:, :, 0, :], rk(e_al), rk(e_c), ALU.mult))
                        op(V.tensor_tensor(rk(e_t), e_ac[:, :, 1, :], y2r, ALU.mult))
                        op(V.tensor_tensor(e_v[:, :, 1, :], rk(e_t), e_ac[:, :, 0, :], ALU.add))
                        op(V.tensor_tensor(rk(e_t), rk(e_al), x2, ALU.mult))
                        op(V.tensor_tensor(rk(e_t2), e_ac[:, :, 1, :], rk(e_c), ALU.mult))
                        op(V.tensor_tensor(e_t[:, :], e_t[:, :], e_t2[:, :], ALU.add))
                        op(V.tensor_tensor(e_t[:, :], e_t[:, :], e_al[:, :], ALU.mult))
                        op(V.tensor_tensor(rk(e_t2), e_ac[:, :, 1, :], e_v[:, :, 1, :], ALU.mult))
                        op(V.tensor_tensor(e_v[:, :, 3, :], rk(e_t), rk(e_t2), ALU.add), by=PRE - did.n)
                        for r in range(RANKS):
                            hs = ring0[:, j, r, :, 0:D]
                            t_u = tmp[:, 0]
                            t_w = tmp[:, 1]
                            al = rk(e_al)[:, r, :]
                            R = {k: v[:, :] for k, v in r_s.items()}
                            begin = did.n
                            uh = did.did(V.tensor_tensor(t_u, hs, u_g, ALU.mult))
                            op(V.tensor_tensor(r_t[:, :, :], st(0, 2), e_ac[:, r, :, :], ALU.mult))
                            op(V.tensor_tensor(R["ts"], r_t[:, 0, :], r_t[:, 1, :], ALU.add))
                            op(V.tensor_reduce(R["hu"], t_u, X, ALU.add))
                            did.did(V.tensor_tensor(R["om"], st1(2), e_v[:, r, 3, :], ALU.mult))
                            op(V.tensor_tensor(R["xy"], R["hu"], al, ALU.mult))
                            did.did(V.tensor_scalar(R["rest"], st1(2), -1.0, 1.0, ALU.mult, ALU.add))
                            op(V.tensor_tensor(st1(3), R["xy"], R["ts"], ALU.add))
                            did.did(V.tensor_tensor(e_v[:, r, 2, :], R["xy"], R["ts"], ALU.add))
                            op(V.scalar_tensor_tensor(out=R["den"], in0=st1(3), scalar=2.0, in1=R["om"], op0=ALU.mult, op1=ALU.add))
                            did.did(V.scalar_tensor_tensor(out=R["num"], in0=st1(3), scalar=2.0, in1=e_v[:, r, 3, :],
                                                           op0=ALU.mult, op1=ALU.add))
                            op(V.tensor_scalar(R["den"], R["den"], 1.0, EPS_BALL, ALU.add, ALU.max))
                            op(V.reciprocal(R["den"], R["den"]))
                            did.did(V.scalar_tensor_tensor(out=r_ab[:, 0, :], in0=R["num"], scalar=1.0, in1=R["den"],
                                                           op0=ALU.add, op1=ALU.mult))
                            op(V.tensor_tensor(r_ab[:, 1, :], R["rest"], R["den"], ALU.mult))
                            did.did(V.tensor_tensor(r_v1[:, :, :], st(0, 4), spread(r_ab[:, 0, :], 1, 4), ALU.mult))
                            op(V.tensor_tensor(R["ba"], r_ab[:, 1, :], al, ALU.mult))
                            did.did(V.tensor_tensor(t_w, hs, spread(R["ba"], 2, D), ALU.mult))
                            did.did(V.tensor_tensor(r_v2[:, :, :], e_v[:, r, :, :], spread(r_ab[:, 1, :], 1, 4), ALU.mult))
                            op(V.tensor_tensor(u_g, u_g, spread(r_ab[:, 0, :], 2, D), ALU.mult))
                            did.did(V.tensor_tensor(st(0, 4), r_v1[:, :, :], r_v2[:, :, :], ALU.add))
                            op(V.tensor_tensor(u_g, u_g, t_w, ALU.add))
                            op(V.tensor_tensor(r_t[:, :, :], st(2, 4), r_ab[:, :, :], ALU.mult))
                            last = V.tensor_tensor(st1(2), r_t[:, 0, :], r_t[:, 1, :], ALU.add)
                            if r < RANKS - 1:
                                op(last, by=PER - (did.n - begin))
                            else:
                                did.did(last, by=PER - (did.n - begin))
                        did.need(dve, did.n)
                        V.memset(r_t[:, 0, 0:1], 0.0).then_inc(scan_free, 1)

        by_g = lambda t3: t3.rearrange("p (g k) d -> p g k d", k=GROUP)
        gamma_g = state[:, :].rearrange("p (g c k) -> p g c k", c=4, k=GROUP)[:, :, 0, :]
        total_v = stage[:, 0:T * D].rearrange("p (t d) -> p t d", d=D)
        nrm, ratio, k1, k2, k3, k4, k5, k6 = (sm[:, n, :] for n in range(8))
        vector_block(
            lambda: V.tensor_tensor(by_g(ta[:, :, :]), by_g(h_all[:, :, :]), spread(gamma_g, 3, D), ALU.mult),
            lambda: V.tensor_tensor(total_v, ta[:, :, :], u_all.rearrange("p (t d) -> p t d", d=D), ALU.add),
            lambda: V.tensor_tensor(ta[:, :, :], total_v, total_v, ALU.mult),
            lambda: V.tensor_reduce(k6, ta[:, :, :], X, ALU.add),
            lambda: V.tensor_tensor(ta[:, :, :], total_v, h_all[:, :, :], ALU.mult),
            lambda: V.tensor_reduce(k5, ta[:, :, :], X, ALU.add),
            lambda: V.tensor_scalar(k4, node_deg[:, :], 1.0, None, ALU.max),
            lambda: V.reciprocal(k4, k4))
        with nc.Block() as block:
            @block.scalar
            def _(act):
                scalar_did.did(A.activation(nrm, k6, ACT.Sqrt))
        norm_c = sm[:, 8, :]
        sq = sm[:, 9, :]
        series = sm[:, 10, :]
        small = sm[:, 11, :]

        def horner(c):
            return lambda: V.tensor_tensor(series, series, sq, ALU.mult), \
                lambda: V.tensor_scalar(series, series, c, None, ALU.add)

        vector_block(
            lambda: V.tensor_scalar(norm_c, nrm, EPS_BALL, 1.0 - EPS_BALL, ALU.max, ALU.min),
            lambda: V.tensor_tensor(sq, norm_c, norm_c, ALU.mult),
            lambda: V.tensor_scalar(series, sq, 1.0 / 15, 1.0 / 13, ALU.mult, ALU.add),
            *horner(1.0 / 11), *horner(1.0 / 9), *horner(1.0 / 7), *horner(1.0 / 5), *horner(1.0 / 3), *horner(1.0),
            lambda: V.tensor_tensor(series, series, norm_c, ALU.mult),
            lambda: V.tensor_scalar(small, norm_c, 0.25, None, ALU.is_lt),
            lambda: V.tensor_scalar(k1, norm_c, -1.0, 1.0, ALU.mult, ALU.add),
            lambda: V.reciprocal(k1, k1),
            lambda: V.tensor_scalar(k2, norm_c, 1.0, None, ALU.add),
            lambda: V.tensor_tensor(k1, k1, k2, ALU.mult))
        with nc.Block() as block:
            @block.scalar
            def _(act):
                scalar_did.did(A.activation(k1, k1, ACT.Ln))
        vector_block(
            lambda: V.tensor_scalar(k1, k1, 0.5, None, ALU.mult),
            lambda: V.tensor_tensor(series, series, k1, ALU.subtract),
            lambda: V.tensor_tensor(series, series, small, ALU.mult),
            lambda: V.tensor_tensor(k1, k1, series, ALU.add),
            lambda: V.tensor_tensor(k1, k1, k4, ALU.mult))
        with nc.Block() as block:
            @block.scalar
            def _(act):
                scalar_did.did(A.activation(k1, k1, ACT.Tanh))
        vector_block(
            lambda: V.reciprocal(norm_c, norm_c),
            lambda: V.tensor_tensor(ratio, k1, norm_c, ALU.mult),
            lambda: V.tensor_scalar(k1, nrm, EPS_BALL, None, ALU.is_gt),
            lambda: V.tensor_tensor(ratio, ratio, k1, ALU.mult),
            lambda: V.tensor_tensor(k5, k5, ratio, ALU.mult),
            lambda: V.tensor_tensor(k6, k6, ratio, ALU.mult),
            lambda: V.tensor_tensor(k6, k6, ratio, ALU.mult),
            lambda: V.tensor_scalar(k5, k5, 2.0, 1.0, ALU.mult, ALU.add),
            lambda: V.tensor_tensor(k1, y2_all[:, :], k6, ALU.mult),
            lambda: V.tensor_tensor(k1, k1, k5, ALU.add),
            lambda: V.tensor_scalar(k1, k1, EPS_BALL, None, ALU.max),
            lambda: V.reciprocal(k1, k1),
            lambda: V.tensor_tensor(k5, k5, k6, ALU.add),
            lambda: V.tensor_tensor(k5, k5, k1, ALU.mult),
            lambda: V.tensor_scalar(k2, y2_all[:, :], -1.0, 1.0, ALU.mult, ALU.add),
            lambda: V.tensor_tensor(k2, k2, k1, ALU.mult),
            lambda: V.tensor_tensor(k2, k2, ratio, ALU.mult),
            lambda: V.tensor_tensor(ta[:, :, :], h_all[:, :, :], spread(k5, 2, D), ALU.mult),
            lambda: V.tensor_tensor(x_all[:, :, :], x_all[:, :, :], ta[:, :, :], ALU.add),
            lambda: V.tensor_tensor(ta[:, :, :], total_v, spread(k2, 2, D), ALU.mult),
            lambda: V.tensor_tensor(x_all[:, :, :], x_all[:, :, :], ta[:, :, :], ALU.add))

        phase_no = [0]

        def attention(table, width, heads, kind, loads, att_dst=None):
            phase = phase_no[0]
            phase_no[0] += 1
            Ch = D // heads
            extra = 2 if kind == "weighted" else 1
            W = heads * (Ch + extra)
            value0 = 0 if kind == "added" else D
            scale = 1.0 if kind == "added" else float(Ch) ** -0.5
            q_col = 2 * D

            with nc.Block() as block:
                @block.sync
                def _(sp):
                    for dst, src in loads:
                        params_in.did(sp.dma_start(dst, src), 16)
                    params_in.need(sp, params_in.n)
                    n = sp.value_load(counts[0:1, 0:1], min_val=2, max_val=ITEMS // RING - 2)
                    before = sp.snap(n * phase)
                    with sp.Fori(0, n) as q:
                        for j in range(RING):
                            sp.wait_ge(ring_free, before * RING + q * RING + (j + 1))
                            sp.dma_start(slot[:, j, :], slots[bass.ds(q * RING + j, 1), :, :].rearrange("o p k -> p (o k)")
                                         ).then_inc(slot_loaded[j], 16)

                @block.gpsimd
                def _(pool):
                    n = pool.value_load(counts[0:1, 0:1], min_val=2, max_val=ITEMS // RING - 2)
                    before = pool.snap(n * phase)
                    with pool.Fori(0, n) as q:
                        for j in range(RING):
                            pool.wait_ge(slot_loaded[j], before * 16 + q * 16 + 16)
                            pool.sem_inc(pool_go, 1)
                            for r in range(RANKS):
                                G.indirect_dma_start(
                                    out=rows[:, j, r, 0:table.shape[1]], out_offset=None, in_=table,
                                    in_offset=bass.IndirectOffsetOnAxis(ap=slot[:, j, r:r + 1].bitcast(I32), axis=0)
                                ).then_inc(rows_gathered[j], 16)

                @block.scalar
                def _(act):
                    n = act.value_load(counts[0:1, 0:1], min_val=2, max_val=ITEMS // RING - 2)
                    before = act.snap(n * phase)
                    with act.Fori(0, n) as q:
                        for j in range(RING):
                            act.wait_ge(shifted, before * RING + q * RING + (j + 1))
                            weights = pv[:, j, :, 0:W].rearrange("p r (h c) -> p r h c", h=heads)[:, :, :, Ch]
                            A.activation(weights, dif[:, j, 0:RANKS, 0:heads], ACT.Exp)
                            A.activation(alpha[:, j, 0:heads], dif[:, j, RANKS, 0:heads], ACT.Exp).then_inc(exp_did, 1)

                @block.tensor
                def _(pe):
                    n = pe.value_load(counts[0:1, 0:1], min_val=2, max_val=ITEMS // RING - 2)
                    before = pe.snap(n * phase)
                    with pe.Fori(0, n) as q:
                        for j in range(RING):
                            pe.wait_ge(ring_free, before * RING + q * RING + (RING + j + 1))
                            for r in range(RANKS):
                                mm = nc.tensor.matmul(ps[:, j % 2, 0:W], ident[:, :], pv[:, j, r, 0:W],
                                                      start=(r == 0), stop=(r == RANKS - 1))
                            mm.then_inc(summed, 1)

                @block.vector
                def _(dve):
                    n = dve.value_load(counts[0:1, 0:1], min_val=2, max_val=ITEMS // RING - 2)
                    before = dve.snap(n * phase)
                    last = dve.value_load(counts[0:1, 3:4], min_val=1, max_val=ITEMS // RING - 3)
                    steps_before = dve.snap(n * (phase * RING * STEPS) + (phase * 2 * STEPS + 1))

                    def tile(i):
                        return dve.value_load(tile_row[0:1, bass.ds(i, 1)], min_val=0, max_val=T - 1)

                    def step(quad, k, new=True, old=True, older=True):
                        i = quad * RING + k
                        did = Count(step_did, dve.snap(steps_before + quad * (RING * STEPS) + (k + 1) * STEPS))
                        number = dve.snap(before * RING + quad * RING)

                        def op(ins):
                            did.need(dve, did.did(ins))

                        t = tile(i + 1) if new else None
                        t_old = tile(i - 1) if not new else None
                        dve.wait_ge(step_did, did.base)
                        jn, jo, jp = (k + 1) % RING, k % RING, (k - 1) % RING
                        S = s[:, :, 0:heads]
                        M = mx[:, 0:heads]
                        NM = new_max[:, 0:heads]
                        if new:
                            state_m = run_max[:, :, :].rearrange("p t h -> p (t h)")[:, bass.ds(t * HEADS, heads)]
                            row = rows[:, jn, :, :]
                            dve.wait_ge(rows_gathered[jn], (before + quad + (k + 1) // RING) * (16 * RANKS) + 16 * RANKS)
                            if kind == "added":
                                dst_part = att_dst.rearrange("p t h -> p (t h)")[:, bass.ds(t * HEADS, heads)]
                                m_prod = did.did(V.tensor_tensor(S, row[:, :, D:D + heads], spread(dst_part, 1, RANKS), ALU.add))
                            else:
                                query = stage[:, bass.ds(t * width + q_col, D)]
                                m_prod = did.did(V.tensor_tensor(prod[:, :, :], row[:, :, 0:D], spread(query, 1, RANKS), ALU.mult))
                        if older:
                            if new:
                                t_old = tile(i - 1)
                            sums = acc[:, bass.ds(t_old * (HEADS * (C + 2)), W)]
                            dve.wait_ge(summed, number + k)
                            if heads == 1:
                                did.did(V.scalar_tensor_tensor(out=sums, in0=sums, scalar=alpha[:, jp, 0:1], in1=ps[:, jp % 2, 0:W],
                                                               op0=ALU.mult, op1=ALU.add))
                            else:
                                sums3 = sums.rearrange("p (h c) -> p h c", h=heads)
                                m_sum = did.did(V.tensor_tensor(sums3, sums3, spread(alpha[:, jp, 0:heads], 2, Ch + extra), ALU.mult))
                        if new:
                            did.need(dve, m_prod)
                            if kind != "added":
                                m_s = did.did(V.tensor_reduce(S, prod[:, :, :].rearrange("p r (h c) -> p r h c", h=heads), X, ALU.add))
                            else:
                                m_s = did.did(V.scalar_tensor_tensor(out=S, in0=S, scalar=0.2, in1=S, op0=ALU.mult, op1=ALU.max))
                            if kind == "weighted":
                                qe_t = qe[:, :, :].rearrange("p t h -> p (t h)")[:, bass.ds(t * HEADS, heads)]
                                did.did(V.tensor_tensor(s_w[:, :, :], spread(slot[:, jn, RANKS:2 * RANKS], 2, heads),
                                                        spread(qe_t, 1, RANKS), ALU.mult))
                        if older and heads > 1:
                            did.need(dve, m_sum)
                            did.did(V.tensor_tensor(sums, sums, ps[:, jp % 2, 0:W], ALU.add))
                        if old:
                            out4 = pv[:, jo, :, 0:W].rearrange("p r (h c) -> p r h c", h=heads)
                            dve.wait_ge(exp_did, number + (k + 1))
                            if kind == "weighted":
                                did.did(V.tensor_tensor(out4[:, :, :, Ch + 1], out4[:, :, :, Ch],
                                                        spread(slot[:, jo, RANKS:2 * RANKS], 2, heads), ALU.mult))
                            V.tensor_tensor(out4[:, :, :, 0:Ch], rows[:, jo, :, value0:value0 + D].rearrange("p r (h c) -> p r h c", h=heads),
                                            spread(out4[:, :, :, Ch], 3, Ch), ALU.mult).then_inc(ring_free, 1)
                        if new:
                            if kind == "weighted":
                                did.need(dve, did.n)
                                op(V.tensor_tensor(S, S, s_w[:, :, :], ALU.add))
                            else:
                                did.need(dve, m_s)
                            op(V.scalar_tensor_tensor(out=S, in0=S, scalar=scale, in1=spread(slot[:, jn, 2 * RANKS:3 * RANKS], 2, heads),
                                                      op0=ALU.mult, op1=ALU.add))
                            op(V.tensor_reduce(M, S.rearrange("p r h -> p h r"), X, ALU.max))
                            op(V.tensor_tensor(NM, M, state_m, ALU.max))
                            did.did(V.tensor_tensor(dif[:, jn, 0:RANKS, 0:heads], S, spread(NM, 1, RANKS), ALU.subtract))
                            V.tensor_tensor(dif[:, jn, RANKS, 0:heads], state_m, NM, ALU.subtract).then_inc(shifted, 1)
                            dve.wait_ge(shifted, number + (k + 2))
                            V.tensor_tensor(state_m, NM, NM, ALU.max).then_inc(step_did, STEPS - did.n)
                        else:
                            V.memset(mx[:, 0:1], 0.0).then_inc(step_did, STEPS - did.n)

                    def first_step():
                        step(0, -1, old=False, older=False)

                    first_step()
                    step(0, 0, older=False)
                    with dve.Fori(0, last) as q:
                        for k in range(1, RING + 1):
                            step(q, k)
                    for k in range(1, RING - 1):
                        step(last, k)
                    step(last, RING - 1, new=False)
                    step(last, RING, new=False, old=False)

        heads_of = lambda t3: t3.rearrange("p t (h c) -> p t h c", h=HEADS)

        def sums_of(heads, extra):
            Ch = D // heads
            view = acc[:, :].rearrange("p (t w) -> p t w", t=T)[:, :, 0:heads * (Ch + extra)]
            return view.rearrange("p t (h c) -> p t h c", h=heads)

        def add_to_x(what):
            vector_block(lambda: V.tensor_tensor(x_all[:, :, :], x_all[:, :, :], what, ALU.add))

        def clear_sums():
            vector_block(lambda: V.memset(acc[:, :], 0.0),
                         lambda: V.memset(run_max[:, :, :], UNSET))

        def node_sum(src):
            with nc.Block() as block:
                @block.tensor
                def _(pe):
                    nc.tensor.matmul(ps[:, 0, 0:D], onesf[:, :], src[:, 0, :], start=True, stop=False)
                    with pe.Fori(1, T - 1) as t:
                        nc.tensor.matmul(ps[:, 0, 0:D], onesf[:, :], flat(src)[:, bass.ds(t * D, D)], start=False, stop=False)
                    tensor_did.did(nc.tensor.matmul(ps[:, 0, 0:D], valid[:, :], src[:, T - 1, :], start=False, stop=True))

        layer_norm(h_all[:, :, :], x_all[:, :, :], relu=True)
        project(flat(h_all[:, :, :]), w["L1"][:, :], None, lambda t: stage[:, bass.ds(t * TW, D)], D)
        att_d = sb("att_d", [P, T, HEADS])
        hw = table_rows[:, :, 0:D]
        a_src = table_rows[:, :, D:TW]
        sums = sums_of(HEADS, 1)
        vector_block(
            lambda: V.tensor_tensor(ta[:, :, :], hw, spread(vec["att_src"][:, :], 1, T), ALU.mult),
            lambda: V.tensor_reduce(a_src, heads_of(ta[:, :, :]), X, ALU.add),
            lambda: V.tensor_tensor(ta[:, :, :], hw, spread(vec["att_dst"][:, :], 1, T), ALU.mult),
            lambda: V.tensor_reduce(att_d[:, :, :], heads_of(ta[:, :, :]), X, ALU.add),
            lambda: V.tensor_tensor(qe[:, :, :], a_src, att_d[:, :, :], ALU.add),
            lambda: V.scalar_tensor_tensor(out=run_max[:, :, :], in0=qe[:, :, :], scalar=0.2, in1=qe[:, :, :],
                                           op0=ALU.mult, op1=ALU.max),
            lambda: V.memset(sums[:, :, :, C], 1.0),
            lambda: V.tensor_copy(sums[:, :, :, 0:C], heads_of(hw)))
        scatter(tables[1], TW)
        attention(tables[1], TW, HEADS, "added", into_L2(0), att_dst=att_d[:, :, :])
        vector_block(
            lambda: V.tensor_scalar(qe[:, :, :], sums[:, :, :, C], 1e-16, None, ALU.add),
            lambda: V.reciprocal(qe[:, :, :], qe[:, :, :]),
            lambda: V.tensor_tensor(heads_of(ta[:, :, :]), sums[:, :, :, 0:C], spread(qe[:, :, :], 3, C), ALU.mult),
            lambda: V.tensor_tensor(ta[:, :, :], ta[:, :, :], spread(vec["L1_bias"][:, :], 1, T), ALU.add),
            lambda: V.tensor_tensor(ta[:, :, :], ta[:, :, :], h_all[:, :, :], ALU.add))
        layer_norm(h_all[:, :, :], ta[:, :, :], gamma=vec["L1_gamma"][:, :], beta=vec["L1_beta"][:, :])
        add_to_x(h_all[:, :, :])

        layer_norm(h_all[:, :, :], x_all[:, :, :], relu=True)
        h_tile = lambda t: flat(h_all[:, :, :])[:, bass.ds(t * D, D)]
        a_tile = lambda t: flat(ta[:, :, :])[:, bass.ds(t * D, D)]
        project(flat(h_all[:, :, :]), w["Win"][:, :], vec["bin"][:, :], h_tile, D)
        vector_block(lambda: V.tensor_scalar(flat(h_all[:, :, :]), flat(h_all[:, :, :]), 0.0, None, ALU.max))
        col = sb("col", [P, 4, D])
        sums = sums_of(HEADS, 2)
        for l in range(L2_LAYERS):
            W2 = 4 * D
            cols2 = stage[:, 0:T * W2].rearrange("p (t d) -> p t d", d=W2)
            skip = cols2[:, :, 3 * D:4 * D]
            We = vec[f"We_{l}"][:, :]
            wb = v_out
            project(flat(h_all[:, :, :]), w_in[:, :], b_in[:, :],
                    lambda t: stage[:, bass.ds(t * W2, W2)], W2, table=tables[2 + l], width=W2)
            clear_sums()
            vector_block(
                lambda: V.tensor_tensor(ta[:, :, :], cols2[:, :, 2 * D:3 * D], spread(We, 1, T), ALU.mult),
                lambda: V.tensor_reduce(qe[:, :, :], heads_of(ta[:, :, :]), X, ALU.add))
            attention(tables[2 + l], W2, HEADS, "weighted",
                      out_of_L2(l) + (into_L2(l + 1) if l + 1 < L2_LAYERS else into_L3(0)))
            gate = sm[:, 0, :]
            gate2 = sm[:, 1, :]
            vector_block(
                lambda: V.tensor_scalar(qe[:, :, :], sums[:, :, :, C], 1e-30, None, ALU.max),
                lambda: V.reciprocal(qe[:, :, :], qe[:, :, :]),
                lambda: V.tensor_copy(tb[:, :, :], spread(We, 1, T)),
                lambda: V.tensor_tensor(heads_of(tb[:, :, :]), heads_of(tb[:, :, :]), spread(sums[:, :, :, C + 1], 3, C), ALU.mult),
                lambda: V.tensor_tensor(heads_of(tb[:, :, :]), heads_of(tb[:, :, :]), sums[:, :, :, 0:C], ALU.add),
                lambda: V.tensor_tensor(heads_of(ta[:, :, :]), heads_of(tb[:, :, :]), spread(qe[:, :, :], 3, C), ALU.mult),
                lambda: V.tensor_tensor(col[:, 0, :], wb[:, 0:D], wb[:, 2 * D:3 * D], ALU.add),
                lambda: V.tensor_tensor(col[:, 1, :], wb[:, D:2 * D], wb[:, 2 * D:3 * D], ALU.subtract),
                lambda: V.tensor_tensor(tb[:, :, :], ta[:, :, :], spread(col[:, 0, :], 1, T), ALU.mult),
                lambda: V.tensor_reduce(gate, tb[:, :, :], X, ALU.add),
                lambda: V.tensor_tensor(tb[:, :, :], skip, spread(col[:, 1, :], 1, T), ALU.mult),
                lambda: V.tensor_reduce(gate2, tb[:, :, :], X, ALU.add),
                lambda: V.tensor_tensor(gate, gate, gate2, ALU.add))
            with nc.Block() as block:
                @block.scalar
                def _(act):
                    scalar_did.did(A.activation(gate, gate, ACT.Exp, scale=-1.0))
            vector_block(
                lambda: V.tensor_scalar(gate, gate, 1.0, None, ALU.add),
                lambda: V.reciprocal(gate, gate),
                lambda: V.tensor_tensor(tb[:, :, :], skip, ta[:, :, :], ALU.subtract),
                lambda: V.tensor_tensor(tb[:, :, :], tb[:, :, :], spread(gate, 2, D), ALU.mult),
                lambda: V.tensor_tensor(tb[:, :, :], tb[:, :, :], ta[:, :, :], ALU.add))
            node_sum(tb[:, :, :])
            vector_block(
                lambda: V.tensor_scalar(col[:, 2, :], ps[:, 0, 0:D], 1.0 / N, None, ALU.mult),
                lambda: V.tensor_tensor(ta[:, :, :], tb[:, :, :], spread(col[:, 2, :], 1, T), ALU.subtract),
                lambda: V.tensor_tensor(tb[:, :, :], ta[:, :, :], ta[:, :, :], ALU.mult))
            node_sum(tb[:, :, :])
            with nc.Block() as block:
                @block.scalar
                def _(act):
                    scalar_did.did(A.activation(col[:, 3, :], ps[:, 0, 0:D], ACT.Sqrt, bias=eps_ln[:, 0:1], scale=1.0 / N))
            vector_block(
                lambda: V.reciprocal(col[:, 3, :], col[:, 3, :]),
                lambda: V.tensor_tensor(col[:, 3, :], col[:, 3, :], v_out[:, 3 * D:4 * D], ALU.mult),
                lambda: V.tensor_tensor(ta[:, :, :], ta[:, :, :], spread(col[:, 3, :], 1, T), ALU.mult),
                lambda: V.tensor_tensor(ta[:, :, :], ta[:, :, :], spread(v_out[:, 4 * D:5 * D], 1, T), ALU.add),
                lambda: V.scalar_tensor_tensor(out=h_all[:, :, :], in0=ta[:, :, :], scalar=0.0, in1=h_all[:, :, :],
                                               op0=ALU.max, op1=ALU.add))
        add_to_x(h_all[:, :, :])

        layer_norm(h_all[:, :, :], x_all[:, :, :], relu=True)
        project(flat(h_all[:, :, :]), w["Wn"][:, :], vec["bn"][:, :], h_tile, D)
        sums = sums_of(1, 1)
        for l in range(L3_LAYERS):
            W3 = 3 * D
            n_table = 2 + L2_LAYERS + l
            project(flat(h_all[:, :, :]), w_in[:, 0:3 * D], b_in[:, 0:3 * D],
                    lambda t: stage[:, bass.ds(t * W3, W3)], W3, table=tables[n_table], width=W3)
            clear_sums()
            attention(tables[n_table], W3, 1, "plain", out_of_L3(l) + (into_L3(l + 1) if l + 1 < L3_LAYERS else []))
            vector_block(
                lambda: V.tensor_scalar(sm[:, 0, :], sums[:, :, 0, D], 1e-30, None, ALU.max),
                lambda: V.reciprocal(sm[:, 0, :], sm[:, 0, :]),
                lambda: V.tensor_tensor(ta[:, :, :], sums[:, :, 0, 0:D], spread(sm[:, 0, :], 2, D), ALU.mult))
            project(flat(ta[:, :, :]), w_out[:, :], v_out[:, 0:D], a_tile, D)
            vector_block(lambda: V.tensor_tensor(ta[:, :, :], ta[:, :, :], h_all[:, :, :], ALU.add))
            layer_norm(h_all[:, :, :], ta[:, :, :], gamma=v_out[:, D:2 * D], beta=v_out[:, 2 * D:3 * D])
        project(flat(h_all[:, :, :]), w["Wout"][:, :], vec["bout"][:, :], a_tile, D)
        add_to_x(ta[:, :, :])

        with nc.Block() as block:
            @block.gpsimd
            def _(pool):
                for t in range(T):
                    rows_here = P if t < T - 1 else LAST
                    out_stored.did(G.indirect_dma_start(
                        out=out, out_offset=bass.IndirectOffsetOnAxis(ap=node_id[0:rows_here, t:t + 1], axis=0),
                        in_=x_all[0:rows_here, t, :], in_offset=None), 16)
                out_stored.need(pool, out_stored.n)


_INS = ["x", "src", "dst", "edge_weight1"] + [f"L1_gnn_{n}" for n in ("W", "att_src", "att_dst", "bias", "gamma", "beta")] + [
    f"L2_gnn_{n}" for n in ("W_in", "b_in", "Wq", "bq", "Wk", "bk", "Wv", "bv", "We", "Wskip", "bskip", "Wbeta",
                            "bn_gamma", "bn_beta")] + [
    f"L3_gnn_{n}" for n in ("Wn", "bn", "WQ", "bQ", "WK", "bK", "WV", "bV", "WO", "bO", "ln_g", "ln_b", "Wout", "bout")]


def kernel(**inputs):
    import numpy as _np
    import concourse.bacc as _bacc
    from concourse import mybir as _mybir
    from concourse.bass_utils import run_bass_kernel_spmd as _run

    nc = _bacc.Bacc("TRN2", target_bir_lowering=False, num_devices=1)
    arrays, args = {}, {}
    for name in _INS:
        arr = _np.ascontiguousarray(inputs[name])
        arrays[f"in_{name}"] = arr
        args[name] = nc.dram_tensor(f"in_{name}", arr.shape, _mybir.dt.from_np(arr.dtype), kind="ExternalInput").ap()
    shape = tuple(inputs["x"].shape)
    out = nc.dram_tensor("out_x", shape, _mybir.dt.float32, kind="ExternalOutput").ap()
    program(nc, args, out)
    r = _run(nc, [arrays], core_ids=[0])
    return r.results[0]["out_x"]
```

```python
from contextlib import ExitStack

import concourse.bass as bass
from concourse import mybir

ALU = mybir.AluOpType
ACT = mybir.ActivationFunctionType
X = mybir.AxisListType.X
F32 = mybir.dt.float32
I32 = mybir.dt.int32
BF16 = mybir.dt.bfloat16
U8 = mybir.dt.uint8

P = 128
D = 128
HEADS = 4
RANKS = 4
RING = 4
RECORDS = 8
GROUP = 5
L1_LAYERS, L2_LAYERS, L3_LAYERS = 1, 2, 4
STEPS = 16
MASKED = 1e30
UNSET = -1e29
EPS_BALL = 1e-7
EPS_LN = 1e-5
SLOT = 16
NULL_KEY = 4095
RANK_VECTOR_TILES = 12
LN_VECTOR_TILES = 15


class Count:

    def __init__(self, sem, base=0):
        self.sem, self.base, self.n = sem, base, 0

    def did(self, instruction, by=1):
        instruction.then_inc(self.sem, by)
        self.n += by
        return self.n

    def need(self, engine, mark):
        if isinstance(self.base, int) and self.base + mark == 0:
            return
        engine.wait_ge(self.sem, self.base + mark)


def spread(ap, axis, n):
    shape = list(ap.shape)
    return ap.unsqueeze(axis).to_broadcast(shape[:axis] + [n] + shape[axis:])


def program(nc, a, out):
    N = a["x"].shape[0]
    E = a["src"].shape[0]
    T = -(-N // P)
    NP = T * P
    LAST = N - (T - 1) * P
    GROUPS = T // GROUP
    EC = 8 * -(-E // (8 * P))
    EROWS = P * EC
    CHUNK = EC // 14
    IC = -(-(E // RANKS + T + E // (RANKS * P) + 3 * RECORDS) // P)
    ITEMS = P * IC
    C = D // HEADS
    EF = E % EC
    EL = E // EC
    assert T % GROUP == 0 and EC % 14 == 0 and EL == P - 1 and NP < 4096 and E > RANKS

    with ExitStack() as ctx:
        def sb(name, shape, dt=F32):
            return ctx.enter_context(nc.sbuf_tensor(name, shape, dt))

        def sem(name):
            return ctx.enter_context(nc.semaphore(name))

        edge_rows = nc.dram_tensor("edge_rows", [EROWS, 2 * RANKS], F32).ap()
        key_row = nc.dram_tensor("key_row", [T, P], F32).ap()
        ranked = nc.dram_tensor("ranked", [NP, 4], I32).ap()
        tile_of_item = nc.dram_tensor("tile_of_item", [P, IC], U8).ap()
        group_of_step = nc.dram_tensor("group_of_step", [P, IC], U8).ap()
        step_items = nc.dram_tensor("step_items", [ITEMS, 8], I32).ap()
        slots = nc.dram_tensor("slots", [ITEMS, P, SLOT], F32).ap()
        row_width = [132, 132] + [256] * (L2_LAYERS + L3_LAYERS)
        tables = [nc.dram_tensor(f"table{n}", [NP, w], F32).ap() for n, w in enumerate(row_width)]

        x_all = sb("x_all", [P, T, D])
        h_all = sb("h_all", [P, T, D])
        stage = sb("stage", [P, T * 512])
        acc = sb("acc", [P, T * HEADS * (C + 2)])
        ta = sb("ta", [P, T, D])
        tb = sb("tb", [P, T, D])
        rows = sb("rows", [P, RING, RANKS, 256])
        prod = sb("prod", [P, RANKS, D])
        pv = sb("pv", [P, RING, RANKS, HEADS * (C + 2)])
        slot = sb("slot", [P, RING, SLOT])
        sources = sb("sources", [P, RING, RANKS])
        ident = sb("ident", [P, P])
        onesf = sb("onesf", [P, P])
        tile_row = sb("tile_row", [1, ITEMS], U8)
        counts = sb("counts", [1, 4], I32)
        node_id = sb("node_id", [P, T], I32)
        node_start = sb("node_start", [P, T])
        node_deg = sb("node_deg", [P, T])
        x_id = sb("x_id", [P, T], I32)
        run_max = sb("run_max", [P, T, HEADS])
        qe = sb("qe", [P, T, HEADS])
        s = sb("s", [P, RANKS + 1, HEADS])
        s_w = sb("s_w", [P, RANKS, HEADS])
        mx = sb("mx", [P, HEADS])
        new_max = sb("new_max", [P, HEADS])
        dif = sb("dif", [P, RING, RANKS + 1, HEADS])
        alpha = sb("alpha", [P, RING, HEADS])
        htile = sb("htile", [P, GROUP, D])
        hT = sb("hT", [P, GROUP, D])
        sm = sb("sm", [P, 12, T])
        eps_ln = sb("eps_ln", [P, 1])
        ln_stats = sb("ln_stats", [P, T, 6])
        ln_mv = sb("ln_mv", [P, T, 2])
        left = sb("left", [P, T])
        n_blk = sb("n_blk", [1, 4, T])
        n_blk_i = sb("n_blk_i", [1, 2, T], I32)
        maxT = sb("maxT", [T, 1])
        per_tile = sb("per_tile", [P, 4, T])
        step_grid = sb("step_grid", [P, T])
        item_i = sb("item_i", [P, IC], I32)
        item_f = sb("item_f", [P, IC])
        tile_f = sb("tile_f", [P, IC])
        tile_u = sb("tile_u", [P, IC], U8)
        group_u = sb("group_u", [P, IC], U8)
        step_b = sb("step_b", [P, IC])
        step_off = ta[:, :, :].rearrange("p t d -> p (t d)")[:, 0:2 * IC * GROUP].rearrange("p (k n) -> p k n", k=2)
        step_off_i = tb[:, :, :].rearrange("p t d -> p (t d)")[:, 0:IC * 8].bitcast(I32).rearrange("p (i k) -> p i k", k=8)
        big = stage[:, 0:IC * T]
        big2 = stage[:, IC * T:2 * IC * T]
        group_row = acc[:, :].bitcast(U8)[0:1, 0:ITEMS]
        ps = ctx.enter_context(nc.psum_tensor("ps", [P, 8, 512], F32))

        w = {}
        vec = {}
        weight_parts = [("L1", [a["L1_gnn_W"]]), ("Win", [a["L2_gnn_W_in"]]), ("Wn", [a["L3_gnn_Wn"]]),
                        ("Wout", [a["L3_gnn_Wout"]])]
        vector_parts = [("att_src", [a["L1_gnn_att_src"].rearrange("h c -> (h c)")]),
                        ("att_dst", [a["L1_gnn_att_dst"].rearrange("h c -> (h c)")]),
                        ("L1_bias", [a["L1_gnn_bias"]]), ("L1_gamma", [a["L1_gnn_gamma"]]),
                        ("L1_beta", [a["L1_gnn_beta"]]), ("bin", [a["L2_gnn_b_in"]]),
                        ("bn", [a["L3_gnn_bn"]]), ("bout", [a["L3_gnn_bout"]])]
        for l in range(L2_LAYERS):
            vector_parts.append((f"We_{l}", [a["L2_gnn_We"][l, 0]]))
        for name, parts in weight_parts:
            w[name] = sb("w_" + name, [P, sum(p.shape[1] for p in parts)])
        for name, parts in vector_parts:
            vec[name] = sb("v_" + name, [P, sum(p.shape[0] for p in parts)])
        w_in = sb("w_in", [P, 4 * D])
        b_in = sb("b_in", [P, 4 * D])
        w_out = sb("w_out", [P, D])
        v_out = sb("v_out", [P, 5 * D])

        def into_layer(weights, biases):
            return [(w_in[:, k * D:(k + 1) * D], p) for k, p in enumerate(weights)] + [
                (b_in[:, k * D:(k + 1) * D], p.partition_broadcast(P)) for k, p in enumerate(biases)]

        def into_L2(l):
            return into_layer([a[f"L2_gnn_W{k}"][l] for k in ("k", "v", "q", "skip")],
                              [a[f"L2_gnn_b{k}"][l] for k in ("k", "v", "q", "skip")])

        def into_L3(l):
            return into_layer([a[f"L3_gnn_W{k}"][l] for k in ("K", "V", "Q")],
                              [a[f"L3_gnn_b{k}"][l] for k in ("K", "V", "Q")])

        def out_of_L2(l):
            return [(v_out[:, 0:3 * D], a["L2_gnn_Wbeta"][l].rearrange("k o -> (k o)").partition_broadcast(P)),
                    (v_out[:, 3 * D:4 * D], a["L2_gnn_bn_gamma"][l].partition_broadcast(P)),
                    (v_out[:, 4 * D:5 * D], a["L2_gnn_bn_beta"][l].partition_broadcast(P))]

        def out_of_L3(l):
            return [(w_out[:, :], a["L3_gnn_WO"][l])] + [
                (v_out[:, k * D:(k + 1) * D], a[f"L3_gnn_{n}"][l].partition_broadcast(P))
                for k, n in enumerate(("bO", "ln_g", "ln_b"))]

        params_in = Count(sem("params_in"))
        loaded = Count(sem("loaded"))
        x_gathered = Count(sem("x_gathered"))
        out_stored = Count(sem("out_stored"))
        stored = Count(sem("stored"))
        scattered = Count(sem("scattered"))
        vector_did = Count(sem("vector_did"))
        scalar_did = Count(sem("scalar_did"))
        tensor_did = Count(sem("tensor_did"))
        pool_did = Count(sem("pool_did"))
        hots_ready, hots_used = sem("hots_ready"), sem("hots_used")
        transposed, turned, staged_tile = sem("transposed"), sem("turned"), sem("staged_tile")
        projected, evacuated = sem("projected"), sem("evacuated")

        record_stored = [sem(f"record_stored{j}") for j in range(RECORDS)]
        record_gathered = [sem(f"record_gathered{j}") for j in range(RECORDS)]
        scan_slots_in = [sem(f"scan_slots_in{j}") for j in range(2)]
        scan_gathered = [sem(f"scan_gathered{j}") for j in range(2)]
        scan_did, scan_free, record_did = sem("scan_did"), sem("scan_free"), sem("record_did")
        sources_loaded = [sem(f"sources_loaded{j}") for j in range(RING)]
        slot_loaded = [sem(f"slot_loaded{j}") for j in range(RING)]
        rows_gathered = [sem(f"rows_gathered{j}") for j in range(RING)]
        pool_go, sync_go = sem("pool_go"), sem("sync_go")
        step_did = sem("step_did")
        shifted, exp_did, summed, ring_free = sem("shifted"), sem("exp_did"), sem("summed"), sem("ring_free")

        V, A, G, Q = nc.vector, nc.scalar, nc.gpsimd, nc.sync

        def vec_op(ins):
            vector_did.need(V, vector_did.did(ins))

        def act_op(ins):
            scalar_did.need(A, scalar_did.did(ins))

        def tiles(engine, quad):
            word = engine.value_load(tile_row.bitcast(I32)[0:1, bass.ds(quad, 1)], min_val=0, max_val=0x7FFFFFFF)
            return [engine.snap((word >> (8 * j)) & 31).with_bounds(min_val=0, max_val=T - 1) for j in range(4)]

        flat = lambda t3: t3.rearrange("p t d -> p (t d)")

        ones_col = sb("ones_col", [P, 1])
        iota_i = sb("iota_i", [P, P], I32)
        iota_f = sb("iota_f", [P, P])
        part_i = sb("part_i", [P, 1], I32)
        part_f = sb("part_f", [P, 1])
        below = sb("below", [P, P])
        valid = sb("valid", [P, P])
        iota_b = sb("iota_b", [P, P], BF16)
        rank_f = iota_f[:, 0:RANKS]

        at = [0]

        def scratch(n, dt=F32):
            size = n if dt in (F32, I32) else -(-n // 2)
            v = stage[:, at[0]:at[0] + size]
            at[0] += size + size % 2
            return v if dt == F32 else v.bitcast(dt)

        src_e, w_e, dst_e = scratch(EC + RANKS, I32), scratch(EC + RANKS), scratch(EC, I32)
        lo_i, hi_i = scratch(EC, I32), scratch(EC, I32)
        lo_b, hi_b = scratch(EC, BF16), scratch(EC, BF16)
        ebs = scratch(EC * 2 * RANKS).rearrange("p (e k) -> p e k", k=2 * RANKS)
        lo_hot = [scratch(CHUNK * P, BF16).rearrange("p (c n) -> p c n", n=P) for _ in range(2)]
        hi_hot = [scratch(CHUNK * T, BF16).rearrange("p (c n) -> p c n", n=T) for _ in range(2)]
        zero_b = scratch(P, BF16)

        with nc.Block() as block:
            @block.sync
            def _(sp):
                pool_did.need(sp, 3)
                params_in_now = [(src_e, a["src"]), (w_e, a["edge_weight1"].rearrange("e o -> (e o)"))]
                for dst, arr in params_in_now:
                    body = bass.AP(arr.tensor, arr.offset, [[EC, P - 1], [1, EC + RANKS]])
                    loaded.did(sp.dma_start(dst[0:P - 1, :], body), 16)
                    loaded.did(sp.dma_start(dst[P - 1:P, 0:EF], arr[EL * EC:E].rearrange("(o e) -> o e", o=1)), 16)
                arr = a["dst"]
                loaded.did(sp.dma_start(dst_e[0:P - 1, :], arr[0:EL * EC].rearrange("(p e) -> p e", e=EC)), 16)
                loaded.did(sp.dma_start(dst_e[P - 1:P, 0:EF], arr[EL * EC:E].rearrange("(o e) -> o e", o=1)), 16)
                for name, parts in weight_parts:
                    c = 0
                    for p in parts:
                        params_in.did(sp.dma_start(w[name][:, c:c + p.shape[1]], p), 16)
                        c += p.shape[1]
                for name, parts in vector_parts:
                    c = 0
                    for p in parts:
                        params_in.did(sp.dma_start(vec[name][:, c:c + p.shape[0]], p.partition_broadcast(P)), 16)
                        c += p.shape[0]
                loaded.need(sp, loaded.n)

            @block.gpsimd
            def _(pool):
                pool_did.did(G.memset(src_e, 0))
                pool_did.did(G.memset(w_e, 0.0))
                pool_did.did(G.memset(dst_e, NULL_KEY))
                pool_did.did(G.iota(iota_i[:, :], [[1, P]], 0, 0))
                pool_did.did(G.iota(part_i[:, :], [[0, 1]], 0, 1))
                pool_did.did(G.memset(onesf[:, :], 1.0))

            @block.vector
            def _(dve):
                pool_did.need(dve, 6)
                vec_op(V.tensor_copy(iota_f[:, :], iota_i[:, :]))
                vec_op(V.tensor_copy(iota_b[:, :], iota_i[:, :]))
                vec_op(V.tensor_copy(part_f[:, :], part_i[:, :]))
                vec_op(V.tensor_scalar(ident[:, :], iota_f[:, :], part_f[:, 0:1], None, ALU.is_equal))
                vec_op(V.tensor_scalar(below[:, :], iota_f[:, :], part_f[:, 0:1], None, ALU.is_gt))
                vec_op(V.tensor_scalar(part_f[:, 0:1], part_f[:, 0:1], float(LAST), None, ALU.is_lt))
                vec_op(V.tensor_scalar(valid[:, :], onesf[:, :], part_f[:, 0:1], None, ALU.mult))
                vec_op(V.memset(eps_ln[:, :], EPS_LN))
                vec_op(V.memset(zero_b, 0.0))

        hist = ps[:, 0, 0:T]
        cnt = sm[:, 0, :]
        start = sm[:, 1, :]
        with nc.Block() as block:
            @block.vector
            def _(dve):
                vec_op(V.tensor_scalar(lo_i, dst_e, P - 1, None, ALU.bitwise_and))
                vec_op(V.tensor_scalar(hi_i, dst_e, 7, None, ALU.logical_shift_right))
                vec_op(V.tensor_copy(lo_b, lo_i))
                vec_op(V.tensor_copy(hi_b, hi_i))
                with dve.Fori(0, EC // CHUNK // 2) as q:
                    for b in range(2):
                        dve.wait_ge(hots_used, 2 * q + b + 1)
                        cols = bass.ds(q * (2 * CHUNK) + b * CHUNK, CHUNK)
                        V.tensor_tensor(lo_hot[b], spread(lo_b[:, cols], 2, P), spread(iota_b[:, :], 1, CHUNK),
                                        ALU.is_equal).then_inc(hots_ready, 1)
                        V.tensor_tensor(hi_hot[b], spread(hi_b[:, cols], 2, T), spread(iota_b[:, 0:T], 1, CHUNK),
                                        ALU.is_equal).then_inc(hots_ready, 1)

            @block.tensor
            def _(pe):
                nc.tensor.matmul(hist, zero_b, zero_b[:, 0:T], start=True, stop=False,
                                 skip_group_check=True).then_inc(hots_used, 2)
                with pe.Fori(0, EC // CHUNK // 2) as q:
                    for b in range(2):
                        pe.wait_ge(hots_ready, 4 * q + 2 * b + 2)
                        for c in range(CHUNK):
                            mm = nc.tensor.matmul(hist, lo_hot[b][:, c, :], hi_hot[b][:, c, :],
                                                  start=False, stop=False, skip_group_check=True)
                        mm.then_inc(hots_used, 1)
                tensor_did.did(nc.tensor.matmul(hist, zero_b, zero_b[:, 0:T], start=False, stop=True,
                                                skip_group_check=True))

            @block.gpsimd
            def _(pool):
                for k in range(RANKS):
                    pool_did.did(G.tensor_copy(ebs.bitcast(I32)[:, :, k], src_e[:, k:k + EC]))
                    pool_did.did(G.tensor_copy(ebs[:, :, RANKS + k], w_e[:, k:k + EC]))

            @block.sync
            def _(sp):
                pool_did.need(sp, pool_did.n)
                stored.did(sp.dma_start(edge_rows.rearrange("(p e) k -> p (e k)", p=P),
                                        ebs.rearrange("p e k -> p (e k)")), 16)
                stored.need(sp, stored.n)

        key = sm[:, 2, :]
        pos = sm[:, 3, :]
        n_rev = sm[:, 4, :]
        pos_i = sb("pos_i", [P, T], I32)
        n_i = sb("n_i", [P, T], I32)
        rec = sb("rec", [P, T, 4], I32)
        keyT = sb("keyT", [T, P])
        with nc.Block() as block:
            @block.gpsimd
            def _(pool):
                pool_did.did(G.iota(n_i[:, :], [[P, T]], 0, 1))

            @block.vector
            def _(dve):
                vec_op(V.tensor_copy(cnt, hist))
                pool_did.need(dve, pool_did.n)
                vec_op(V.tensor_copy(n_rev, n_i[:, :]))
                vec_op(V.tensor_scalar(n_rev, n_rev, -1.0, 4095.0, ALU.mult, ALU.add))
                vec_op(V.tensor_scalar(key, cnt, 4095.0, 4096.0, ALU.min, ALU.mult))
                vec_op(V.tensor_tensor(key, key, n_rev, ALU.add))

            @block.tensor
            def _(pe):
                vector_did.need(pe, vector_did.n)
                nc.tensor.matmul(ps[:, 1, 0:T], below[:, :], cnt, start=True, stop=True)
                nc.tensor.matmul(ps[:, 2, 0:T], onesf[:, :], cnt, start=True, stop=True)
                tensor_did.did(nc.tensor.transpose(ps[0:T, 3, 0:P], key, ident[:, :]))

            @block.scalar
            def _(act):
                tensor_did.need(act, tensor_did.n)
                scalar_did.did(A.copy(keyT[:, :], ps[0:T, 3, 0:P]))

            @block.sync
            def _(sp):
                scalar_did.need(sp, scalar_did.n)
                stored.did(sp.dma_start(key_row, keyT[:, :]), 16)
                stored.need(sp, stored.n)
                loaded.did(sp.dma_start(flat(ta[:, :, :]), key_row.rearrange("t p -> (t p)").partition_broadcast(P)), 16)
                loaded.need(sp, loaded.n)

        keys_ready = vector_did.n + 9
        with nc.Block() as block:
            @block.vector
            def _(dve):
                vec_op(V.tensor_copy(sm[:, 5, :], ps[:, 2, 0:T]))
                vec_op(V.tensor_tensor_scan(sm[:, 6, :], onesf[:, 0:T], sm[:, 5, :], 0.0, ALU.mult, ALU.add))
                vec_op(V.tensor_tensor(start, sm[:, 6, :], sm[:, 5, :], ALU.subtract))
                vec_op(V.tensor_tensor(start, start, ps[:, 1, 0:T], ALU.add))
                vec_op(V.tensor_copy(rec[:, :, 0], n_i[:, :]))
                vec_op(V.tensor_copy(rec[:, :, 1], start))
                vec_op(V.tensor_copy(rec[:, :, 2], cnt))
                vec_op(V.memset(rec[:, :, 3], 0))
                vec_op(V.tensor_scalar(sm[:, 5, :], key, -1.0, None, ALU.mult))
                for t in range(RANK_VECTOR_TILES):
                    vec_op(V.tensor_scalar(flat(tb[:, :, :]), flat(ta[:, :, :]), key[:, t:t + 1], 0.0,
                                           ALU.is_gt, ALU.add, accum_out=pos[:, t:t + 1]))
                    vec_op(V.tensor_copy(pos_i[:, t:t + 1], pos[:, t:t + 1]))
                scalar_did.need(dve, scalar_did.n + T - RANK_VECTOR_TILES)
                rest = slice(RANK_VECTOR_TILES, T)
                vec_op(V.tensor_scalar(pos[:, rest], pos[:, rest], float(NP - 1), 0.5, ALU.add, ALU.mult))
                vec_op(V.tensor_copy(pos_i[:, rest], pos[:, rest]))

            @block.scalar
            def _(act):
                vector_did.need(act, keys_ready)
                for t in range(RANK_VECTOR_TILES, T):
                    act_op(A.activation(flat(h_all[:, :, :]), flat(ta[:, :, :]), ACT.Sign, bias=sm[:, 5, t:t + 1],
                                        accum_out=pos[:, t:t + 1]))

            @block.gpsimd
            def _(pool):
                for t in range(T):
                    vector_did.need(pool, min(keys_ready + 2 * t + 2, vector_did.n))
                    scattered.did(G.indirect_dma_start(
                        out=ranked, out_offset=bass.IndirectOffsetOnAxis(ap=pos_i[:, t:t + 1], axis=0),
                        in_=rec[:, t, :], in_offset=None), 16)

            @block.sync
            def _(sp):
                scattered.need(sp, scattered.n)
                loaded.did(sp.dma_start(rec[:, :, :], ranked.rearrange("(t p) c -> p t c", p=P)), 16)
                loaded.need(sp, loaded.n)

        def vector_block(*steps):
            with nc.Block() as block:
                @block.vector
                def _(dve):
                    for step in steps:
                        vec_op(step())

        def load_and_wait(*copies):
            with nc.Block() as block:
                @block.sync
                def _(sp):
                    for dst, src in copies:
                        loaded.did(sp.dma_start(dst, src), 16)
                    loaded.need(sp, loaded.n)

        vector_block(
            lambda: V.tensor_scalar(x_id[:, :], rec[:, :, 0], float(N - 1), None, ALU.min),
            lambda: V.tensor_copy(node_id[:, :], rec[:, :, 0]),
            lambda: V.tensor_copy(node_start[:, :], rec[:, :, 1]),
            lambda: V.tensor_copy(node_deg[:, :], rec[:, :, 2]),
            lambda: V.tensor_copy(left[:, :], rec[:, :, 2]))

        with nc.Block() as block:
            @block.tensor
            def _(pe):
                tensor_did.did(nc.tensor.transpose(ps[0:T, 0, 0:P], node_deg[:, :], ident[:, :]))

            @block.vector
            def _(dve):
                tensor_did.need(dve, tensor_did.n)
                vec_op(V.tensor_reduce(maxT[:, :], ps[0:T, 0, 0:P], X, ALU.max))

        with nc.Block() as block:
            @block.tensor
            def _(pe):
                tensor_did.did(nc.tensor.transpose(ps[0:1, 1, 0:T], maxT[:, :], ident[0:T, 0:T]))

            @block.vector
            def _(dve):
                tensor_did.need(dve, tensor_did.n)
                row = lambda k: n_blk[:, k, :]
                vec_op(V.tensor_scalar(row(0), ps[0:1, 1, 0:T], float(RANKS - 1), None, ALU.add))
                vec_op(V.tensor_copy(n_blk_i[:, 0, :], row(0)))
                vec_op(V.tensor_scalar(n_blk_i[:, 1, :], n_blk_i[:, 0, :], 2, None, ALU.arith_shift_right))
                vec_op(V.tensor_copy(row(0), n_blk_i[:, 1, :]))
                vec_op(V.tensor_tensor_scan(row(2), onesf[0:1, 0:T], row(0), 0.0, ALU.mult, ALU.add))
                vec_op(V.tensor_tensor(row(1), row(2), row(0), ALU.subtract))
                vec_op(V.memset(row(3), 0.0))
                vec_op(V.tensor_reduce(n_blk[:, 3, 0:GROUPS], row(0).rearrange("p (g k) -> p g k", k=GROUP), X, ALU.max))
                vec_op(V.tensor_tensor_scan(n_blk[:, 3, GROUPS:2 * GROUPS], onesf[0:1, 0:GROUPS],
                                            n_blk[:, 3, 0:GROUPS], 0.0, ALU.mult, ALU.add))
                vec_op(V.tensor_copy(n_blk_i[:, 0, 0:1], n_blk[:, 2, T - 1:T]))
                vec_op(V.tensor_scalar(n_blk_i[:, 0, 1:2], n_blk[:, 2, T - 1:T], float(RING - 1), None, ALU.add))
                vec_op(V.tensor_scalar(n_blk_i[:, 0, 2:3], n_blk[:, 3, 2 * GROUPS - 1:2 * GROUPS], 1.0, None, ALU.add))
                vec_op(V.tensor_scalar(counts[:, 0:1], n_blk_i[:, 0, 1:2], 2, None, ALU.arith_shift_right))
                vec_op(V.tensor_scalar(counts[:, 1:2], n_blk_i[:, 0, 0:1], 3, None, ALU.arith_shift_right))
                vec_op(V.tensor_scalar(counts[:, 0:1], counts[:, 0:1], 2.0, None, ALU.max))
                vec_op(V.tensor_scalar(counts[:, 1:2], counts[:, 1:2], 1.0, None, ALU.add))
                vec_op(V.tensor_scalar(counts[:, 3:4], counts[:, 0:1], -1.0, None, ALU.add))
                vec_op(V.tensor_scalar(counts[:, 2:3], n_blk_i[:, 0, 2:3], 1, None, ALU.arith_shift_right))

            @block.gpsimd
            def _(pool):
                pool_did.did(G.iota(item_i[:, :], [[1, IC]], 0, IC))

        with nc.Block() as block:
            @block.tensor
            def _(pe):
                tensor_did.did(nc.tensor.matmul(ps[:, 2, 0:4 * T], onesf[0:1, :], n_blk[:, :, :].rearrange("p k t -> p (k t)"),
                                                start=True, stop=True))

            @block.vector
            def _(dve):
                tensor_did.need(dve, tensor_did.n)
                vec_op(V.tensor_copy(per_tile[:, :, :].rearrange("p k t -> p (k t)"), ps[:, 2, 0:4 * T]))
                vec_op(V.tensor_copy(item_f[:, :], item_i[:, :]))
                blocks, before, upto = per_tile[:, 0, :], per_tile[:, 1, :], per_tile[:, 2, :]
                g_blocks, g_upto = per_tile[:, 3, 0:GROUPS], per_tile[:, 3, GROUPS:2 * GROUPS]
                all_items = per_tile[:, 2, T - 1:T]
                by_tile = big.rearrange("p (i t) -> p i t", t=T)
                by_group = big2[:, 0:IC * GROUPS].rearrange("p (i g) -> p i g", g=GROUPS)
                by_both = big.rearrange("p (i k g) -> p i k g", k=GROUP, g=GROUPS)
                vec_op(V.tensor_tensor(by_tile, spread(item_f[:, :], 2, T), spread(upto, 1, IC), ALU.is_ge))
                vec_op(V.tensor_reduce(tile_f[:, :], by_tile, X, ALU.add))
                vec_op(V.tensor_scalar(tile_f[:, :], tile_f[:, :], float(T - 1), None, ALU.min))
                vec_op(V.tensor_copy(tile_u[:, :], tile_f[:, :]))
                vec_op(V.tensor_tensor(by_group, spread(item_f[:, :], 2, GROUPS), spread(g_upto, 1, IC), ALU.is_ge))
                vec_op(V.tensor_reduce(tile_f[:, :], by_group, X, ALU.add))
                vec_op(V.tensor_scalar(tile_f[:, :], tile_f[:, :], float(GROUPS - 1), None, ALU.min))
                vec_op(V.tensor_copy(group_u[:, :], tile_f[:, :]))
                vec_op(V.tensor_tensor(by_group, by_group, spread(g_blocks, 1, IC), ALU.mult))
                vec_op(V.tensor_reduce(step_b[:, :], by_group[:, :, 0:GROUPS - 1], X, ALU.add))
                vec_op(V.tensor_tensor(step_b[:, :], item_f[:, :], step_b[:, :], ALU.subtract))
                vec_op(V.tensor_tensor(by_group, spread(tile_f[:, :], 2, GROUPS), spread(iota_f[:, 0:GROUPS], 1, IC), ALU.is_equal))
                for k, what in ((0, blocks), (1, before)):
                    grid = what.rearrange("p (g k) -> p k g", k=GROUP)
                    vec_op(V.tensor_copy(step_grid[:, :], grid))
                    vec_op(V.tensor_tensor(by_both, spread(by_group, 2, GROUP),
                                           spread(step_grid[:, :].rearrange("p (k g) -> p k g", g=GROUPS), 1, IC), ALU.mult))
                    vec_op(V.tensor_reduce(step_off[:, k, :], by_both, X, ALU.add))
                off = lambda k: step_off[:, k, :].rearrange("p (i k) -> p i k", k=GROUP)
                vec_op(V.tensor_tensor(off(0), off(0), spread(step_b[:, :], 2, GROUP), ALU.is_gt))
                vec_op(V.tensor_tensor(off(1), off(1), spread(step_b[:, :], 2, GROUP), ALU.add))
                vec_op(V.tensor_scalar(off(1), off(1), all_items, None, ALU.subtract))
                vec_op(V.tensor_tensor(off(1), off(1), off(0), ALU.mult))
                vec_op(V.tensor_scalar(off(1), off(1), all_items, None, ALU.add))
                vec_op(V.memset(step_off_i[:, :, :], 0))
                vec_op(V.tensor_copy(step_off_i[:, :, 0:GROUP], off(1)))

            @block.gpsimd
            def _(pool):
                for t in range(T):
                    x_gathered.did(G.indirect_dma_start(
                        out=x_all[:, t, :], out_offset=None, in_=a["x"],
                        in_offset=bass.IndirectOffsetOnAxis(ap=x_id[:, t:t + 1], axis=0)), 16)
                x_gathered.need(pool, x_gathered.n)

            @block.sync
            def _(sp):
                vector_did.need(sp, vector_did.n)
                stored.did(sp.dma_start(tile_of_item, tile_u[:, :]), 16)
                stored.did(sp.dma_start(group_of_step, group_u[:, :]), 16)
                stored.did(sp.dma_start(step_items.rearrange("(p i) k -> p (i k)", p=P),
                                        step_off_i[:, :, :].rearrange("p i k -> p (i k)")), 16)
                stored.need(sp, stored.n)
                loaded.did(sp.dma_start(tile_row[:, :], tile_of_item.rearrange("(o p) i -> o (p i)", o=1)), 16)
                loaded.did(sp.dma_start(group_row, group_of_step.rearrange("(o p) i -> o (p i)", o=1)), 16)
                loaded.need(sp, loaded.n)

        index_of = sb("index_of", [P, RECORDS], I32)
        record = sb("record", [P, RECORDS, SLOT])
        with nc.Block() as block:
            @block.vector
            def _(dve):
                for first, credit in ((record_did, 1), (scan_did, 1), (step_did, RING * STEPS + 1), (ring_free, RING), (scan_free, 2)):
                    V.sem_inc(first, credit)

            @block.tensor
            def _(pe):
                nc.tensor.sem_inc(evacuated, GROUP)
                nc.tensor.sem_inc(projected, 1)

            @block.sync
            def _(sp):
                for j in range(RECORDS):
                    sp.sem_inc(record_stored[j], 16)

        with nc.Block() as block:
            @block.vector
            def _(dve):
                n = dve.value_load(counts[0:1, 1:2], min_val=1, max_val=ITEMS // RECORDS - 2)
                with dve.Fori(0, n) as q:
                    tile_of = tiles(dve, q * 2) + tiles(dve, q * 2 + 1)
                    for j in range(RECORDS):
                        did = Count(record_did, q * (5 * RECORDS) + (5 * j + 1))
                        t = tile_of[j]
                        dve.wait_ge(record_stored[j], q * 16 + 16)
                        dve.wait_ge(record_did, q * (5 * RECORDS) + (5 * j + 1))
                        node = node_start[:, bass.ds(t, 1)]
                        rest = left[:, bass.ds(t, 1)]
                        did.did(V.tensor_scalar(index_of[:, j:j + 1], node, float(E), None, ALU.min))
                        did.did(V.tensor_scalar(record[:, j, 3 * RANKS:4 * RANKS], rank_f, rest, None, ALU.is_lt))
                        did.need(dve, 2)
                        did.did(V.tensor_scalar(node, node, float(RANKS), None, ALU.add))
                        did.did(V.tensor_scalar(rest, rest, -float(RANKS), None, ALU.add))
                        did.did(V.tensor_scalar(record[:, j, 2 * RANKS:3 * RANKS], record[:, j, 3 * RANKS:4 * RANKS],
                                                MASKED, -MASKED, ALU.mult, ALU.add))

            @block.gpsimd
            def _(pool):
                n = pool.value_load(counts[0:1, 1:2], min_val=1, max_val=ITEMS // RECORDS - 2)
                with pool.Fori(0, n) as q:
                    for j in range(RECORDS):
                        pool.wait_ge(record_did, q * (5 * RECORDS) + (5 * j + 2))
                        pool.sem_inc(pool_go, 1)
                        G.indirect_dma_start(
                            out=record[:, j, 0:2 * RANKS], out_offset=None, in_=edge_rows,
                            in_offset=bass.IndirectOffsetOnAxis(ap=index_of[:, j:j + 1], axis=0)
                        ).then_inc(record_gathered[j], 16)

            @block.sync
            def _(sp):
                n = sp.value_load(counts[0:1, 1:2], min_val=1, max_val=ITEMS // RECORDS - 2)
                with sp.Fori(0, n) as q:
                    for j in range(RECORDS):
                        sp.wait_ge(record_did, q * (5 * RECORDS) + (5 * j + 6))
                        sp.wait_ge(record_gathered[j], q * 16 + 16)
                        sp.dma_start(slots[bass.ds(q * RECORDS + j, 1), :, :].rearrange("o p k -> p (o k)"),
                                     record[:, j, :]).then_inc(record_stored[j], 16)
                for j in range(RECORDS):
                    sp.wait_ge(record_stored[j], n * 16 + 16)
                    sp.sem_inc(sync_go, 1)

        def copy_all(dst, src):
            vector_block(lambda: V.tensor_copy(dst, src))

        def layer_norm(dst, src, relu=False, gamma=None, beta=None):
            stats, mean_var, rstd, shift = ln_stats[:, :, :], ln_mv[:, :, :], sm[:, 0, :], sm[:, 1, :]
            with nc.Block() as block:
                @block.vector
                def _(dve):
                    for t in range(T):
                        mark = vector_did.did(V.bn_stats(stats[:, t, :], src[:, t, :]))
                    for t in range(T):
                        if t == 0:
                            vector_did.need(dve, mark)
                        mark = vector_did.did(V.bn_aggr(mean_var[:, t, :], stats[:, t, :]))
                    scalar_did.need(dve, scalar_did.n + 1)
                    vec_op(V.reciprocal(rstd, rstd))
                    vec_op(V.scalar_tensor_tensor(out=shift, in0=mean_var[:, :, 0], scalar=-1.0, in1=rstd,
                                                  op0=ALU.mult, op1=ALU.mult))
                    for t in range(LN_VECTOR_TILES):
                        did = vector_did.did(V.tensor_scalar(dst[:, t, :], src[:, t, :], rstd[:, t:t + 1], shift[:, t:t + 1],
                                                             ALU.mult, ALU.add))
                    part = dst[:, 0:LN_VECTOR_TILES, :]
                    vector_did.need(dve, did)
                    if relu:
                        vec_op(V.tensor_scalar(part, part, 0.0, None, ALU.max))
                    if gamma is not None:
                        vec_op(V.tensor_tensor(part, part, spread(gamma, 1, LN_VECTOR_TILES), ALU.mult))
                        vec_op(V.tensor_tensor(part, part, spread(beta, 1, LN_VECTOR_TILES), ALU.add))
                        part = dst[:, LN_VECTOR_TILES:T, :]
                        scalar_did.need(dve, scalar_did.n + 1 + T - LN_VECTOR_TILES)
                        vec_op(V.tensor_tensor(part, part, spread(gamma, 1, T - LN_VECTOR_TILES), ALU.mult))
                        vec_op(V.tensor_tensor(part, part, spread(beta, 1, T - LN_VECTOR_TILES), ALU.add))

                after_shift = vector_did.n - (4 if gamma is not None else 1 if relu else 0) - LN_VECTOR_TILES

                @block.scalar
                def _(act):
                    vector_did.need(act, after_shift - 2)
                    scalar_did.did(A.activation(rstd, mean_var[:, :, 1], ACT.Sqrt, bias=eps_ln[:, 0:1]))
                    vector_did.need(act, after_shift)
                    for t in range(LN_VECTOR_TILES, T):
                        scalar_did.did(A.activation(dst[:, t, :], src[:, t, :], ACT.Relu if relu else ACT.Identity,
                                                    bias=shift[:, t:t + 1], scale=rstd[:, t:t + 1]))

        projections = [0]

        def project(src, weight, bias, dst_of, cols, table=None, width=0):
            base = projections[0] * T
            projections[0] += 1
            with nc.Block() as block:
                @block.scalar
                def _(act):
                    with act.Fori(0, T // GROUP) as q:
                        A.copy(htile[:, :, :].rearrange("p k d -> p (k d)"),
                               src[:, bass.ds(q * (GROUP * D), GROUP * D)]).then_inc(staged_tile, 1)
                        act.wait_ge(transposed, q + (base // GROUP + 1))
                        act.wait_ge(projected, q * GROUP + (base + 1))
                        hT_flat = hT[:, :, :].rearrange("p k d -> p (k d)")
                        A.copy(hT_flat[:, 0:4 * D], ps[:, 5, :])
                        A.copy(hT_flat[:, 4 * D:GROUP * D], ps[:, 6, 0:D]).then_inc(turned, 1)

                @block.tensor
                def _(pe):
                    with pe.Fori(0, T // GROUP) as q:
                        pe.wait_ge(staged_tile, q + (base // GROUP + 1))
                        for k in range(GROUP):
                            mm = nc.tensor.transpose(ps[:, 5 + k // 4, (k % 4) * D:(k % 4) * D + D], htile[:, k, :], ident[:, :])
                        mm.then_inc(transposed, 1)
                        pe.wait_ge(turned, q + (base // GROUP + 1))
                        for k in range(GROUP):
                            pe.wait_ge(evacuated, q * GROUP + (base + k + 1))
                            nc.tensor.matmul(ps[:, k, 0:cols], hT[:, k, :], weight, start=True,
                                             stop=True).then_inc(projected, 1)

                @block.vector
                def _(dve):
                    with dve.Fori(0, T // GROUP) as q:
                        for k in range(GROUP):
                            dve.wait_ge(projected, q * GROUP + (base + k + 2))
                            if bias is None:
                                V.tensor_scalar(dst_of(q * GROUP + k), ps[:, k, 0:cols], 1.0, None, ALU.mult
                                                ).then_inc(evacuated, 1)
                            else:
                                V.tensor_tensor(dst_of(q * GROUP + k), ps[:, k, 0:cols], bias, ALU.add
                                                ).then_inc(evacuated, 1)

                if table is not None:
                    @block.gpsimd
                    def _(pool):
                        for t in range(T):
                            pool.wait_ge(evacuated, base + GROUP + t + 1)
                            scattered.did(G.indirect_dma_start(
                                out=table, out_offset=bass.IndirectOffsetOnAxis(ap=node_id[:, t:t + 1], axis=0),
                                in_=stage[:, t * width:t * width + table.shape[1]], in_offset=None), 16)
                        scattered.need(pool, scattered.n)

        def scatter(table, width):
            with nc.Block() as block:
                @block.gpsimd
                def _(pool):
                    for t in range(T):
                        scattered.did(G.indirect_dma_start(
                            out=table, out_offset=bass.IndirectOffsetOnAxis(ap=node_id[:, t:t + 1], axis=0),
                            in_=stage[:, t * width:t * width + table.shape[1]], in_offset=None), 16)
                    scattered.need(pool, scattered.n)

        layer_norm(h_all[:, :, :], x_all[:, :, :], relu=True)
        TW = row_width[0]
        table_rows = stage[:, 0:T * TW].rearrange("p (t d) -> p t d", d=TW)
        u_all = stage[:, T * TW:T * TW + T * D]
        ring0 = stage[:, T * (TW + D):T * (TW + D) + 2 * RANKS * GROUP * TW].rearrange(
            "p (j r k d) -> p j r k d", j=2, r=RANKS, k=GROUP)
        slot0 = sb("slot0", [P, 2, GROUP, SLOT])
        y2_all = sb("y2_all", [P, T])
        state = sb("state", [P, GROUPS * 4 * GROUP])
        RG = RANKS * GROUP
        e_c, e_a, e_al, e_den, e_t, e_t2 = (sb(f"edge_{n}", [P, RG]) for n in ("c", "a", "al", "den", "t", "t2"))
        e_ac = sb("edge_ac", [P, RANKS, 2, GROUP])
        e_v = sb("edge_v", [P, RANKS, 4, GROUP])
        r_s = {n: sb("r_" + n, [P, GROUP]) for n in ("ts", "om", "rest", "hu", "xy", "den", "num", "ba")}
        r_t = sb("r_t", [P, 2, GROUP])
        r_ab = sb("r_ab", [P, 2, GROUP])
        r_v1 = sb("r_v1", [P, 4, GROUP])
        r_v2 = sb("r_v2", [P, 4, GROUP])
        PRE, PER = 24, 26
        vector_block(
            lambda: V.tensor_tensor(ta[:, :, :], h_all[:, :, :], h_all[:, :, :], ALU.mult),
            lambda: V.tensor_reduce(y2_all[:, :], ta[:, :, :], X, ALU.add),
            lambda: V.memset(table_rows[:, :, D:TW], 0.0),
            lambda: V.tensor_copy(table_rows[:, :, D], y2_all[:, :]),
            lambda: V.tensor_copy(table_rows[:, :, 0:D], h_all[:, :, :]),
            lambda: V.memset(u_all, 0.0),
            lambda: V.memset(state[:, :], 0.0))
        scatter(tables[0], TW)

        with nc.Block() as block:
            @block.sync
            def _(sp):
                n = sp.value_load(counts[0:1, 2:3], min_val=1, max_val=ITEMS // 2 - 1)
                with sp.Fori(0, n) as q:
                    for j in range(2):
                        sp.wait_ge(scan_free, q * 2 + (j + 1))
                        sp.sem_inc(sync_go, 1)
                        for k in range(GROUP):
                            item = sp.value_load(step_items[bass.ds(q * 2 + j, 1), k:k + 1], min_val=0, max_val=ITEMS - 1)
                            sp.dma_start(slot0[:, j, k, :], slots[bass.ds(item, 1), :, :].rearrange("o p k -> p (o k)")
                                         ).then_inc(scan_slots_in[j], 16)

            @block.gpsimd
            def _(pool):
                n = pool.value_load(counts[0:1, 2:3], min_val=1, max_val=ITEMS // 2 - 1)
                with pool.Fori(0, n) as q:
                    for j in range(2):
                        pool.wait_ge(scan_slots_in[j], q * (16 * GROUP) + 16 * GROUP)
                        pool.sem_inc(pool_go, 1)
                        for r in range(RANKS):
                            for k in range(GROUP):
                                G.indirect_dma_start(
                                    out=ring0[:, j, r, k, :], out_offset=None, in_=tables[0],
                                    in_offset=bass.IndirectOffsetOnAxis(ap=slot0[:, j, k, r:r + 1].bitcast(I32), axis=0)
                                ).then_inc(scan_gathered[j], 16)

            @block.vector
            def _(dve):
                K = PRE + RANKS * PER
                n = dve.value_load(counts[0:1, 2:3], min_val=1, max_val=ITEMS // 2 - 1)
                with dve.Fori(0, n) as q:
                    for j in range(2):
                        base = dve.snap(q * (2 * K) + (j * K + 1))
                        did = Count(scan_did, base)
                        g = dve.value_load(group_row[0:1, bass.ds(q * 2 + j, 1)], min_val=0, max_val=GROUPS - 1)
                        h_g = flat(h_all[:, :, :])[:, bass.ds(g * (GROUP * D), GROUP * D)].rearrange("p (k d) -> p k d", k=GROUP)
                        u_g = u_all[:, bass.ds(g * (GROUP * D), GROUP * D)].rearrange("p (k d) -> p k d", k=GROUP)
                        y2 = y2_all[:, bass.ds(g * GROUP, GROUP)]
                        st = lambda a0, a1: state[:, bass.ds(g * (4 * GROUP) + a0 * GROUP, (a1 - a0) * GROUP)].rearrange(
                            "p (c k) -> p c k", k=GROUP)
                        st1 = lambda a0: state[:, bass.ds(g * (4 * GROUP) + a0 * GROUP, GROUP)]
                        rk = lambda t: t[:, :].rearrange("p (r k) -> p r k", k=GROUP)
                        src_h = ring0[:, j, :, :, 0:D]
                        x2 = ring0[:, j, :, :, D]
                        mask = slot0[:, j, :, 3 * RANKS:4 * RANKS].rearrange("p k r -> p r k")
                        tmp = flat(ta[:, :, :])[:, 0:RG * D].rearrange("p (r k d) -> p r k d", r=RANKS, k=GROUP)
                        y2r = spread(y2, 1, RANKS)

                        def op(ins, by=1):
                            did.need(dve, did.did(ins, by))

                        dve.wait_ge(scan_gathered[j], q * (16 * RG) + 16 * RG)
                        dve.wait_ge(scan_did, base)
                        op(V.tensor_tensor(tmp, src_h, spread(h_g, 1, RANKS), ALU.mult))
                        op(V.tensor_reduce(rk(e_c), tmp, X, ALU.add))
                        op(V.tensor_scalar(e_a[:, :], e_c[:, :], -2.0, 1.0, ALU.mult, ALU.add))
                        op(V.tensor_tensor(rk(e_den), x2, y2r, ALU.mult))
                        op(V.tensor_tensor(e_den[:, :], e_den[:, :], e_a[:, :], ALU.add))
                        op(V.tensor_scalar(e_den[:, :], e_den[:, :], EPS_BALL, None, ALU.max))
                        op(V.reciprocal(e_den[:, :], e_den[:, :]))
                        op(V.tensor_tensor(rk(e_den), rk(e_den), mask, ALU.mult))
                        op(V.tensor_tensor(rk(e_a), rk(e_a), y2r, ALU.add))
                        op(V.tensor_tensor(e_al[:, :], e_a[:, :], e_den[:, :], ALU.mult))
                        op(V.tensor_scalar(rk(e_t), x2, -1.0, None, ALU.add))
                        op(V.tensor_tensor(e_ac[:, :, 1, :], rk(e_t), rk(e_den), ALU.mult))
                        op(V.tensor_copy(e_v[:, :, 0, :], e_ac[:, :, 1, :]))
                        op(V.tensor_tensor(e_ac[:, :, 0, :], rk(e_al), rk(e_c), ALU.mult))
                        op(V.tensor_tensor(rk(e_t), e_ac[:, :, 1, :], y2r, ALU.mult))
                        op(V.tensor_tensor(e_v[:, :, 1, :], rk(e_t), e_ac[:, :, 0, :], ALU.add))
                        op(V.tensor_tensor(rk(e_t), rk(e_al), x2, ALU.mult))
                        op(V.tensor_tensor(rk(e_t2), e_ac[:, :, 1, :], rk(e_c), ALU.mult))
                        op(V.tensor_tensor(e_t[:, :], e_t[:, :], e_t2[:, :], ALU.add))
                        op(V.tensor_tensor(e_t[:, :], e_t[:, :], e_al[:, :], ALU.mult))
                        op(V.tensor_tensor(rk(e_t2), e_ac[:, :, 1, :], e_v[:, :, 1, :], ALU.mult))
                        op(V.tensor_tensor(e_v[:, :, 3, :], rk(e_t), rk(e_t2), ALU.add), by=PRE - did.n)
                        for r in range(RANKS):
                            hs = ring0[:, j, r, :, 0:D]
                            t_u = tmp[:, 0]
                            t_w = tmp[:, 1]
                            al = rk(e_al)[:, r, :]
                            R = {k: v[:, :] for k, v in r_s.items()}
                            begin = did.n
                            uh = did.did(V.tensor_tensor(t_u, hs, u_g, ALU.mult))
                            op(V.tensor_tensor(r_t[:, :, :], st(0, 2), e_ac[:, r, :, :], ALU.mult))
                            op(V.tensor_tensor(R["ts"], r_t[:, 0, :], r_t[:, 1, :], ALU.add))
                            op(V.tensor_reduce(R["hu"], t_u, X, ALU.add))
                            did.did(V.tensor_tensor(R["om"], st1(2), e_v[:, r, 3, :], ALU.mult))
                            op(V.tensor_tensor(R["xy"], R["hu"], al, ALU.mult))
                            did.did(V.tensor_scalar(R["rest"], st1(2), -1.0, 1.0, ALU.mult, ALU.add))
                            op(V.tensor_tensor(st1(3), R["xy"], R["ts"], ALU.add))
                            did.did(V.tensor_tensor(e_v[:, r, 2, :], R["xy"], R["ts"], ALU.add))
                            op(V.scalar_tensor_tensor(out=R["den"], in0=st1(3), scalar=2.0, in1=R["om"], op0=ALU.mult, op1=ALU.add))
                            did.did(V.scalar_tensor_tensor(out=R["num"], in0=st1(3), scalar=2.0, in1=e_v[:, r, 3, :],
                                                           op0=ALU.mult, op1=ALU.add))
                            op(V.tensor_scalar(R["den"], R["den"], 1.0, EPS_BALL, ALU.add, ALU.max))
                            op(V.reciprocal(R["den"], R["den"]))
                            did.did(V.scalar_tensor_tensor(out=r_ab[:, 0, :], in0=R["num"], scalar=1.0, in1=R["den"],
                                                           op0=ALU.add, op1=ALU.mult))
                            op(V.tensor_tensor(r_ab[:, 1, :], R["rest"], R["den"], ALU.mult))
                            did.did(V.tensor_tensor(r_v1[:, :, :], st(0, 4), spread(r_ab[:, 0, :], 1, 4), ALU.mult))
                            op(V.tensor_tensor(R["ba"], r_ab[:, 1, :], al, ALU.mult))
                            did.did(V.tensor_tensor(t_w, hs, spread(R["ba"], 2, D), ALU.mult))
                            did.did(V.tensor_tensor(r_v2[:, :, :], e_v[:, r, :, :], spread(r_ab[:, 1, :], 1, 4), ALU.mult))
                            op(V.tensor_tensor(u_g, u_g, spread(r_ab[:, 0, :], 2, D), ALU.mult))
                            did.did(V.tensor_tensor(st(0, 4), r_v1[:, :, :], r_v2[:, :, :], ALU.add))
                            op(V.tensor_tensor(u_g, u_g, t_w, ALU.add))
                            op(V.tensor_tensor(r_t[:, :, :], st(2, 4), r_ab[:, :, :], ALU.mult))
                            last = V.tensor_tensor(st1(2), r_t[:, 0, :], r_t[:, 1, :], ALU.add)
                            if r < RANKS - 1:
                                op(last, by=PER - (did.n - begin))
                            else:
                                did.did(last, by=PER - (did.n - begin))
                        did.need(dve, did.n)
                        V.memset(r_t[:, 0, 0:1], 0.0).then_inc(scan_free, 1)

        by_g = lambda t3: t3.rearrange("p (g k) d -> p g k d", k=GROUP)
        gamma_g = state[:, :].rearrange("p (g c k) -> p g c k", c=4, k=GROUP)[:, :, 0, :]
        total_v = stage[:, 0:T * D].rearrange("p (t d) -> p t d", d=D)
        nrm, ratio, k1, k2, k3, k4, k5, k6 = (sm[:, n, :] for n in range(8))
        vector_block(
            lambda: V.tensor_tensor(by_g(ta[:, :, :]), by_g(h_all[:, :, :]), spread(gamma_g, 3, D), ALU.mult),
            lambda: V.tensor_tensor(total_v, ta[:, :, :], u_all.rearrange("p (t d) -> p t d", d=D), ALU.add),
            lambda: V.tensor_tensor(ta[:, :, :], total_v, total_v, ALU.mult),
            lambda: V.tensor_reduce(k6, ta[:, :, :], X, ALU.add),
            lambda: V.tensor_tensor(ta[:, :, :], total_v, h_all[:, :, :], ALU.mult),
            lambda: V.tensor_reduce(k5, ta[:, :, :], X, ALU.add),
            lambda: V.tensor_scalar(k4, node_deg[:, :], 1.0, None, ALU.max),
            lambda: V.reciprocal(k4, k4))
        with nc.Block() as block:
            @block.scalar
            def _(act):
                scalar_did.did(A.activation(nrm, k6, ACT.Sqrt))
        norm_c = sm[:, 8, :]
        sq = sm[:, 9, :]
        series = sm[:, 10, :]
        small = sm[:, 11, :]

        def horner(c):
            return lambda: V.tensor_tensor(series, series, sq, ALU.mult), \
                lambda: V.tensor_scalar(series, series, c, None, ALU.add)

        vector_block(
            lambda: V.tensor_scalar(norm_c, nrm, EPS_BALL, 1.0 - EPS_BALL, ALU.max, ALU.min),
            lambda: V.tensor_tensor(sq, norm_c, norm_c, ALU.mult),
            lambda: V.tensor_scalar(series, sq, 1.0 / 15, 1.0 / 13, ALU.mult, ALU.add),
            *horner(1.0 / 11), *horner(1.0 / 9), *horner(1.0 / 7), *horner(1.0 / 5), *horner(1.0 / 3), *horner(1.0),
            lambda: V.tensor_tensor(series, series, norm_c, ALU.mult),
            lambda: V.tensor_scalar(small, norm_c, 0.25, None, ALU.is_lt),
            lambda: V.tensor_scalar(k1, norm_c, -1.0, 1.0, ALU.mult, ALU.add),
            lambda: V.reciprocal(k1, k1),
            lambda: V.tensor_scalar(k2, norm_c, 1.0, None, ALU.add),
            lambda: V.tensor_tensor(k1, k1, k2, ALU.mult))
        with nc.Block() as block:
            @block.scalar
            def _(act):
                scalar_did.did(A.activation(k1, k1, ACT.Ln))
        vector_block(
            lambda: V.tensor_scalar(k1, k1, 0.5, None, ALU.mult),
            lambda: V.tensor_tensor(series, series, k1, ALU.subtract),
            lambda: V.tensor_tensor(series, series, small, ALU.mult),
            lambda: V.tensor_tensor(k1, k1, series, ALU.add),
            lambda: V.tensor_tensor(k1, k1, k4, ALU.mult))
        with nc.Block() as block:
            @block.scalar
            def _(act):
                scalar_did.did(A.activation(k1, k1, ACT.Tanh))
        vector_block(
            lambda: V.reciprocal(norm_c, norm_c),
            lambda: V.tensor_tensor(ratio, k1, norm_c, ALU.mult),
            lambda: V.tensor_scalar(k1, nrm, EPS_BALL, None, ALU.is_gt),
            lambda: V.tensor_tensor(ratio, ratio, k1, ALU.mult),
            lambda: V.tensor_tensor(k5, k5, ratio, ALU.mult),
            lambda: V.tensor_tensor(k6, k6, ratio, ALU.mult),
            lambda: V.tensor_tensor(k6, k6, ratio, ALU.mult),
            lambda: V.tensor_scalar(k5, k5, 2.0, 1.0, ALU.mult, ALU.add),
            lambda: V.tensor_tensor(k1, y2_all[:, :], k6, ALU.mult),
            lambda: V.tensor_tensor(k1, k1, k5, ALU.add),
            lambda: V.tensor_scalar(k1, k1, EPS_BALL, None, ALU.max),
            lambda: V.reciprocal(k1, k1),
            lambda: V.tensor_tensor(k5, k5, k6, ALU.add),
            lambda: V.tensor_tensor(k5, k5, k1, ALU.mult),
            lambda: V.tensor_scalar(k2, y2_all[:, :], -1.0, 1.0, ALU.mult, ALU.add),
            lambda: V.tensor_tensor(k2, k2, k1, ALU.mult),
            lambda: V.tensor_tensor(k2, k2, ratio, ALU.mult),
            lambda: V.tensor_tensor(ta[:, :, :], h_all[:, :, :], spread(k5, 2, D), ALU.mult),
            lambda: V.tensor_tensor(x_all[:, :, :], x_all[:, :, :], ta[:, :, :], ALU.add),
            lambda: V.tensor_tensor(ta[:, :, :], total_v, spread(k2, 2, D), ALU.mult),
            lambda: V.tensor_tensor(x_all[:, :, :], x_all[:, :, :], ta[:, :, :], ALU.add))

        phase_no = [0]

        def attention(table, width, heads, kind, loads, att_dst=None):
            phase = phase_no[0]
            phase_no[0] += 1
            Ch = D // heads
            extra = 2 if kind == "weighted" else 1
            W = heads * (Ch + extra)
            value0 = 0 if kind == "added" else D
            scale = 1.0 if kind == "added" else float(Ch) ** -0.5
            q_col = 2 * D

            with nc.Block() as block:
                @block.sync
                def _(sp):
                    for dst, src in loads:
                        params_in.did(sp.dma_start(dst, src), 16)
                    params_in.need(sp, params_in.n)
                    n = sp.value_load(counts[0:1, 0:1], min_val=2, max_val=ITEMS // RING - 2)
                    before = sp.snap(n * phase)
                    steps_before = sp.snap(n * (phase * RING * STEPS) + (phase * STEPS + 1))
                    with sp.Fori(0, n) as q:
                        for j in range(RING):
                            item = slots[bass.ds(q * RING + j, 1), :, :].rearrange("o p k -> p (o k)")
                            sp.wait_ge(step_did, steps_before + q * (RING * STEPS) + (j * STEPS + 1))
                            sp.dma_start(sources[:, j, :], item[:, 0:RANKS]).then_inc(sources_loaded[j], 16)
                            sp.wait_ge(ring_free, before * RING + q * RING + (j + 1))
                            sp.dma_start(slot[:, j, RANKS:3 * RANKS], item[:, RANKS:3 * RANKS]).then_inc(slot_loaded[j], 16)

                @block.gpsimd
                def _(pool):
                    n = pool.value_load(counts[0:1, 0:1], min_val=2, max_val=ITEMS // RING - 2)
                    before = pool.snap(n * phase)
                    with pool.Fori(0, n) as q:
                        for j in range(RING):
                            pool.wait_ge(sources_loaded[j], before * 16 + q * 16 + 16)
                            pool.wait_ge(ring_free, before * RING + q * RING + (j + 1))
                            pool.sem_inc(pool_go, 1)
                            for r in range(RANKS):
                                G.indirect_dma_start(
                                    out=rows[:, j, r, 0:table.shape[1]], out_offset=None, in_=table,
                                    in_offset=bass.IndirectOffsetOnAxis(ap=sources[:, j, r:r + 1].bitcast(I32), axis=0)
                                ).then_inc(rows_gathered[j], 16)

                @block.scalar
                def _(act):
                    n = act.value_load(counts[0:1, 0:1], min_val=2, max_val=ITEMS // RING - 2)
                    before = act.snap(n * phase)
                    with act.Fori(0, n) as q:
                        for j in range(RING):
                            act.wait_ge(shifted, before * RING + q * RING + (j + 1))
                            weights = pv[:, j, :, 0:W].rearrange("p r (h c) -> p r h c", h=heads)[:, :, :, Ch]
                            A.activation(weights, dif[:, j, 0:RANKS, 0:heads], ACT.Exp)
                            A.activation(alpha[:, j, 0:heads], dif[:, j, RANKS, 0:heads], ACT.Exp).then_inc(exp_did, 1)

                @block.tensor
                def _(pe):
                    n = pe.value_load(counts[0:1, 0:1], min_val=2, max_val=ITEMS // RING - 2)
                    before = pe.snap(n * phase)
                    with pe.Fori(0, n) as q:
                        for j in range(RING):
                            pe.wait_ge(ring_free, before * RING + q * RING + (RING + j + 1))
                            for r in range(RANKS):
                                mm = nc.tensor.matmul(ps[:, j % 2, 0:W], ident[:, :], pv[:, j, r, 0:W],
                                                      start=(r == 0), stop=(r == RANKS - 1))
                            mm.then_inc(summed, 1)

                @block.vector
                def _(dve):
                    n = dve.value_load(counts[0:1, 0:1], min_val=2, max_val=ITEMS // RING - 2)
                    before = dve.snap(n * phase)
                    steps_before = dve.snap(n * (phase * RING * STEPS) + ((phase + RING) * STEPS + 1))

                    def scale_sums(did, t, j):
                        sums = acc[:, bass.ds(t * (HEADS * (C + 2)), W)].rearrange("p (h c) -> p h c", h=heads)
                        return did.did(V.tensor_tensor(sums, sums, spread(alpha[:, j, 0:heads], 2, Ch + extra), ALU.mult))

                    def add_item(did, t, j, scaled, last=False):
                        sums = acc[:, bass.ds(t * (HEADS * (C + 2)), W)]
                        did.need(dve, scaled)
                        did.did(V.tensor_tensor(sums, sums, ps[:, j % 2, 0:W], ALU.add), by=STEPS - did.n if last else 1)

                    def step(quad, k, t, t_old=None):
                        first = t_old is None
                        did = Count(step_did, dve.snap(steps_before + quad * (RING * STEPS) + k * STEPS))
                        number = dve.snap(before * RING + quad * RING)

                        def op(ins):
                            did.need(dve, did.did(ins))

                        SM, S, NM = s[:, :, 0:heads], s[:, 0:RANKS, 0:heads], new_max[:, 0:heads]
                        state_m = run_max[:, :, :].rearrange("p t h -> p (t h)")[:, bass.ds(t * HEADS, heads)]
                        row = rows[:, k, :, :]
                        dve.wait_ge(step_did, did.base)
                        dve.wait_ge(rows_gathered[k], (before + quad) * (16 * RANKS) + 16 * RANKS)
                        dve.wait_ge(slot_loaded[k], (before + quad) * 16 + 16)
                        if kind == "added":
                            dst_part = att_dst.rearrange("p t h -> p (t h)")[:, bass.ds(t * HEADS, heads)]
                            m_prod = did.did(V.tensor_tensor(S, row[:, :, D:D + heads], spread(dst_part, 1, RANKS), ALU.add))
                        else:
                            query = stage[:, bass.ds(t * width + q_col, D)]
                            m_prod = did.did(V.tensor_tensor(prod[:, :, :], row[:, :, 0:D], spread(query, 1, RANKS), ALU.mult))
                        did.did(V.tensor_tensor(s[:, RANKS, 0:heads], state_m, state_m, ALU.max))
                        mask = spread(slot[:, k, 2 * RANKS:3 * RANKS], 2, heads)
                        if kind == "weighted":
                            qe_t = qe[:, :, :].rearrange("p t h -> p (t h)")[:, bass.ds(t * HEADS, heads)]
                            m_w = did.did(V.tensor_tensor(s_w[:, :, :], spread(slot[:, k, RANKS:2 * RANKS], 2, heads),
                                                          spread(qe_t, 1, RANKS), ALU.mult))
                        did.need(dve, m_prod)
                        if kind == "added":
                            op(V.scalar_tensor_tensor(out=S, in0=S, scalar=0.2, in1=S, op0=ALU.mult, op1=ALU.max))
                        else:
                            did.did(V.tensor_reduce(S, prod[:, :, :].rearrange("p r (h c) -> p r h c", h=heads), X, ALU.add))
                            m_s = did.n
                            if kind == "weighted":
                                did.need(dve, m_w)
                                did.did(V.scalar_tensor_tensor(out=s_w[:, :, :], in0=s_w[:, :, :], scalar=scale, in1=mask,
                                                               op0=ALU.mult, op1=ALU.add))
                                m_s = did.n
                                mask = s_w[:, :, :]
                            did.need(dve, m_s)
                        op(V.scalar_tensor_tensor(out=S, in0=S, scalar=scale, in1=mask, op0=ALU.mult, op1=ALU.add))
                        op(V.tensor_reduce(NM, SM.rearrange("p r h -> p h r"), X, ALU.max))
                        V.tensor_tensor(dif[:, k, :, 0:heads], SM, spread(NM, 1, RANKS + 1), ALU.subtract).then_inc(shifted, 1)
                        did.did(V.tensor_tensor(state_m, NM, NM, ALU.max))
                        if not first:
                            dve.wait_ge(summed, number + k)
                            scaled = scale_sums(did, t_old, (k - 1) % RING)
                        out4 = pv[:, k, :, 0:W].rearrange("p r (h c) -> p r h c", h=heads)
                        dve.wait_ge(exp_did, number + (k + 1))
                        if kind == "weighted":
                            did.did(V.tensor_tensor(out4[:, :, :, Ch + 1], out4[:, :, :, Ch],
                                                    spread(slot[:, k, RANKS:2 * RANKS], 2, heads), ALU.mult))
                        V.tensor_tensor(out4[:, :, :, 0:Ch], row[:, :, value0:value0 + D].rearrange("p r (h c) -> p r h c", h=heads),
                                        spread(out4[:, :, :, Ch], 3, Ch), ALU.mult).then_inc(ring_free, 1)
                        if not first:
                            add_item(did, t_old, (k - 1) % RING, scaled, last=True)
                        else:
                            V.memset(mx[:, 0:1], 0.0).then_inc(step_did, STEPS - did.n)

                    here = tiles(dve, 0)
                    step(0, 0, here[0])
                    for k in range(1, RING):
                        step(0, k, here[k], here[k - 1])
                    with dve.Fori(1, n) as q:
                        t_before = tiles(dve, q - 1)[RING - 1]
                        here = tiles(dve, q)
                        step(q, 0, here[0], t_before)
                        for k in range(1, RING):
                            step(q, k, here[k], here[k - 1])
                    did = Count(step_did, dve.snap(steps_before + n * (RING * STEPS)))
                    t = tiles(dve, n - 1)[RING - 1]
                    dve.wait_ge(step_did, did.base)
                    dve.wait_ge(summed, dve.snap((before + n) * RING))
                    add_item(did, t, RING - 1, scale_sums(did, t, RING - 1))
                    did.need(dve, did.n)
                    V.memset(mx[:, 0:1], 0.0).then_inc(step_did, STEPS - did.n)

        heads_of = lambda t3: t3.rearrange("p t (h c) -> p t h c", h=HEADS)

        def sums_of(heads, extra):
            Ch = D // heads
            view = acc[:, :].rearrange("p (t w) -> p t w", t=T)[:, :, 0:heads * (Ch + extra)]
            return view.rearrange("p t (h c) -> p t h c", h=heads)

        def add_to_x(what):
            vector_block(lambda: V.tensor_tensor(x_all[:, :, :], x_all[:, :, :], what, ALU.add))

        def clear_sums():
            vector_block(lambda: V.memset(acc[:, :], 0.0),
                         lambda: V.memset(run_max[:, :, :], UNSET))

        def node_sum(src):
            with nc.Block() as block:
                @block.tensor
                def _(pe):
                    nc.tensor.matmul(ps[:, 0, 0:D], onesf[:, :], src[:, 0, :], start=True, stop=False)
                    with pe.Fori(1, T - 1) as t:
                        nc.tensor.matmul(ps[:, 0, 0:D], onesf[:, :], flat(src)[:, bass.ds(t * D, D)], start=False, stop=False)
                    tensor_did.did(nc.tensor.matmul(ps[:, 0, 0:D], valid[:, :], src[:, T - 1, :], start=False, stop=True))

        layer_norm(h_all[:, :, :], x_all[:, :, :], relu=True)
        project(flat(h_all[:, :, :]), w["L1"][:, :], None, lambda t: stage[:, bass.ds(t * TW, D)], D)
        att_d = sb("att_d", [P, T, HEADS])
        hw = table_rows[:, :, 0:D]
        a_src = table_rows[:, :, D:TW]
        sums = sums_of(HEADS, 1)
        vector_block(
            lambda: V.tensor_tensor(ta[:, :, :], hw, spread(vec["att_src"][:, :], 1, T), ALU.mult),
            lambda: V.tensor_reduce(a_src, heads_of(ta[:, :, :]), X, ALU.add),
            lambda: V.tensor_tensor(ta[:, :, :], hw, spread(vec["att_dst"][:, :], 1, T), ALU.mult),
            lambda: V.tensor_reduce(att_d[:, :, :], heads_of(ta[:, :, :]), X, ALU.add),
            lambda: V.tensor_tensor(qe[:, :, :], a_src, att_d[:, :, :], ALU.add),
            lambda: V.scalar_tensor_tensor(out=run_max[:, :, :], in0=qe[:, :, :], scalar=0.2, in1=qe[:, :, :],
                                           op0=ALU.mult, op1=ALU.max),
            lambda: V.memset(sums[:, :, :, C], 1.0),
            lambda: V.tensor_copy(sums[:, :, :, 0:C], heads_of(hw)))
        scatter(tables[1], TW)
        attention(tables[1], TW, HEADS, "added", into_L2(0), att_dst=att_d[:, :, :])
        vector_block(
            lambda: V.tensor_scalar(qe[:, :, :], sums[:, :, :, C], 1e-16, None, ALU.add),
            lambda: V.reciprocal(qe[:, :, :], qe[:, :, :]),
            lambda: V.tensor_tensor(heads_of(ta[:, :, :]), sums[:, :, :, 0:C], spread(qe[:, :, :], 3, C), ALU.mult),
            lambda: V.tensor_tensor(ta[:, :, :], ta[:, :, :], spread(vec["L1_bias"][:, :], 1, T), ALU.add),
            lambda: V.tensor_tensor(ta[:, :, :], ta[:, :, :], h_all[:, :, :], ALU.add))
        layer_norm(h_all[:, :, :], ta[:, :, :], gamma=vec["L1_gamma"][:, :], beta=vec["L1_beta"][:, :])
        add_to_x(h_all[:, :, :])

        layer_norm(h_all[:, :, :], x_all[:, :, :], relu=True)
        h_tile = lambda t: flat(h_all[:, :, :])[:, bass.ds(t * D, D)]
        a_tile = lambda t: flat(ta[:, :, :])[:, bass.ds(t * D, D)]
        project(flat(h_all[:, :, :]), w["Win"][:, :], vec["bin"][:, :], h_tile, D)
        vector_block(lambda: V.tensor_scalar(flat(h_all[:, :, :]), flat(h_all[:, :, :]), 0.0, None, ALU.max))
        col = sb("col", [P, 4, D])
        sums = sums_of(HEADS, 2)
        for l in range(L2_LAYERS):
            W2 = 4 * D
            cols2 = stage[:, 0:T * W2].rearrange("p (t d) -> p t d", d=W2)
            skip = cols2[:, :, 3 * D:4 * D]
            We = vec[f"We_{l}"][:, :]
            wb = v_out
            project(flat(h_all[:, :, :]), w_in[:, :], b_in[:, :],
                    lambda t: stage[:, bass.ds(t * W2, W2)], W2, table=tables[2 + l], width=W2)
            clear_sums()
            vector_block(
                lambda: V.tensor_tensor(ta[:, :, :], cols2[:, :, 2 * D:3 * D], spread(We, 1, T), ALU.mult),
                lambda: V.tensor_reduce(qe[:, :, :], heads_of(ta[:, :, :]), X, ALU.add))
            attention(tables[2 + l], W2, HEADS, "weighted",
                      out_of_L2(l) + (into_L2(l + 1) if l + 1 < L2_LAYERS else into_L3(0)))
            gate = sm[:, 0, :]
            gate2 = sm[:, 1, :]
            vector_block(
                lambda: V.tensor_scalar(qe[:, :, :], sums[:, :, :, C], 1e-30, None, ALU.max),
                lambda: V.reciprocal(qe[:, :, :], qe[:, :, :]),
                lambda: V.tensor_copy(tb[:, :, :], spread(We, 1, T)),
                lambda: V.tensor_tensor(heads_of(tb[:, :, :]), heads_of(tb[:, :, :]), spread(sums[:, :, :, C + 1], 3, C), ALU.mult),
                lambda: V.tensor_tensor(heads_of(tb[:, :, :]), heads_of(tb[:, :, :]), sums[:, :, :, 0:C], ALU.add),
                lambda: V.tensor_tensor(heads_of(ta[:, :, :]), heads_of(tb[:, :, :]), spread(qe[:, :, :], 3, C), ALU.mult),
                lambda: V.tensor_tensor(col[:, 0, :], wb[:, 0:D], wb[:, 2 * D:3 * D], ALU.add),
                lambda: V.tensor_tensor(col[:, 1, :], wb[:, D:2 * D], wb[:, 2 * D:3 * D], ALU.subtract),
                lambda: V.tensor_tensor(tb[:, :, :], ta[:, :, :], spread(col[:, 0, :], 1, T), ALU.mult),
                lambda: V.tensor_reduce(gate, tb[:, :, :], X, ALU.add),
                lambda: V.tensor_tensor(tb[:, :, :], skip, spread(col[:, 1, :], 1, T), ALU.mult),
                lambda: V.tensor_reduce(gate2, tb[:, :, :], X, ALU.add),
                lambda: V.tensor_tensor(gate, gate, gate2, ALU.add))
            with nc.Block() as block:
                @block.scalar
                def _(act):
                    scalar_did.did(A.activation(gate, gate, ACT.Exp, scale=-1.0))
            vector_block(
                lambda: V.tensor_scalar(gate, gate, 1.0, None, ALU.add),
                lambda: V.reciprocal(gate, gate),
                lambda: V.tensor_tensor(tb[:, :, :], skip, ta[:, :, :], ALU.subtract),
                lambda: V.tensor_tensor(tb[:, :, :], tb[:, :, :], spread(gate, 2, D), ALU.mult),
                lambda: V.tensor_tensor(tb[:, :, :], tb[:, :, :], ta[:, :, :], ALU.add))
            node_sum(tb[:, :, :])
            vector_block(
                lambda: V.tensor_scalar(col[:, 2, :], ps[:, 0, 0:D], 1.0 / N, None, ALU.mult),
                lambda: V.tensor_tensor(ta[:, :, :], tb[:, :, :], spread(col[:, 2, :], 1, T), ALU.subtract),
                lambda: V.tensor_tensor(tb[:, :, :], ta[:, :, :], ta[:, :, :], ALU.mult))
            node_sum(tb[:, :, :])
            with nc.Block() as block:
                @block.scalar
                def _(act):
                    scalar_did.did(A.activation(col[:, 3, :], ps[:, 0, 0:D], ACT.Sqrt, bias=eps_ln[:, 0:1], scale=1.0 / N))
            vector_block(
                lambda: V.reciprocal(col[:, 3, :], col[:, 3, :]),
                lambda: V.tensor_tensor(col[:, 3, :], col[:, 3, :], v_out[:, 3 * D:4 * D], ALU.mult),
                lambda: V.tensor_tensor(ta[:, :, :], ta[:, :, :], spread(col[:, 3, :], 1, T), ALU.mult),
                lambda: V.tensor_tensor(ta[:, :, :], ta[:, :, :], spread(v_out[:, 4 * D:5 * D], 1, T), ALU.add),
                lambda: V.scalar_tensor_tensor(out=h_all[:, :, :], in0=ta[:, :, :], scalar=0.0, in1=h_all[:, :, :],
                                               op0=ALU.max, op1=ALU.add))
        add_to_x(h_all[:, :, :])

        layer_norm(h_all[:, :, :], x_all[:, :, :], relu=True)
        project(flat(h_all[:, :, :]), w["Wn"][:, :], vec["bn"][:, :], h_tile, D)
        sums = sums_of(1, 1)
        for l in range(L3_LAYERS):
            W3 = 3 * D
            n_table = 2 + L2_LAYERS + l
            project(flat(h_all[:, :, :]), w_in[:, 0:3 * D], b_in[:, 0:3 * D],
                    lambda t: stage[:, bass.ds(t * W3, W3)], W3, table=tables[n_table], width=W3)
            clear_sums()
            attention(tables[n_table], W3, 1, "plain", out_of_L3(l) + (into_L3(l + 1) if l + 1 < L3_LAYERS else []))
            vector_block(
                lambda: V.tensor_scalar(sm[:, 0, :], sums[:, :, 0, D], 1e-30, None, ALU.max),
                lambda: V.reciprocal(sm[:, 0, :], sm[:, 0, :]),
                lambda: V.tensor_tensor(ta[:, :, :], sums[:, :, 0, 0:D], spread(sm[:, 0, :], 2, D), ALU.mult))
            project(flat(ta[:, :, :]), w_out[:, :], v_out[:, 0:D], a_tile, D)
            vector_block(lambda: V.tensor_tensor(ta[:, :, :], ta[:, :, :], h_all[:, :, :], ALU.add))
            layer_norm(h_all[:, :, :], ta[:, :, :], gamma=v_out[:, D:2 * D], beta=v_out[:, 2 * D:3 * D])
        project(flat(h_all[:, :, :]), w["Wout"][:, :], vec["bout"][:, :], a_tile, D)
        add_to_x(ta[:, :, :])

        with nc.Block() as block:
            @block.gpsimd
            def _(pool):
                for t in range(T):
                    rows_here = P if t < T - 1 else LAST
                    out_stored.did(G.indirect_dma_start(
                        out=out, out_offset=bass.IndirectOffsetOnAxis(ap=node_id[0:rows_here, t:t + 1], axis=0),
                        in_=x_all[0:rows_here, t, :], in_offset=None), 16)
                out_stored.need(pool, out_stored.n)


_INS = ["x", "src", "dst", "edge_weight1"] + [f"L1_gnn_{n}" for n in ("W", "att_src", "att_dst", "bias", "gamma", "beta")] + [
    f"L2_gnn_{n}" for n in ("W_in", "b_in", "Wq", "bq", "Wk", "bk", "Wv", "bv", "We", "Wskip", "bskip", "Wbeta",
                            "bn_gamma", "bn_beta")] + [
    f"L3_gnn_{n}" for n in ("Wn", "bn", "WQ", "bQ", "WK", "bK", "WV", "bV", "WO", "bO", "ln_g", "ln_b", "Wout", "bout")]


def kernel(**inputs):
    import numpy as _np
    import concourse.bacc as _bacc
    from concourse import mybir as _mybir
    from concourse.bass_utils import run_bass_kernel_spmd as _run

    nc = _bacc.Bacc("TRN2", target_bir_lowering=False, num_devices=1)
    arrays, args = {}, {}
    for name in _INS:
        arr = _np.ascontiguousarray(inputs[name])
        arrays[f"in_{name}"] = arr
        args[name] = nc.dram_tensor(f"in_{name}", arr.shape, _mybir.dt.from_np(arr.dtype), kind="ExternalInput").ap()
    shape = tuple(inputs["x"].shape)
    out = nc.dram_tensor("out_x", shape, _mybir.dt.float32, kind="ExternalOutput").ap()
    program(nc, args, out)
    r = _run(nc, [arrays], core_ids=[0])
    return r.results[0]["out_x"]
```

```python
from contextlib import ExitStack

import concourse.bass as bass
from concourse import mybir

ALU = mybir.AluOpType
ACT = mybir.ActivationFunctionType
X = mybir.AxisListType.X
F32 = mybir.dt.float32
I32 = mybir.dt.int32
BF16 = mybir.dt.bfloat16
U8 = mybir.dt.uint8

P = 128
D = 128
HEADS = 4
RANKS = 4
RING = 4
RECORDS = 16
GROUP = 5
L1_LAYERS, L2_LAYERS, L3_LAYERS = 1, 2, 4
STEPS = 16
MASKED = 1e30
UNSET = -1e29
EPS_BALL = 1e-7
EPS_LN = 1e-5
SLOT = 16
NULL_KEY = 4095
RANK_VECTOR_TILES = 12
SCAN_VECTOR_TILES = 2
LN_VECTOR_TILES = 15


class Count:

    def __init__(self, sem, base=0):
        self.sem, self.base, self.n = sem, base, 0

    def did(self, instruction, by=1):
        instruction.then_inc(self.sem, by)
        self.n += by
        return self.n

    def need(self, engine, mark):
        if isinstance(self.base, int) and self.base + mark == 0:
            return
        engine.wait_ge(self.sem, self.base + mark)


def spread(ap, axis, n):
    shape = list(ap.shape)
    return ap.unsqueeze(axis).to_broadcast(shape[:axis] + [n] + shape[axis:])


def program(nc, a, out):
    N = a["x"].shape[0]
    E = a["src"].shape[0]
    T = -(-N // P)
    NP = T * P
    LAST = N - (T - 1) * P
    GROUPS = T // GROUP
    EC = 8 * -(-E // (8 * P))
    EROWS = P * EC
    CHUNK = EC // 14
    IC = -(-(E // RANKS + T + E // (RANKS * P) + 3 * RECORDS) // P)
    ITEMS = P * IC
    C = D // HEADS
    EF = E % EC
    EL = E // EC
    assert T % GROUP == 0 and GROUPS % 2 == 1 and EC % 14 == 0 and EL == P - 1 and NP < 4096 and E > RANKS

    with ExitStack() as ctx:
        def sb(name, shape, dt=F32):
            return ctx.enter_context(nc.sbuf_tensor(name, shape, dt))

        def sem(name):
            return ctx.enter_context(nc.semaphore(name))

        edge_rows = nc.dram_tensor("edge_rows", [EROWS, 2 * RANKS], F32).ap()
        key_row = nc.dram_tensor("key_row", [T, P], F32).ap()
        ranked = nc.dram_tensor("ranked", [NP, 4], I32).ap()
        tile_of_item = nc.dram_tensor("tile_of_item", [P, IC], U8).ap()
        group_of_step = nc.dram_tensor("group_of_step", [P, IC], U8).ap()
        step_items = nc.dram_tensor("step_items", [ITEMS, 8], I32).ap()
        slots = nc.dram_tensor("slots", [ITEMS, P, SLOT], F32).ap()
        row_width = [132, 132] + [256] * (L2_LAYERS + L3_LAYERS)
        tables = [nc.dram_tensor(f"table{n}", [NP, w], F32).ap() for n, w in enumerate(row_width)]

        x_all = sb("x_all", [P, T, D])
        h_all = sb("h_all", [P, T, D])
        stage = sb("stage", [P, T * 512])
        acc = sb("acc", [P, T * HEADS * (C + 2)])
        ta = sb("ta", [P, T, D])
        tb = sb("tb", [P, T, D])
        rows = sb("rows", [P, RING, RANKS, 256])
        prod = sb("prod", [P, RANKS, D])
        pv = sb("pv", [P, RING, RANKS, HEADS * (C + 2)])
        slot = sb("slot", [P, RING, SLOT])
        sources = sb("sources", [P, RING, RANKS])
        ident = sb("ident", [P, P])
        onesf = sb("onesf", [P, P])
        tile_row = sb("tile_row", [1, ITEMS], U8)
        counts = sb("counts", [1, 4], I32)
        node_id = sb("node_id", [P, T], I32)
        node_start = sb("node_start", [P, T])
        node_deg = sb("node_deg", [P, T])
        x_id = sb("x_id", [P, T], I32)
        run_max = sb("run_max", [P, T, HEADS])
        qe = sb("qe", [P, T, HEADS])
        s = sb("s", [P, RANKS + 1, HEADS])
        s_w = sb("s_w", [P, RANKS, HEADS])
        step_mark = sb("step_mark", [P, 1])
        new_max = sb("new_max", [P, HEADS])
        dif = sb("dif", [P, RING, RANKS + 1, HEADS])
        alpha = sb("alpha", [P, RING, HEADS])
        htile = sb("htile", [P, 2, GROUP * D])
        hT = sb("hT", [P, 2, GROUP * D])
        sm = sb("sm", [P, 12, T])
        eps_ln = sb("eps_ln", [P, 1])
        ln_stats = sb("ln_stats", [P, T, 6])
        ln_mv = sb("ln_mv", [P, T, 2])
        left = sb("left", [P, T])
        n_blk = sb("n_blk", [1, 4, T])
        n_blk_i = sb("n_blk_i", [1, 2, T], I32)
        maxT = sb("maxT", [T, 1])
        per_tile = sb("per_tile", [P, 4, T])
        step_grid = sb("step_grid", [P, T])
        item_i = sb("item_i", [P, IC], I32)
        item_f = sb("item_f", [P, IC])
        tile_f = sb("tile_f", [P, IC])
        tile_u = sb("tile_u", [P, IC], U8)
        group_u = sb("group_u", [P, IC], U8)
        step_b = sb("step_b", [P, IC])
        step_off = ta[:, :, :].rearrange("p t d -> p (t d)")[:, 0:2 * IC * GROUP].rearrange("p (k n) -> p k n", k=2)
        step_off_i = tb[:, :, :].rearrange("p t d -> p (t d)")[:, 0:IC * 8].bitcast(I32).rearrange("p (i k) -> p i k", k=8)
        big = stage[:, 0:IC * T]
        big2 = stage[:, IC * T:2 * IC * T]
        group_row = acc[:, :].bitcast(U8)[0:1, 0:ITEMS]
        ps = ctx.enter_context(nc.psum_tensor("ps", [P, 8, 512], F32))

        w = {}
        vec = {}
        weight_parts = [("L1", [a["L1_gnn_W"]]), ("Win", [a["L2_gnn_W_in"]]), ("Wn", [a["L3_gnn_Wn"]]),
                        ("Wout", [a["L3_gnn_Wout"]])]
        vector_parts = [("att_src", [a["L1_gnn_att_src"].rearrange("h c -> (h c)")]),
                        ("att_dst", [a["L1_gnn_att_dst"].rearrange("h c -> (h c)")]),
                        ("L1_bias", [a["L1_gnn_bias"]]), ("L1_gamma", [a["L1_gnn_gamma"]]),
                        ("L1_beta", [a["L1_gnn_beta"]]), ("bin", [a["L2_gnn_b_in"]]),
                        ("bn", [a["L3_gnn_bn"]]), ("bout", [a["L3_gnn_bout"]])]
        for l in range(L2_LAYERS):
            vector_parts.append((f"We_{l}", [a["L2_gnn_We"][l, 0]]))
        for name, parts in weight_parts:
            w[name] = sb("w_" + name, [P, sum(p.shape[1] for p in parts)])
        for name, parts in vector_parts:
            vec[name] = sb("v_" + name, [P, sum(p.shape[0] for p in parts)])
        w_in = sb("w_in", [P, 4 * D])
        b_in = sb("b_in", [P, 4 * D])
        w_out = sb("w_out", [P, D])
        v_out = sb("v_out", [P, 3 * D])
        v_gate = sb("v_gate", [P, L2_LAYERS, 5 * D])

        def into_layer(weights, biases):
            return [(w_in[:, k * D:(k + 1) * D], p) for k, p in enumerate(weights)] + [
                (b_in[:, k * D:(k + 1) * D], p.partition_broadcast(P)) for k, p in enumerate(biases)]

        def into_L2(l):
            return into_layer([a[f"L2_gnn_W{k}"][l] for k in ("k", "v", "q", "skip")],
                              [a[f"L2_gnn_b{k}"][l] for k in ("k", "v", "q", "skip")])

        def into_L3(l):
            return into_layer([a[f"L3_gnn_W{k}"][l] for k in ("K", "V", "Q")],
                              [a[f"L3_gnn_b{k}"][l] for k in ("K", "V", "Q")])

        def out_of_L2(l):
            return [(v_gate[:, l, 0:3 * D], a["L2_gnn_Wbeta"][l].rearrange("k o -> (k o)").partition_broadcast(P)),
                    (v_gate[:, l, 3 * D:4 * D], a["L2_gnn_bn_gamma"][l].partition_broadcast(P)),
                    (v_gate[:, l, 4 * D:5 * D], a["L2_gnn_bn_beta"][l].partition_broadcast(P))]

        def out_of_L3(l):
            return [(w_out[:, :], a["L3_gnn_WO"][l])] + [
                (v_out[:, k * D:(k + 1) * D], a[f"L3_gnn_{n}"][l].partition_broadcast(P))
                for k, n in enumerate(("bO", "ln_g", "ln_b"))]

        params_in = Count(sem("params_in"))
        loaded = Count(sem("loaded"))
        x_gathered = Count(sem("x_gathered"))
        out_stored = Count(sem("out_stored"))
        stored = Count(sem("stored"))
        scattered = Count(sem("scattered"))
        vector_did = Count(sem("vector_did"))
        scalar_did = Count(sem("scalar_did"))
        tensor_did = Count(sem("tensor_did"))
        pool_did = Count(sem("pool_did"))
        hots_ready, hots_used = sem("hots_ready"), sem("hots_used")
        transposed, turned, staged_tile = sem("transposed"), sem("turned"), sem("staged_tile")
        projected, evacuated, group_added = sem("projected"), sem("evacuated"), sem("group_added")
        stats_did = sem("stats_did")

        record_stored = [sem(f"record_stored{j}") for j in range(RECORDS)]
        record_gathered = [sem(f"record_gathered{j}") for j in range(RECORDS)]
        scan_slots_in = [sem(f"scan_slots_in{j}") for j in range(2)]
        scan_gathered = [[sem(f"scan_gathered{j}_{r}") for r in range(RANKS)] for j in range(2)]
        h_copied = sem("h_copied")
        factor_ready, rows_scaled = sem("factor_ready"), sem("rows_scaled")
        scan_did, scan_free, scan_slots_free = sem("scan_did"), sem("scan_free"), sem("scan_slots_free")
        record_did = sem("record_did")
        sources_loaded = [sem(f"sources_loaded{j}") for j in range(RING)]
        slot_loaded = [sem(f"slot_loaded{j}") for j in range(RING)]
        rows_gathered_in = [[sem(f"rows_gathered{n}_{j}") for j in range(RING)] for n in range(1 + L2_LAYERS + L3_LAYERS)]
        pool_go, sync_go, vector_go, scalar_go = sem("pool_go"), sem("sync_go"), sem("vector_go"), sem("scalar_go")
        step_did = sem("step_did")
        shifted, exp_did, summed, ring_free = sem("shifted"), sem("exp_did"), sem("summed"), sem("ring_free")

        V, A, G, Q = nc.vector, nc.scalar, nc.gpsimd, nc.sync

        def vec_op(ins):
            vector_did.need(V, vector_did.did(ins))

        def act_op(ins):
            scalar_did.need(A, scalar_did.did(ins))

        def tiles(engine, quad):
            word = engine.value_load(tile_row.bitcast(I32)[0:1, bass.ds(quad, 1)], min_val=0, max_val=0x7FFFFFFF)
            return [engine.snap((word >> (8 * j)) & 31).with_bounds(min_val=0, max_val=T - 1) for j in range(4)]

        flat = lambda t3: t3.rearrange("p t d -> p (t d)")

        iota_i = sb("iota_i", [P, P], I32)
        iota_f = sb("iota_f", [P, P])
        part_i = sb("part_i", [P, 1], I32)
        part_f = sb("part_f", [P, 1])
        below = sb("below", [P, P])
        valid = sb("valid", [P, P])
        iota_b = sb("iota_b", [P, P], BF16)
        rank_f = iota_f[:, 0:RANKS]

        at = [0]

        def scratch(n, dt=F32):
            size = n if dt in (F32, I32) else -(-n // 2)
            v = stage[:, at[0]:at[0] + size]
            at[0] += size + size % 2
            return v if dt == F32 else v.bitcast(dt)

        src_e, w_e, dst_e = scratch(EC + RANKS, I32), scratch(EC + RANKS), scratch(EC, I32)
        lo_i, hi_i = scratch(EC, I32), scratch(EC, I32)
        lo_b, hi_b = scratch(EC, BF16), scratch(EC, BF16)
        ebs = scratch(EC * 2 * RANKS).rearrange("p (e k) -> p e k", k=2 * RANKS)
        lo_hot = [scratch(CHUNK * P, BF16).rearrange("p (c n) -> p c n", n=P) for _ in range(2)]
        hi_hot = [scratch(CHUNK * T, BF16).rearrange("p (c n) -> p c n", n=T) for _ in range(2)]
        zero_b = scratch(P, BF16)

        with nc.Block() as block:
            @block.sync
            def _(sp):
                pool_did.need(sp, 3)
                for dst, arr in ((src_e, a["src"]), (w_e, a["edge_weight1"].rearrange("e o -> (e o)"))):
                    body = bass.AP(arr.tensor, arr.offset, [[EC, P - 1], [1, EC + RANKS]])
                    loaded.did(sp.dma_start(dst[0:P - 1, :], body), 16)
                    loaded.did(sp.dma_start(dst[P - 1:P, 0:EF], arr[EL * EC:E].rearrange("(o e) -> o e", o=1)), 16)
                arr = a["dst"]
                loaded.did(sp.dma_start(dst_e[0:P - 1, :], arr[0:EL * EC].rearrange("(p e) -> p e", e=EC)), 16)
                loaded.did(sp.dma_start(dst_e[P - 1:P, 0:EF], arr[EL * EC:E].rearrange("(o e) -> o e", o=1)), 16)
                for name, parts in weight_parts:
                    c = 0
                    for p in parts:
                        params_in.did(sp.dma_start(w[name][:, c:c + p.shape[1]], p), 16)
                        c += p.shape[1]
                for name, parts in vector_parts:
                    c = 0
                    for p in parts:
                        params_in.did(sp.dma_start(vec[name][:, c:c + p.shape[0]], p.partition_broadcast(P)), 16)
                        c += p.shape[0]
                loaded.need(sp, loaded.n)

            @block.gpsimd
            def _(pool):
                pool_did.did(G.memset(src_e, 0))
                pool_did.did(G.memset(w_e, 0.0))
                pool_did.did(G.memset(dst_e, NULL_KEY))
                pool_did.did(G.iota(iota_i[:, :], [[1, P]], 0, 0))
                pool_did.did(G.iota(part_i[:, :], [[0, 1]], 0, 1))
                pool_did.did(G.memset(onesf[:, :], 1.0))

            @block.vector
            def _(dve):
                pool_did.need(dve, 6)
                vec_op(V.tensor_copy(iota_f[:, :], iota_i[:, :]))
                vec_op(V.tensor_copy(iota_b[:, :], iota_i[:, :]))
                vec_op(V.tensor_copy(part_f[:, :], part_i[:, :]))
                vec_op(V.tensor_scalar(ident[:, :], iota_f[:, :], part_f[:, 0:1], None, ALU.is_equal))
                vec_op(V.tensor_scalar(below[:, :], iota_f[:, :], part_f[:, 0:1], None, ALU.is_gt))
                vec_op(V.tensor_scalar(part_f[:, 0:1], part_f[:, 0:1], float(LAST), None, ALU.is_lt))
                vec_op(V.tensor_scalar(valid[:, :], onesf[:, :], part_f[:, 0:1], None, ALU.mult))
                vec_op(V.memset(eps_ln[:, :], EPS_LN))
                vec_op(V.memset(zero_b, 0.0))

        hist = ps[:, 0, 0:T]
        cnt = sm[:, 0, :]
        start = sm[:, 1, :]
        with nc.Block() as block:
            @block.vector
            def _(dve):
                vec_op(V.tensor_scalar(lo_i, dst_e, P - 1, None, ALU.bitwise_and))
                vec_op(V.tensor_scalar(hi_i, dst_e, 7, None, ALU.logical_shift_right))
                vec_op(V.tensor_copy(lo_b, lo_i))
                vec_op(V.tensor_copy(hi_b, hi_i))
                with dve.Fori(0, EC // CHUNK // 2) as q:
                    for b in range(2):
                        dve.wait_ge(hots_used, 2 * q + b + 1)
                        cols = bass.ds(q * (2 * CHUNK) + b * CHUNK, CHUNK)
                        V.tensor_tensor(lo_hot[b], spread(lo_b[:, cols], 2, P), spread(iota_b[:, :], 1, CHUNK),
                                        ALU.is_equal).then_inc(hots_ready, 1)
                        V.tensor_tensor(hi_hot[b], spread(hi_b[:, cols], 2, T), spread(iota_b[:, 0:T], 1, CHUNK),
                                        ALU.is_equal).then_inc(hots_ready, 1)

            @block.tensor
            def _(pe):
                nc.tensor.matmul(hist, zero_b, zero_b[:, 0:T], start=True, stop=False,
                                 skip_group_check=True).then_inc(hots_used, 2)
                with pe.Fori(0, EC // CHUNK // 2) as q:
                    for b in range(2):
                        pe.wait_ge(hots_ready, 4 * q + 2 * b + 2)
                        for c in range(CHUNK):
                            mm = nc.tensor.matmul(hist, lo_hot[b][:, c, :], hi_hot[b][:, c, :],
                                                  start=False, stop=False, skip_group_check=True)
                        mm.then_inc(hots_used, 1)
                tensor_did.did(nc.tensor.matmul(hist, zero_b, zero_b[:, 0:T], start=False, stop=True,
                                                skip_group_check=True))

            @block.gpsimd
            def _(pool):
                for k in range(RANKS):
                    pool_did.did(G.tensor_copy(ebs.bitcast(I32)[:, :, k], src_e[:, k:k + EC]))
                    pool_did.did(G.tensor_copy(ebs[:, :, RANKS + k], w_e[:, k:k + EC]))

            @block.sync
            def _(sp):
                pool_did.need(sp, pool_did.n)
                stored.did(sp.dma_start(edge_rows.rearrange("(p e) k -> p (e k)", p=P),
                                        ebs.rearrange("p e k -> p (e k)")), 16)
                stored.need(sp, stored.n)

        key = sm[:, 2, :]
        pos = sm[:, 3, :]
        n_rev = sm[:, 4, :]
        pos_i = sb("pos_i", [P, T], I32)
        n_i = sb("n_i", [P, T], I32)
        rec = sb("rec", [P, T, 4], I32)
        keyT = sb("keyT", [T, P])
        with nc.Block() as block:
            @block.gpsimd
            def _(pool):
                pool_did.did(G.iota(n_i[:, :], [[P, T]], 0, 1))

            @block.vector
            def _(dve):
                vec_op(V.tensor_copy(cnt, hist))
                pool_did.need(dve, pool_did.n)
                vec_op(V.tensor_copy(n_rev, n_i[:, :]))
                vec_op(V.tensor_scalar(n_rev, n_rev, -1.0, 4095.0, ALU.mult, ALU.add))
                vec_op(V.tensor_scalar(key, cnt, 4095.0, 4096.0, ALU.min, ALU.mult))
                vec_op(V.tensor_tensor(key, key, n_rev, ALU.add))

            @block.tensor
            def _(pe):
                vector_did.need(pe, vector_did.n)
                nc.tensor.matmul(ps[:, 1, 0:T], below[:, :], cnt, start=True, stop=True)
                nc.tensor.matmul(ps[:, 2, 0:T], onesf[:, :], cnt, start=True, stop=True)
                tensor_did.did(nc.tensor.transpose(ps[0:T, 3, 0:P], key, ident[:, :]))

            @block.scalar
            def _(act):
                tensor_did.need(act, tensor_did.n)
                scalar_did.did(A.copy(keyT[:, :], ps[0:T, 3, 0:P]))

            @block.sync
            def _(sp):
                scalar_did.need(sp, scalar_did.n)
                stored.did(sp.dma_start(key_row, keyT[:, :]), 16)
                stored.need(sp, stored.n)
                loaded.did(sp.dma_start(flat(ta[:, :, :]), key_row.rearrange("t p -> (t p)").partition_broadcast(P)), 16)
                loaded.need(sp, loaded.n)

        keys_ready = vector_did.n + 9
        with nc.Block() as block:
            @block.vector
            def _(dve):
                vec_op(V.tensor_copy(sm[:, 5, :], ps[:, 2, 0:T]))
                vec_op(V.tensor_tensor_scan(sm[:, 6, :], onesf[:, 0:T], sm[:, 5, :], 0.0, ALU.mult, ALU.add))
                vec_op(V.tensor_tensor(start, sm[:, 6, :], sm[:, 5, :], ALU.subtract))
                vec_op(V.tensor_tensor(start, start, ps[:, 1, 0:T], ALU.add))
                vec_op(V.tensor_copy(rec[:, :, 0], n_i[:, :]))
                vec_op(V.tensor_copy(rec[:, :, 1], start))
                vec_op(V.tensor_copy(rec[:, :, 2], cnt))
                vec_op(V.memset(rec[:, :, 3], 0))
                vec_op(V.tensor_scalar(sm[:, 5, :], key, -1.0, None, ALU.mult))
                for t in range(RANK_VECTOR_TILES):
                    vec_op(V.tensor_scalar(flat(tb[:, :, :]), flat(ta[:, :, :]), key[:, t:t + 1], 0.0,
                                           ALU.is_gt, ALU.add, accum_out=pos[:, t:t + 1]))
                    vec_op(V.tensor_copy(pos_i[:, t:t + 1], pos[:, t:t + 1]))
                scalar_did.need(dve, scalar_did.n + T - RANK_VECTOR_TILES)
                rest = slice(RANK_VECTOR_TILES, T)
                vec_op(V.tensor_scalar(pos[:, rest], pos[:, rest], float(NP - 1), 0.5, ALU.add, ALU.mult))
                vec_op(V.tensor_copy(pos_i[:, rest], pos[:, rest]))

            @block.scalar
            def _(act):
                vector_did.need(act, keys_ready)
                for t in range(RANK_VECTOR_TILES, T):
                    act_op(A.activation(flat(h_all[:, :, :]), flat(ta[:, :, :]), ACT.Sign, bias=sm[:, 5, t:t + 1],
                                        accum_out=pos[:, t:t + 1]))

            @block.gpsimd
            def _(pool):
                for t in range(T):
                    vector_did.need(pool, min(keys_ready + 2 * t + 2, vector_did.n))
                    scattered.did(G.indirect_dma_start(
                        out=ranked, out_offset=bass.IndirectOffsetOnAxis(ap=pos_i[:, t:t + 1], axis=0),
                        in_=rec[:, t, :], in_offset=None), 16)

            @block.sync
            def _(sp):
                scattered.need(sp, scattered.n)
                loaded.did(sp.dma_start(rec[:, :, :], ranked.rearrange("(t p) c -> p t c", p=P)), 16)
                loaded.need(sp, loaded.n)

        def vector_block(*steps):
            with nc.Block() as block:
                @block.vector
                def _(dve):
                    for step in steps:
                        vec_op(step())

        def load_and_wait(*copies):
            with nc.Block() as block:
                @block.sync
                def _(sp):
                    for dst, src in copies:
                        loaded.did(sp.dma_start(dst, src), 16)
                    loaded.need(sp, loaded.n)

        vector_block(
            lambda: V.tensor_scalar(x_id[:, :], rec[:, :, 0], float(N - 1), None, ALU.min),
            lambda: V.tensor_copy(node_id[:, :], rec[:, :, 0]),
            lambda: V.tensor_copy(node_start[:, :], rec[:, :, 1]),
            lambda: V.tensor_copy(node_deg[:, :], rec[:, :, 2]),
            lambda: V.tensor_copy(left[:, :], rec[:, :, 2]))

        with nc.Block() as block:
            @block.tensor
            def _(pe):
                tensor_did.did(nc.tensor.transpose(ps[0:T, 0, 0:P], node_deg[:, :], ident[:, :]))

            @block.vector
            def _(dve):
                tensor_did.need(dve, tensor_did.n)
                vec_op(V.tensor_reduce(maxT[:, :], ps[0:T, 0, 0:P], X, ALU.max))

        with nc.Block() as block:
            @block.tensor
            def _(pe):
                tensor_did.did(nc.tensor.transpose(ps[0:1, 1, 0:T], maxT[:, :], ident[0:T, 0:T]))

            @block.vector
            def _(dve):
                tensor_did.need(dve, tensor_did.n)
                row = lambda k: n_blk[:, k, :]
                vec_op(V.tensor_scalar(row(0), ps[0:1, 1, 0:T], float(RANKS - 1), None, ALU.add))
                vec_op(V.tensor_copy(n_blk_i[:, 0, :], row(0)))
                vec_op(V.tensor_scalar(n_blk_i[:, 1, :], n_blk_i[:, 0, :], 2, None, ALU.arith_shift_right))
                vec_op(V.tensor_copy(row(0), n_blk_i[:, 1, :]))
                vec_op(V.tensor_tensor_scan(row(2), onesf[0:1, 0:T], row(0), 0.0, ALU.mult, ALU.add))
                vec_op(V.tensor_tensor(row(1), row(2), row(0), ALU.subtract))
                vec_op(V.memset(row(3), 0.0))
                vec_op(V.tensor_reduce(n_blk[:, 3, 0:GROUPS], row(0).rearrange("p (g k) -> p g k", k=GROUP), X, ALU.max))
                vec_op(V.tensor_tensor_scan(n_blk[:, 3, GROUPS:2 * GROUPS], onesf[0:1, 0:GROUPS],
                                            n_blk[:, 3, 0:GROUPS], 0.0, ALU.mult, ALU.add))
                vec_op(V.tensor_copy(n_blk_i[:, 0, 0:1], n_blk[:, 2, T - 1:T]))
                vec_op(V.tensor_scalar(n_blk_i[:, 0, 1:2], n_blk[:, 2, T - 1:T], float(RING - 1), None, ALU.add))
                vec_op(V.tensor_scalar(n_blk_i[:, 0, 2:3], n_blk[:, 3, 2 * GROUPS - 1:2 * GROUPS], 1.0, None, ALU.add))
                vec_op(V.tensor_scalar(counts[:, 0:1], n_blk_i[:, 0, 1:2], 2, None, ALU.arith_shift_right))
                vec_op(V.tensor_scalar(counts[:, 1:2], n_blk_i[:, 0, 0:1], RECORDS.bit_length() - 1, None,
                                       ALU.arith_shift_right))
                vec_op(V.tensor_scalar(counts[:, 0:1], counts[:, 0:1], 2.0, None, ALU.max))
                vec_op(V.tensor_scalar(counts[:, 1:2], counts[:, 1:2], 1.0, None, ALU.add))
                vec_op(V.tensor_scalar(counts[:, 2:3], n_blk_i[:, 0, 2:3], 1, None, ALU.arith_shift_right))
                vec_op(V.tensor_scalar(counts[:, 2:3], counts[:, 2:3], 2.0, None, ALU.max))
                vec_op(V.tensor_scalar(counts[:, 3:4], counts[:, 2:3], -1.0, None, ALU.add))

            @block.gpsimd
            def _(pool):
                pool_did.did(G.iota(item_i[:, :], [[1, IC]], 0, IC))

        with nc.Block() as block:
            @block.tensor
            def _(pe):
                tensor_did.did(nc.tensor.matmul(ps[:, 2, 0:4 * T], onesf[0:1, :], n_blk[:, :, :].rearrange("p k t -> p (k t)"),
                                                start=True, stop=True))

            @block.vector
            def _(dve):
                tensor_did.need(dve, tensor_did.n)
                vec_op(V.tensor_copy(per_tile[:, :, :].rearrange("p k t -> p (k t)"), ps[:, 2, 0:4 * T]))
                vec_op(V.tensor_copy(item_f[:, :], item_i[:, :]))
                blocks, before, upto = per_tile[:, 0, :], per_tile[:, 1, :], per_tile[:, 2, :]
                g_blocks, g_upto = per_tile[:, 3, 0:GROUPS], per_tile[:, 3, GROUPS:2 * GROUPS]
                all_items = per_tile[:, 2, T - 1:T]
                by_tile = big.rearrange("p (i t) -> p i t", t=T)
                by_group = big2[:, 0:IC * GROUPS].rearrange("p (i g) -> p i g", g=GROUPS)
                by_both = big.rearrange("p (i k g) -> p i k g", k=GROUP, g=GROUPS)
                vec_op(V.tensor_tensor(by_tile, spread(item_f[:, :], 2, T), spread(upto, 1, IC), ALU.is_ge))
                vec_op(V.tensor_reduce(tile_f[:, :], by_tile, X, ALU.add))
                vec_op(V.tensor_scalar(tile_f[:, :], tile_f[:, :], float(T - 1), None, ALU.min))
                vec_op(V.tensor_copy(tile_u[:, :], tile_f[:, :]))
                vec_op(V.tensor_tensor(by_group, spread(item_f[:, :], 2, GROUPS), spread(g_upto, 1, IC), ALU.is_ge))
                vec_op(V.tensor_reduce(tile_f[:, :], by_group, X, ALU.add))
                vec_op(V.tensor_scalar(tile_f[:, :], tile_f[:, :], float(GROUPS - 1), None, ALU.min))
                vec_op(V.tensor_copy(group_u[:, :], tile_f[:, :]))
                vec_op(V.tensor_tensor(by_group, by_group, spread(g_blocks, 1, IC), ALU.mult))
                vec_op(V.tensor_reduce(step_b[:, :], by_group[:, :, 0:GROUPS - 1], X, ALU.add))
                vec_op(V.tensor_tensor(step_b[:, :], item_f[:, :], step_b[:, :], ALU.subtract))
                vec_op(V.tensor_tensor(by_group, spread(tile_f[:, :], 2, GROUPS), spread(iota_f[:, 0:GROUPS], 1, IC), ALU.is_equal))
                for k, what in ((0, blocks), (1, before)):
                    grid = what.rearrange("p (g k) -> p k g", k=GROUP)
                    vec_op(V.tensor_copy(step_grid[:, :], grid))
                    vec_op(V.tensor_tensor(by_both, spread(by_group, 2, GROUP),
                                           spread(step_grid[:, :].rearrange("p (k g) -> p k g", g=GROUPS), 1, IC), ALU.mult))
                    vec_op(V.tensor_reduce(step_off[:, k, :], by_both, X, ALU.add))
                off = lambda k: step_off[:, k, :].rearrange("p (i k) -> p i k", k=GROUP)
                vec_op(V.tensor_tensor(off(0), off(0), spread(step_b[:, :], 2, GROUP), ALU.is_gt))
                vec_op(V.tensor_tensor(off(1), off(1), spread(step_b[:, :], 2, GROUP), ALU.add))
                vec_op(V.tensor_scalar(off(1), off(1), all_items, None, ALU.subtract))
                vec_op(V.tensor_tensor(off(1), off(1), off(0), ALU.mult))
                vec_op(V.tensor_scalar(off(1), off(1), all_items, None, ALU.add))
                vec_op(V.memset(step_off_i[:, :, :], 0))
                vec_op(V.tensor_copy(step_off_i[:, :, 0:GROUP], off(1)))

            @block.gpsimd
            def _(pool):
                for t in range(T):
                    x_gathered.did(G.indirect_dma_start(
                        out=x_all[:, t, :], out_offset=None, in_=a["x"],
                        in_offset=bass.IndirectOffsetOnAxis(ap=x_id[:, t:t + 1], axis=0)), 16)
                x_gathered.need(pool, x_gathered.n)

            @block.sync
            def _(sp):
                vector_did.need(sp, vector_did.n)
                stored.did(sp.dma_start(tile_of_item, tile_u[:, :]), 16)
                stored.did(sp.dma_start(group_of_step, group_u[:, :]), 16)
                stored.did(sp.dma_start(step_items.rearrange("(p i) k -> p (i k)", p=P),
                                        step_off_i[:, :, :].rearrange("p i k -> p (i k)")), 16)
                stored.need(sp, stored.n)
                loaded.did(sp.dma_start(tile_row[:, :], tile_of_item.rearrange("(o p) i -> o (p i)", o=1)), 16)
                loaded.did(sp.dma_start(group_row, group_of_step.rearrange("(o p) i -> o (p i)", o=1)), 16)
                loaded.need(sp, loaded.n)

        def layer_norm(dst, src, relu=False, gamma=None, beta=None, stats_at=None, factors_only=False):
            stats, mean_var, rstd, shift = ln_stats[:, :, :], ln_mv[:, :, :], sm[:, 0, :], sm[:, 1, :]
            with nc.Block() as block:
                @block.vector
                def _(dve):
                    if stats_at is None:
                        for t in range(T):
                            mark = vector_did.did(V.bn_stats(stats[:, t, :], src[:, t, :]))
                        vector_did.need(dve, mark)
                    else:
                        dve.wait_ge(stats_did, stats_at)
                    for t in range(T):
                        mark = vector_did.did(V.bn_aggr(mean_var[:, t, :], stats[:, t, :]))
                    scalar_did.need(dve, scalar_did.n + 1)
                    vec_op(V.reciprocal(rstd, rstd))
                    vec_op(V.scalar_tensor_tensor(out=shift, in0=mean_var[:, :, 0], scalar=-1.0, in1=rstd,
                                                  op0=ALU.mult, op1=ALU.mult))
                    if factors_only:
                        return
                    for t in range(LN_VECTOR_TILES):
                        did = vector_did.did(V.tensor_scalar(dst[:, t, :], src[:, t, :], rstd[:, t:t + 1], shift[:, t:t + 1],
                                                             ALU.mult, ALU.add))
                    part = dst[:, 0:LN_VECTOR_TILES, :]
                    vector_did.need(dve, did)
                    if relu:
                        vec_op(V.tensor_scalar(part, part, 0.0, None, ALU.max))
                    if gamma is not None:
                        vec_op(V.tensor_tensor(part, part, spread(gamma, 1, LN_VECTOR_TILES), ALU.mult))
                        vec_op(V.tensor_tensor(part, part, spread(beta, 1, LN_VECTOR_TILES), ALU.add))
                        part = dst[:, LN_VECTOR_TILES:T, :]
                        scalar_did.need(dve, scalar_did.n + 1 + T - LN_VECTOR_TILES)
                        vec_op(V.tensor_tensor(part, part, spread(gamma, 1, T - LN_VECTOR_TILES), ALU.mult))
                        vec_op(V.tensor_tensor(part, part, spread(beta, 1, T - LN_VECTOR_TILES), ALU.add))

                after_shift = vector_did.n
                if not factors_only:
                    after_shift -= (4 if gamma is not None else 1 if relu else 0) + LN_VECTOR_TILES

                @block.scalar
                def _(act):
                    vector_did.need(act, after_shift - 2)
                    scalar_did.did(A.activation(rstd, mean_var[:, :, 1], ACT.Sqrt, bias=eps_ln[:, 0:1]))
                    if factors_only:
                        return
                    vector_did.need(act, after_shift)
                    for t in range(LN_VECTOR_TILES, T):
                        scalar_did.did(A.activation(dst[:, t, :], src[:, t, :], ACT.Relu if relu else ACT.Identity,
                                                    bias=shift[:, t:t + 1], scale=rstd[:, t:t + 1]))

        layer_norm(None, x_all[:, :, :], factors_only=True)
        TW = row_width[0]
        table_rows = stage[:, 0:T * TW].rearrange("p (t d) -> p t d", d=TW)
        y2_all = sb("y2_all", [P, T])

        index_of = sb("index_of", [P, RECORDS], I32)
        record = sb("record", [P, RECORDS, SLOT])
        with nc.Block() as block:
            @block.vector
            def _(dve):
                for first, credit in ((record_did, 1), (scan_did, 1), (step_did, RING * STEPS + 1), (ring_free, RING),
                                      (scan_free, 2 * RANKS), (scan_slots_free, 2)):
                    V.sem_inc(first, credit)

            @block.tensor
            def _(pe):
                nc.tensor.sem_inc(evacuated, GROUP)
                nc.tensor.sem_inc(projected, GROUP + 1)

            @block.scalar
            def _(act):
                A.sem_inc(turned, 1)

            @block.sync
            def _(sp):
                for j in range(RECORDS):
                    sp.sem_inc(record_stored[j], 16)

        with nc.Block() as block:
            @block.scalar
            def _(act):
                for t in range(T):
                    scalar_did.did(A.activation(h_all[:, t, :], x_all[:, t, :], ACT.Relu, bias=sm[:, 1, t:t + 1],
                                                scale=sm[:, 0, t:t + 1]))
                for t in range(T):
                    if t == 0:
                        scalar_did.need(act, scalar_did.n)
                    scalar_did.did(A.activation(ta[:, t, :], h_all[:, t, :], ACT.Square, accum_out=y2_all[:, t:t + 1]))
                scalar_did.need(act, scalar_did.n)
                act_op(A.copy(table_rows[:, :, D], y2_all[:, :]))
                act_op(A.copy(table_rows[:, :, 0:D], h_all[:, :, :]))

            @block.vector
            def _(dve):
                vec_op(V.memset(table_rows[:, :, D + 1:TW], 0.0))
                n = dve.value_load(counts[0:1, 1:2], min_val=1, max_val=ITEMS // RECORDS - 2)
                with dve.Fori(0, n) as q:
                    tile_of = []
                    for k in range(RECORDS // 4):
                        tile_of += tiles(dve, q * (RECORDS // 4) + k)
                    for j in range(RECORDS):
                        did = Count(record_did, q * (5 * RECORDS) + (5 * j + 1))
                        t = tile_of[j]
                        dve.wait_ge(record_stored[j], q * 16 + 16)
                        dve.wait_ge(record_did, q * (5 * RECORDS) + (5 * j + 1))
                        node = node_start[:, bass.ds(t, 1)]
                        rest = left[:, bass.ds(t, 1)]
                        did.did(V.tensor_scalar(index_of[:, j:j + 1], node, float(E), None, ALU.min))
                        did.did(V.tensor_scalar(record[:, j, 3 * RANKS:4 * RANKS], rank_f, rest, None, ALU.is_lt))
                        did.did(V.tensor_scalar(node, node, float(RANKS), None, ALU.add))
                        did.did(V.tensor_scalar(rest, rest, -float(RANKS), None, ALU.add))
                        did.need(dve, 2)
                        did.did(V.tensor_scalar(record[:, j, 2 * RANKS:3 * RANKS], record[:, j, 3 * RANKS:4 * RANKS],
                                                MASKED, -MASKED, ALU.mult, ALU.add))

            @block.gpsimd
            def _(pool):
                n = pool.value_load(counts[0:1, 1:2], min_val=1, max_val=ITEMS // RECORDS - 2)
                with pool.Fori(0, n) as q:
                    for j in range(RECORDS):
                        pool.wait_ge(record_did, q * (5 * RECORDS) + (5 * j + 2))
                        pool.sem_inc(pool_go, 1)
                        G.indirect_dma_start(
                            out=record[:, j, 0:2 * RANKS], out_offset=None, in_=edge_rows,
                            in_offset=bass.IndirectOffsetOnAxis(ap=index_of[:, j:j + 1], axis=0)
                        ).then_inc(record_gathered[j], 16)

            @block.sync
            def _(sp):
                n = sp.value_load(counts[0:1, 1:2], min_val=1, max_val=ITEMS // RECORDS - 2)
                with sp.Fori(0, n) as q:
                    for j in range(RECORDS):
                        sp.wait_ge(record_did, q * (5 * RECORDS) + (5 * j + 6))
                        sp.wait_ge(record_gathered[j], q * 16 + 16)
                        sp.dma_start(slots[bass.ds(q * RECORDS + j, 1), :, :].rearrange("o p k -> p (o k)"),
                                     record[:, j, :]).then_inc(record_stored[j], 16)
                for j in range(RECORDS):
                    sp.wait_ge(record_stored[j], n * 16 + 16)
                    sp.sem_inc(sync_go, 1)

        projections, groups_added = [0], [0]
        ln_flat = ln_stats[:, :, :].rearrange("p t k -> p (t k)")

        def project(src, weight, bias, dst_of, cols, table=None, width=0, afterwards=(), plus=None,
                    dst=None, stats=False):
            added = groups_added[0]
            groups_added[0] += GROUPS if plus is not None else 0
            base = projections[0] * T
            projections[0] += 1
            with nc.Block() as block:
                @block.scalar
                def _(act):
                    def stage_group(group, j):
                        A.copy(htile[:, j, :], src[:, bass.ds(group * (GROUP * D), GROUP * D)]).then_inc(staged_tile, 1)

                    def turn(group, j):
                        act.wait_ge(transposed, group + (base // GROUP + 1))
                        act.wait_ge(projected, group * GROUP + (base + 1))
                        A.copy(hT[:, j, 0:4 * D], ps[:, 5, :])
                        A.copy(hT[:, j, 4 * D:GROUP * D], ps[:, 6, 0:D]).then_inc(turned, 1)

                    stage_group(0, 0)
                    with act.Fori(0, GROUPS // 2) as q:
                        stage_group(q * 2 + 1, 1)
                        turn(q * 2, 0)
                        stage_group(q * 2 + 2, 0)
                        turn(q * 2 + 1, 1)
                    turn(GROUPS - 1, 0)

                @block.tensor
                def _(pe):
                    def transposes(group, j):
                        pe.wait_ge(staged_tile, group + (base // GROUP + 1))
                        pe.wait_ge(turned, group + (base // GROUP + 1))
                        for k in range(GROUP):
                            mm = nc.tensor.transpose(ps[:, 5 + k // 4, (k % 4) * D:(k % 4) * D + D],
                                                     htile[:, j, k * D:(k + 1) * D], ident[:, :])
                        mm.then_inc(transposed, 1)

                    def products(group, j):
                        pe.wait_ge(turned, group + (base // GROUP + 2))
                        for k in range(GROUP):
                            pe.wait_ge(evacuated, group * GROUP + (base + k + 1))
                            nc.tensor.matmul(ps[:, k, 0:cols], hT[:, j, k * D:(k + 1) * D], weight, start=True,
                                             stop=True).then_inc(projected, 1)

                    transposes(0, 0)
                    with pe.Fori(0, GROUPS // 2) as q:
                        transposes(q * 2 + 1, 1)
                        products(q * 2, 0)
                        transposes(q * 2 + 2, 0)
                        products(q * 2 + 1, 1)
                    products(GROUPS - 1, 0)

                @block.vector
                def _(dve):
                    with dve.Fori(0, T // GROUP) as q:
                        for k in range(GROUP):
                            dve.wait_ge(projected, q * GROUP + (base + GROUP + k + 2))
                            if bias is None:
                                V.tensor_scalar(dst_of(q * GROUP + k), ps[:, k, 0:cols], 1.0, None, ALU.mult
                                                ).then_inc(evacuated, 1)
                            else:
                                V.tensor_tensor(dst_of(q * GROUP + k), ps[:, k, 0:cols], bias, ALU.add
                                                ).then_inc(evacuated, 1)
                        if plus is not None:
                            group = bass.ds(q * (GROUP * D), GROUP * D)
                            dve.wait_ge(evacuated, q * GROUP + (base + 2 * GROUP))
                            V.tensor_tensor(plus[:, group], plus[:, group], dst[:, group], ALU.add).then_inc(group_added, 1)
                            if stats:
                                dve.wait_ge(group_added, q + (added + 1))
                                for k in range(GROUP):
                                    V.bn_stats(ln_flat[:, bass.ds(q * (GROUP * 6) + k * 6, 6)],
                                               plus[:, bass.ds(q * (GROUP * D) + k * D, D)]).then_inc(stats_did, 1)
                    for n, step in enumerate(afterwards):
                        if n == 0:
                            dve.wait_ge(evacuated, base + GROUP + T)
                        vec_op(step())

                if table is out:
                    @block.gpsimd
                    def _(pool):
                        for t in range(T):
                            rows_here = P if t < T - 1 else LAST
                            pool.wait_ge(group_added, added + t // GROUP + 1)
                            out_stored.did(G.indirect_dma_start(
                                out=out, out_offset=bass.IndirectOffsetOnAxis(ap=node_id[0:rows_here, t:t + 1], axis=0),
                                in_=x_all[0:rows_here, t, :], in_offset=None), 16)
                        out_stored.need(pool, out_stored.n)
                elif table is not None:
                    @block.gpsimd
                    def _(pool):
                        for t in range(T):
                            pool.wait_ge(evacuated, base + GROUP + t + 1)
                            scattered.did(G.indirect_dma_start(
                                out=table, out_offset=bass.IndirectOffsetOnAxis(ap=node_id[:, t:t + 1], axis=0),
                                in_=stage[:, t * width:t * width + table.shape[1]], in_offset=None), 16)
                        scattered.need(pool, scattered.n)

        def scatter(table, width, meanwhile=()):
            with nc.Block() as block:
                @block.vector
                def _(dve):
                    for step in meanwhile:
                        vec_op(step())

                @block.gpsimd
                def _(pool):
                    for t in range(T):
                        scattered.did(G.indirect_dma_start(
                            out=table, out_offset=bass.IndirectOffsetOnAxis(ap=node_id[:, t:t + 1], axis=0),
                            in_=stage[:, t * width:t * width + table.shape[1]], in_offset=None), 16)
                    scattered.need(pool, scattered.n)

        u_all = stage[:, T * TW:T * TW + T * D]
        ring0 = stage[:, T * (TW + D):T * (TW + D) + 2 * RANKS * GROUP * TW].rearrange(
            "p (j r k d) -> p j r k d", j=2, r=RANKS, k=GROUP)
        slot0 = sb("slot0", [P, 2, GROUP, SLOT])
        state = sb("state", [P, GROUPS * 4 * GROUP])
        RG = RANKS * GROUP
        e_a, e_den, e_t, e_t2, e_t3 = (sb(f"edge_{n}", [P, RANKS, GROUP]) for n in ("a", "den", "t", "t2", "t3"))
        h_copy = sb("h_copy", [P, 2, GROUP * D])
        e_c = sb("edge_c", [P, RANKS, GROUP])
        e_al = sb("edge_al", [P, 2, RANKS, GROUP])
        e_ac = sb("edge_ac", [P, 2, RANKS, 2, GROUP])
        e_v = sb("edge_v", [P, 2, RANKS, 4, GROUP])
        e_m1 = sb("edge_m1", [P, 2, RANKS, GROUP])
        r_ts, r_om, r_hu, r_xy, r_den, r_ba = (sb("r_" + n, [P, GROUP]) for n in ("ts", "om", "hu", "xy", "den", "ba"))
        r_nr = sb("r_nr", [P, 2, GROUP])
        r_t = sb("r_t", [P, 2, GROUP])
        r_t2 = sb("r_t2", [P, 2, GROUP])
        r_ab = sb("r_ab", [P, 2, GROUP])
        r_v1 = sb("r_v1", [P, 4, GROUP])
        r_v2 = sb("r_v2", [P, 4, GROUP])
        MESSAGE_PARTS = 14
        MESSAGES = 24
        STEP = MESSAGES + RANKS * 26
        scatter(tables[0], TW, (lambda: V.memset(u_all, 0.0), lambda: V.memset(state[:, :], 0.0)))

        two_rows = flat(tb[:, :, :])[:, 0:2 * GROUP * D].rearrange("p (c k d) -> p c k d", c=2, k=GROUP)
        u_rows, w_rows = two_rows[:, 0], two_rows[:, 1]

        with nc.Block() as block:
            @block.sync
            def _(sp):
                n = sp.value_load(counts[0:1, 2:3], min_val=2, max_val=ITEMS // 2 - 1)
                with sp.Fori(0, n) as q:
                    for j in range(2):
                        sp.wait_ge(scan_slots_free, q * 2 + (j + 1))
                        sp.sem_inc(sync_go, 1)
                        for k in range(GROUP):
                            item = sp.value_load(step_items[bass.ds(q * 2 + j, 1), k:k + 1], min_val=0, max_val=ITEMS - 1)
                            sp.dma_start(slot0[:, j, k, :], slots[bass.ds(item, 1), :, :].rearrange("o p k -> p (o k)")
                                         ).then_inc(scan_slots_in[j], 16)

            @block.gpsimd
            def _(pool):
                n = pool.value_load(counts[0:1, 2:3], min_val=2, max_val=ITEMS // 2 - 1)
                with pool.Fori(0, n) as q:
                    for j in range(2):
                        pool.wait_ge(scan_slots_in[j], q * (16 * GROUP) + 16 * GROUP)
                        for r in range(RANKS):
                            pool.wait_ge(scan_free, q * (2 * RANKS) + (j * RANKS + r + 1))
                            pool.sem_inc(pool_go, 1)
                            for k in range(GROUP):
                                G.indirect_dma_start(
                                    out=ring0[:, j, r, k, :], out_offset=None, in_=tables[0],
                                    in_offset=bass.IndirectOffsetOnAxis(ap=slot0[:, j, k, r:r + 1].bitcast(I32), axis=0)
                                ).then_inc(scan_gathered[j][r], 16)

            @block.scalar
            def _(act):
                n = act.value_load(counts[0:1, 3:4], min_val=1, max_val=ITEMS // 2 - 2)

                def copy_h(step, j):
                    g = act.value_load(group_row[0:1, bass.ds(step, 1)], min_val=0, max_val=GROUPS - 1)
                    act.wait_ge(scan_slots_free, step + 1)
                    act.sem_inc(scalar_go, 1)
                    A.copy(h_copy[:, j, :], flat(h_all[:, :, :])[:, bass.ds(g * (GROUP * D), GROUP * D)]
                           ).then_inc(h_copied, 1)

                def scale_rows(step, j):
                    for r in range(RANKS):
                        act.wait_ge(factor_ready, step * RANKS + (r + 1))
                        for k in range(SCAN_VECTOR_TILES, GROUP):
                            ins = A.activation(w_rows[:, k, :], ring0[:, j, r, k, 0:D], ACT.Identity, scale=r_ba[:, k:k + 1])
                        ins.then_inc(rows_scaled, 1)

                copy_h(0, 0)
                copy_h(1, 1)
                with act.Fori(0, n) as q:
                    for j in range(2):
                        copy_h(q * 2 + (j + 2), j)
                        scale_rows(q * 2 + j, j)
                for j in range(2):
                    scale_rows(n * 2 + j, j)

            @block.vector
            def _(dve):
                mine = slice(0, SCAN_VECTOR_TILES)
                n = dve.value_load(counts[0:1, 3:4], min_val=1, max_val=ITEMS // 2 - 2)

                def group_of(step):
                    return dve.value_load(group_row[0:1, bass.ds(step, 1)], min_val=0, max_val=GROUPS - 1)

                class Messages:

                    def __init__(self, j, pair, g):
                        self.j, self.pair, self.part = j, pair, 0
                        self.y2 = spread(y2_all[:, bass.ds(g * GROUP, GROUP)], 1, RANKS)

                    def next(self, did):
                        j, y2 = self.j, self.y2
                        src_h, x2 = ring0[:, j, :, :, 0:D], ring0[:, j, :, :, D]
                        mask = slot0[:, j, :, 3 * RANKS:4 * RANKS].rearrange("p k r -> p r k")
                        tmp = flat(ta[:, :, :])[:, 0:RG * D].rearrange("p (r k d) -> p r k d", r=RANKS, k=GROUP)
                        a, den, t, t2, t3, c = (e[:, :, :] for e in (e_a, e_den, e_t, e_t2, e_t3, e_c))
                        alpha_, alpha_c, beta = e_al[:, j], e_ac[:, j, :, 0], e_ac[:, j, :, 1]
                        v = lambda k: e_v[:, j, :, k]
                        part, self.part = self.part, self.part + 1
                        if part == 0:
                            dve.wait_ge(h_copied, self.pair * 2 + (j + 1))
                            for r in range(RANKS):
                                dve.wait_ge(scan_gathered[j][r], self.pair * (16 * GROUP) + 16 * GROUP)
                        else:
                            did.need(dve, self.mark)
                        if part == 0:
                            V.sem_inc(vector_go, 1)
                            for r in range(RANKS):
                                for k in range(GROUP):
                                    dot = V.tensor_tensor_reduce(tmp[:, r, k], src_h[:, r, k], h_copy[:, j, k * D:(k + 1) * D],
                                                                 1.0, 0.0, ALU.mult, ALU.add, c[:, r, k:k + 1])
                            did.did(dot)
                        elif part == 1:
                            did.did(V.tensor_scalar(a, c, -2.0, 1.0, ALU.mult, ALU.add))
                            did.did(V.tensor_tensor(den, x2, y2, ALU.mult))
                        elif part == 2:
                            did.did(V.tensor_tensor(den, den, a, ALU.add))
                        elif part == 3:
                            did.did(V.tensor_scalar(den, den, EPS_BALL, None, ALU.max))
                            did.did(V.tensor_tensor(a, a, y2, ALU.add))
                        elif part == 4:
                            did.did(V.reciprocal(den, den))
                        elif part == 5:
                            did.did(V.tensor_tensor(den, den, mask, ALU.mult))
                            did.did(V.tensor_scalar(t, x2, -1.0, None, ALU.add))
                        elif part == 6:
                            did.did(V.tensor_tensor(alpha_, a, den, ALU.mult))
                            did.did(V.tensor_tensor(beta, t, den, ALU.mult))
                            did.did(V.tensor_tensor(v(0), t, den, ALU.mult))
                        elif part == 7:
                            did.did(V.tensor_tensor(alpha_c, alpha_, c, ALU.mult))
                            did.did(V.tensor_tensor(t2, alpha_, x2, ALU.mult))
                        elif part == 8:
                            did.did(V.tensor_tensor(t, beta, y2, ALU.mult))
                            did.did(V.tensor_tensor(t3, beta, c, ALU.mult))
                        elif part == 9:
                            did.did(V.tensor_tensor(v(1), t, alpha_c, ALU.add))
                            did.did(V.tensor_tensor(t2, t2, t3, ALU.add))
                        elif part == 10:
                            did.did(V.tensor_tensor(t2, t2, alpha_, ALU.mult))
                            did.did(V.tensor_tensor(t, beta, v(1), ALU.mult))
                        elif part == 11:
                            did.did(V.tensor_tensor(v(3), t2, t, ALU.add))
                        elif part == 12:
                            did.did(V.tensor_scalar(e_m1[:, j], v(3), 1.0, None, ALU.add))
                        elif part == 13:
                            V.memset(e_t3[:, 0, 0:1], 0.0).then_inc(scan_slots_free, 1)
                        self.mark = did.n

                def totals(j, g, base, ahead, step):
                    did = Count(scan_did, base)
                    u = u_all[:, bass.ds(g * (GROUP * D), GROUP * D)].rearrange("p (k d) -> p k d", k=GROUP)
                    st = lambda a0, a1: state[:, bass.ds(g * (4 * GROUP) + a0 * GROUP, (a1 - a0) * GROUP)].rearrange(
                        "p (c k) -> p c k", k=GROUP)
                    st1 = lambda a0: state[:, bass.ds(g * (4 * GROUP) + a0 * GROUP, GROUP)]
                    u_h, w_h = u_rows, w_rows
                    ts, om, hu, xy, den, ba = (t[:, :] for t in (r_ts, r_om, r_hu, r_xy, r_den, r_ba))

                    def between():
                        if ahead is not None and ahead.part < MESSAGE_PARTS:
                            ahead.next(did)

                    dve.wait_ge(scan_did, base)
                    m_u, m_st, m_t2 = 0, 0, 0
                    for r in range(RANKS):
                        hs = ring0[:, j, r, :, 0:D]
                        al, v = e_al[:, j, r], e_v[:, j, r]
                        if r > 0:
                            did.need(dve, m_st)
                        m_r = did.did(V.tensor_tensor(r_t[:, :, :], st(0, 2), e_ac[:, j, r], ALU.mult))
                        if r > 0:
                            did.need(dve, m_u)
                        m = did.did(V.tensor_tensor(u_h, hs, u, ALU.mult))
                        if r > 0:
                            did.need(dve, m_t2)
                            m_t2 = did.did(V.tensor_tensor(st1(2), r_t2[:, 0, :], r_t2[:, 1, :], ALU.add))
                        did.need(dve, m_r)
                        did.did(V.tensor_tensor(ts, r_t[:, 0, :], r_t[:, 1, :], ALU.add))
                        did.need(dve, m)
                        m = did.did(V.tensor_reduce(hu, u_h, X, ALU.add))
                        if r > 0:
                            did.need(dve, m_t2)
                        m_o = did.did(V.tensor_tensor(om, st1(2), v[:, 3], ALU.mult))
                        did.did(V.tensor_scalar(r_nr[:, 1, :], st1(2), -1.0, 1.0, ALU.mult, ALU.add))
                        did.need(dve, m)
                        m = did.did(V.tensor_tensor(xy, hu, al, ALU.mult))
                        if r > 0:
                            between()
                        did.need(dve, m_o)
                        did.did(V.tensor_scalar(om, om, 1.0, None, ALU.add))
                        did.need(dve, m)
                        did.did(V.tensor_tensor(st1(3), xy, ts, ALU.add))
                        m = did.did(V.tensor_tensor(v[:, 2], xy, ts, ALU.add))
                        if r > 0:
                            between()
                        did.need(dve, m)
                        m = did.did(V.scalar_tensor_tensor(out=den, in0=v[:, 2], scalar=2.0, in1=om, op0=ALU.mult, op1=ALU.add))
                        did.did(V.scalar_tensor_tensor(out=r_nr[:, 0, :], in0=v[:, 2], scalar=2.0, in1=e_m1[:, j, r],
                                                       op0=ALU.mult, op1=ALU.add))
                        did.need(dve, m)
                        m = did.did(V.tensor_scalar(den, den, EPS_BALL, None, ALU.max))
                        if r > 0:
                            between()
                        did.need(dve, m)
                        m = did.did(V.reciprocal(den, den))
                        if r > 0:
                            between()
                        did.need(dve, m)
                        m = did.did(V.tensor_tensor(r_ab[:, :, :], r_nr[:, :, :], spread(den, 1, 2), ALU.mult))
                        if r > 0:
                            between()
                        did.need(dve, m)
                        V.tensor_tensor(ba, r_ab[:, 1, :], al, ALU.mult).then_inc(factor_ready, 1)
                        did.did(V.tensor_tensor(u, u, spread(r_ab[:, 0, :], 2, D), ALU.mult))
                        dve.wait_ge(factor_ready, step * RANKS + (r + 1))
                        m_u = did.did(V.tensor_tensor(w_h[:, mine], hs[:, mine], spread(ba[:, mine], 2, D), ALU.mult))
                        did.did(V.tensor_tensor(r_v1[:, :, :], st(0, 4), spread(r_ab[:, 0, :], 1, 4), ALU.mult))
                        m = did.did(V.tensor_tensor(r_v2[:, :, :], v, spread(r_ab[:, 1, :], 1, 4), ALU.mult))
                        did.need(dve, m_u)
                        dve.wait_ge(rows_scaled, step * RANKS + (r + 1))
                        V.memset(r_hu[:, 0:1], 0.0).then_inc(scan_free, 1)
                        did.need(dve, m)
                        m_st = did.did(V.tensor_tensor(st(0, 4), r_v1[:, :, :], r_v2[:, :, :], ALU.add))
                        m_u = did.did(V.tensor_tensor(u, u, w_h, ALU.add))
                        did.need(dve, m_st)
                        m_t2 = did.did(V.tensor_tensor(r_t2[:, :, :], st(2, 4), r_ab[:, :, :], ALU.mult))
                        if r == RANKS - 1:
                            did.need(dve, m_t2)
                            did.did(V.tensor_tensor(st1(2), r_t2[:, 0, :], r_t2[:, 1, :], ALU.add), by=STEP - did.n)

                g = group_of(0)
                first = Messages(0, 0, g)
                did = Count(scan_did, 1)
                for _ in range(MESSAGE_PARTS):
                    first.next(did)
                ready = did.base + did.n
                g_next = group_of(1)
                totals(0, g, ready, Messages(1, 0, g_next), 0)
                with dve.Fori(0, n) as q:
                    base = dve.snap(q * (2 * STEP) + (ready + STEP))
                    odd, even, odd_after = group_of(q * 2 + 1), group_of(q * 2 + 2), group_of(q * 2 + 3)
                    totals(1, odd, base, Messages(0, q + 1, even), q * 2 + 1)
                    totals(0, even, dve.snap(base + STEP), Messages(1, q + 1, odd_after), q * 2 + 2)
                totals(1, group_of(n * 2 + 1), dve.snap(n * (2 * STEP) + (ready + STEP)), None,
                       n * 2 + 1)

        by_g = lambda t3: t3.rearrange("p (g k) d -> p g k d", k=GROUP)
        gamma_g = state[:, :].rearrange("p (g c k) -> p g c k", c=4, k=GROUP)[:, :, 0, :]
        total_v = stage[:, 0:T * D].rearrange("p (t d) -> p t d", d=D)
        nrm, ratio, k1, k2, k3, k4, k5, k6 = (sm[:, n, :] for n in range(8))
        vector_block(
            lambda: V.tensor_tensor(by_g(ta[:, :, :]), by_g(h_all[:, :, :]), spread(gamma_g, 3, D), ALU.mult),
            lambda: V.tensor_tensor(total_v, ta[:, :, :], u_all.rearrange("p (t d) -> p t d", d=D), ALU.add))
        with nc.Block() as block:
            @block.vector
            def _(dve):
                vec_op(V.tensor_tensor(ta[:, :, :], total_v, h_all[:, :, :], ALU.mult))
                vec_op(V.tensor_reduce(k5, ta[:, :, :], X, ALU.add))
                vec_op(V.tensor_scalar(k4, node_deg[:, :], 1.0, None, ALU.max))
                vec_op(V.reciprocal(k4, k4))

            @block.scalar
            def _(act):
                for t in range(T):
                    scalar_did.did(A.activation(tb[:, t, :], total_v[:, t, :], ACT.Square, accum_out=k6[:, t:t + 1]))
                scalar_did.need(act, scalar_did.n)
                scalar_did.did(A.activation(nrm, k6, ACT.Sqrt))
        norm_c = sm[:, 8, :]
        sq = sm[:, 9, :]
        series = sm[:, 10, :]
        small = sm[:, 11, :]

        def horner(c):
            return lambda: V.tensor_tensor(series, series, sq, ALU.mult), \
                lambda: V.tensor_scalar(series, series, c, None, ALU.add)

        vector_block(
            lambda: V.tensor_scalar(norm_c, nrm, EPS_BALL, 1.0 - EPS_BALL, ALU.max, ALU.min),
            lambda: V.tensor_tensor(sq, norm_c, norm_c, ALU.mult),
            lambda: V.tensor_scalar(series, sq, 1.0 / 15, 1.0 / 13, ALU.mult, ALU.add),
            *horner(1.0 / 11), *horner(1.0 / 9), *horner(1.0 / 7), *horner(1.0 / 5), *horner(1.0 / 3), *horner(1.0),
            lambda: V.tensor_tensor(series, series, norm_c, ALU.mult),
            lambda: V.tensor_scalar(small, norm_c, 0.25, None, ALU.is_lt),
            lambda: V.tensor_scalar(k1, norm_c, -1.0, 1.0, ALU.mult, ALU.add),
            lambda: V.reciprocal(k1, k1),
            lambda: V.tensor_scalar(k2, norm_c, 1.0, None, ALU.add),
            lambda: V.tensor_tensor(k1, k1, k2, ALU.mult))
        with nc.Block() as block:
            @block.scalar
            def _(act):
                scalar_did.did(A.activation(k1, k1, ACT.Ln))
        vector_block(
            lambda: V.tensor_scalar(k1, k1, 0.5, None, ALU.mult),
            lambda: V.tensor_tensor(series, series, k1, ALU.subtract),
            lambda: V.tensor_tensor(series, series, small, ALU.mult),
            lambda: V.tensor_tensor(k1, k1, series, ALU.add),
            lambda: V.tensor_tensor(k1, k1, k4, ALU.mult))
        with nc.Block() as block:
            @block.scalar
            def _(act):
                scalar_did.did(A.activation(k1, k1, ACT.Tanh))
        vector_block(
            lambda: V.reciprocal(norm_c, norm_c),
            lambda: V.tensor_tensor(ratio, k1, norm_c, ALU.mult),
            lambda: V.tensor_scalar(k1, nrm, EPS_BALL, None, ALU.is_gt),
            lambda: V.tensor_tensor(ratio, ratio, k1, ALU.mult),
            lambda: V.tensor_tensor(k5, k5, ratio, ALU.mult),
            lambda: V.tensor_tensor(k6, k6, ratio, ALU.mult),
            lambda: V.tensor_tensor(k6, k6, ratio, ALU.mult),
            lambda: V.tensor_scalar(k5, k5, 2.0, 1.0, ALU.mult, ALU.add),
            lambda: V.tensor_tensor(k1, y2_all[:, :], k6, ALU.mult),
            lambda: V.tensor_tensor(k1, k1, k5, ALU.add),
            lambda: V.tensor_scalar(k1, k1, EPS_BALL, None, ALU.max),
            lambda: V.reciprocal(k1, k1),
            lambda: V.tensor_tensor(k5, k5, k6, ALU.add),
            lambda: V.tensor_tensor(k5, k5, k1, ALU.mult),
            lambda: V.tensor_scalar(k2, y2_all[:, :], -1.0, 1.0, ALU.mult, ALU.add),
            lambda: V.tensor_tensor(k2, k2, k1, ALU.mult),
            lambda: V.tensor_tensor(k2, k2, ratio, ALU.mult),
            lambda: V.tensor_tensor(ta[:, :, :], h_all[:, :, :], spread(k5, 2, D), ALU.mult),
            lambda: V.tensor_tensor(x_all[:, :, :], x_all[:, :, :], ta[:, :, :], ALU.add),
            lambda: V.tensor_tensor(ta[:, :, :], total_v, spread(k2, 2, D), ALU.mult),
            lambda: V.tensor_tensor(x_all[:, :, :], x_all[:, :, :], ta[:, :, :], ALU.add))

        phase_no = [0]

        def attention(table, width, heads, kind, loads, att_dst=None):
            phase = phase_no[0]
            phase_no[0] += 1
            rows_gathered = rows_gathered_in[phase]
            Ch = D // heads
            extra = 2 if kind == "weighted" else 1
            W = heads * (Ch + extra)
            value0 = 0 if kind == "added" else D
            scale = 1.0 if kind == "added" else float(Ch) ** -0.5
            q_col = 2 * D

            with nc.Block() as block:
                @block.sync
                def _(sp):
                    for dst, src in loads:
                        params_in.did(sp.dma_start(dst, src), 16)
                    n = sp.value_load(counts[0:1, 0:1], min_val=2, max_val=ITEMS // RING - 2)
                    before = sp.snap(n * phase)
                    steps_before = sp.snap(n * (phase * RING * STEPS) + (phase * STEPS + 1))
                    with sp.Fori(0, n) as q:
                        for j in range(RING):
                            item = slots[bass.ds(q * RING + j, 1), :, :].rearrange("o p k -> p (o k)")
                            sp.wait_ge(step_did, steps_before + q * (RING * STEPS) + (j * STEPS + 1))
                            sp.dma_start(sources[:, j, :], item[:, 0:RANKS]).then_inc(sources_loaded[j], 16)
                            sp.wait_ge(ring_free, before * RING + q * RING + (j + 1))
                            sp.dma_start(slot[:, j, RANKS:3 * RANKS], item[:, RANKS:3 * RANKS]).then_inc(slot_loaded[j], 16)
                    params_in.need(sp, params_in.n)

                @block.gpsimd
                def _(pool):
                    n = pool.value_load(counts[0:1, 0:1], min_val=2, max_val=ITEMS // RING - 2)
                    before = pool.snap(n * phase)
                    with pool.Fori(0, n) as q:
                        for j in range(RING):
                            pool.wait_ge(sources_loaded[j], before * 16 + q * 16 + 16)
                            pool.wait_ge(ring_free, before * RING + q * RING + (j + 1))
                            pool.sem_inc(pool_go, 1)
                            for r in range(RANKS):
                                G.indirect_dma_start(
                                    out=rows[:, j, r, 0:table.shape[1]], out_offset=None, in_=table,
                                    in_offset=bass.IndirectOffsetOnAxis(ap=sources[:, j, r:r + 1].bitcast(I32), axis=0)
                                ).then_inc(rows_gathered[j], 16)

                @block.scalar
                def _(act):
                    n = act.value_load(counts[0:1, 0:1], min_val=2, max_val=ITEMS // RING - 2)
                    before = act.snap(n * phase)
                    with act.Fori(0, n) as q:
                        for j in range(RING):
                            act.wait_ge(shifted, before * RING + q * RING + (j + 1))
                            weights = pv[:, j, :, 0:W].rearrange("p r (h c) -> p r h c", h=heads)[:, :, :, Ch]
                            A.activation(weights, dif[:, j, 0:RANKS, 0:heads], ACT.Exp)
                            A.activation(alpha[:, j, 0:heads], dif[:, j, RANKS, 0:heads], ACT.Exp).then_inc(exp_did, 1)

                @block.tensor
                def _(pe):
                    n = pe.value_load(counts[0:1, 0:1], min_val=2, max_val=ITEMS // RING - 2)
                    before = pe.snap(n * phase)
                    with pe.Fori(0, n) as q:
                        for j in range(RING):
                            pe.wait_ge(ring_free, before * RING + q * RING + (RING + j + 1))
                            for r in range(RANKS):
                                mm = nc.tensor.matmul(ps[:, j % 2, 0:W], ident[:, :], pv[:, j, r, 0:W],
                                                      start=(r == 0), stop=(r == RANKS - 1))
                            mm.then_inc(summed, 1)

                @block.vector
                def _(dve):
                    n = dve.value_load(counts[0:1, 0:1], min_val=2, max_val=ITEMS // RING - 2)
                    before = dve.snap(n * phase)
                    steps_before = dve.snap(n * (phase * RING * STEPS) + ((phase + RING) * STEPS + 1))

                    def scale_sums(did, t, j):
                        sums = acc[:, bass.ds(t * (HEADS * (C + 2)), W)].rearrange("p (h c) -> p h c", h=heads)
                        return did.did(V.tensor_tensor(sums, sums, spread(alpha[:, j, 0:heads], 2, Ch + extra), ALU.mult))

                    def add_item(did, t, j, scaled, last=False):
                        sums = acc[:, bass.ds(t * (HEADS * (C + 2)), W)]
                        did.need(dve, scaled)
                        did.did(V.tensor_tensor(sums, sums, ps[:, j % 2, 0:W], ALU.add), by=STEPS - did.n if last else 1)

                    def step(quad, k, t, t_old=None):
                        first = t_old is None
                        did = Count(step_did, dve.snap(steps_before + quad * (RING * STEPS) + k * STEPS))
                        number = dve.snap(before * RING + quad * RING)

                        def op(ins):
                            did.need(dve, did.did(ins))

                        SM, S, NM = s[:, :, 0:heads], s[:, 0:RANKS, 0:heads], new_max[:, 0:heads]
                        state_m = run_max[:, :, :].rearrange("p t h -> p (t h)")[:, bass.ds(t * HEADS, heads)]
                        row = rows[:, k, :, :]
                        dve.wait_ge(step_did, did.base)
                        dve.wait_ge(rows_gathered[k], quad * (16 * RANKS) + 16 * RANKS)
                        dve.wait_ge(slot_loaded[k], (before + quad) * 16 + 16)
                        if kind == "added":
                            dst_part = att_dst.rearrange("p t h -> p (t h)")[:, bass.ds(t * HEADS, heads)]
                            m_prod = did.did(V.tensor_tensor(S, row[:, :, D:D + heads], spread(dst_part, 1, RANKS), ALU.add))
                        else:
                            query = stage[:, bass.ds(t * width + q_col, D)]
                            m_prod = did.did(V.tensor_tensor(prod[:, :, :], row[:, :, 0:D], spread(query, 1, RANKS), ALU.mult))
                        did.did(V.tensor_tensor(s[:, RANKS, 0:heads], state_m, state_m, ALU.max))
                        mask = spread(slot[:, k, 2 * RANKS:3 * RANKS], 2, heads)
                        if kind == "weighted":
                            qe_t = qe[:, :, :].rearrange("p t h -> p (t h)")[:, bass.ds(t * HEADS, heads)]
                            m_w = did.did(V.tensor_tensor(s_w[:, :, :], spread(slot[:, k, RANKS:2 * RANKS], 2, heads),
                                                          spread(qe_t, 1, RANKS), ALU.mult))
                        did.need(dve, m_prod)
                        if kind == "added":
                            op(V.scalar_tensor_tensor(out=S, in0=S, scalar=0.2, in1=S, op0=ALU.mult, op1=ALU.max))
                        else:
                            did.did(V.tensor_reduce(S, prod[:, :, :].rearrange("p r (h c) -> p r h c", h=heads), X, ALU.add))
                            m_s = did.n
                            if kind == "weighted":
                                did.need(dve, m_w)
                                did.did(V.scalar_tensor_tensor(out=s_w[:, :, :], in0=s_w[:, :, :], scalar=scale, in1=mask,
                                                               op0=ALU.mult, op1=ALU.add))
                                m_s = did.n
                                mask = s_w[:, :, :]
                            did.need(dve, m_s)
                        op(V.scalar_tensor_tensor(out=S, in0=S, scalar=scale, in1=mask, op0=ALU.mult, op1=ALU.add))
                        op(V.tensor_reduce(NM, SM.rearrange("p r h -> p h r"), X, ALU.max))
                        V.tensor_tensor(dif[:, k, :, 0:heads], SM, spread(NM, 1, RANKS + 1), ALU.subtract).then_inc(shifted, 1)
                        did.did(V.tensor_tensor(state_m, NM, NM, ALU.max))
                        if not first:
                            dve.wait_ge(summed, number + k)
                            scaled = scale_sums(did, t_old, (k - 1) % RING)
                        out4 = pv[:, k, :, 0:W].rearrange("p r (h c) -> p r h c", h=heads)
                        dve.wait_ge(exp_did, number + (k + 1))
                        if kind == "weighted":
                            did.did(V.tensor_tensor(out4[:, :, :, Ch + 1], out4[:, :, :, Ch],
                                                    spread(slot[:, k, RANKS:2 * RANKS], 2, heads), ALU.mult))
                        V.tensor_tensor(out4[:, :, :, 0:Ch], row[:, :, value0:value0 + D].rearrange("p r (h c) -> p r h c", h=heads),
                                        spread(out4[:, :, :, Ch], 3, Ch), ALU.mult).then_inc(ring_free, 1)
                        if not first:
                            add_item(did, t_old, (k - 1) % RING, scaled, last=True)
                        else:
                            V.memset(step_mark[:, 0:1], 0.0).then_inc(step_did, STEPS - did.n)

                    here = tiles(dve, 0)
                    step(0, 0, here[0])
                    for k in range(1, RING):
                        step(0, k, here[k], here[k - 1])
                    with dve.Fori(1, n) as q:
                        t_before = tiles(dve, q - 1)[RING - 1]
                        here = tiles(dve, q)
                        step(q, 0, here[0], t_before)
                        for k in range(1, RING):
                            step(q, k, here[k], here[k - 1])
                    did = Count(step_did, dve.snap(steps_before + n * (RING * STEPS)))
                    t = tiles(dve, n - 1)[RING - 1]
                    dve.wait_ge(step_did, did.base)
                    dve.wait_ge(summed, dve.snap((before + n) * RING))
                    add_item(did, t, RING - 1, scale_sums(did, t, RING - 1))
                    did.need(dve, did.n)
                    V.memset(step_mark[:, 0:1], 0.0).then_inc(step_did, STEPS - did.n)

        heads_of = lambda t3: t3.rearrange("p t (h c) -> p t h c", h=HEADS)

        def sums_of(heads, extra):
            Ch = D // heads
            view = acc[:, :].rearrange("p (t w) -> p t w", t=T)[:, :, 0:heads * (Ch + extra)]
            return view.rearrange("p t (h c) -> p t h c", h=heads)

        def add_to_x(what):
            vector_block(lambda: V.tensor_tensor(x_all[:, :, :], x_all[:, :, :], what, ALU.add))

        clear_sums = (lambda: V.memset(acc[:, :], 0.0),
                      lambda: V.memset(run_max[:, :, :], UNSET))

        def node_sum(src):
            with nc.Block() as block:
                @block.tensor
                def _(pe):
                    nc.tensor.matmul(ps[:, 0, 0:D], valid[:, :], src[:, T - 1, :], start=True, stop=False)
                    with pe.Fori(0, GROUPS - 1) as q:
                        for k in range(GROUP):
                            nc.tensor.matmul(ps[:, 0, 0:D], onesf[:, :], flat(src)[:, bass.ds(q * (GROUP * D) + k * D, D)],
                                             start=False, stop=False)
                    for t in range(T - GROUP, T - 1):
                        mm = nc.tensor.matmul(ps[:, 0, 0:D], onesf[:, :], src[:, t, :], start=False, stop=(t == T - 2))
                    tensor_did.did(mm)

        layer_norm(h_all[:, :, :], x_all[:, :, :], relu=True)
        project(flat(h_all[:, :, :]), w["L1"][:, :], None, lambda t: stage[:, bass.ds(t * TW, D)], D)
        att_d = sb("att_d", [P, T, HEADS])
        hw = table_rows[:, :, 0:D]
        a_src = table_rows[:, :, D:TW]
        sums = sums_of(HEADS, 1)
        vector_block(
            lambda: V.tensor_tensor(ta[:, :, :], hw, spread(vec["att_src"][:, :], 1, T), ALU.mult),
            lambda: V.tensor_reduce(a_src, heads_of(ta[:, :, :]), X, ALU.add))
        scatter(tables[1], TW, (
            lambda: V.tensor_tensor(ta[:, :, :], hw, spread(vec["att_dst"][:, :], 1, T), ALU.mult),
            lambda: V.tensor_reduce(att_d[:, :, :], heads_of(ta[:, :, :]), X, ALU.add),
            lambda: V.tensor_tensor(qe[:, :, :], a_src, att_d[:, :, :], ALU.add),
            lambda: V.scalar_tensor_tensor(out=run_max[:, :, :], in0=qe[:, :, :], scalar=0.2, in1=qe[:, :, :],
                                           op0=ALU.mult, op1=ALU.max),
            lambda: V.memset(sums[:, :, :, C], 1.0),
            lambda: V.tensor_copy(sums[:, :, :, 0:C], heads_of(hw))))
        attention(tables[1], TW, HEADS, "added", into_L2(0) + [load for l in range(L2_LAYERS) for load in out_of_L2(l)], att_dst=att_d[:, :, :])
        vector_block(
            lambda: V.tensor_scalar(qe[:, :, :], sums[:, :, :, C], 1e-16, None, ALU.add),
            lambda: V.reciprocal(qe[:, :, :], qe[:, :, :]),
            lambda: V.tensor_tensor(heads_of(ta[:, :, :]), sums[:, :, :, 0:C], spread(qe[:, :, :], 3, C), ALU.mult),
            lambda: V.tensor_tensor(ta[:, :, :], ta[:, :, :], spread(vec["L1_bias"][:, :], 1, T), ALU.add),
            lambda: V.tensor_tensor(ta[:, :, :], ta[:, :, :], h_all[:, :, :], ALU.add))
        layer_norm(h_all[:, :, :], ta[:, :, :], gamma=vec["L1_gamma"][:, :], beta=vec["L1_beta"][:, :])
        add_to_x(h_all[:, :, :])

        layer_norm(h_all[:, :, :], x_all[:, :, :], relu=True)
        h_tile = lambda t: flat(h_all[:, :, :])[:, bass.ds(t * D, D)]
        a_tile = lambda t: flat(ta[:, :, :])[:, bass.ds(t * D, D)]
        project(flat(h_all[:, :, :]), w["Win"][:, :], vec["bin"][:, :], h_tile, D)
        vector_block(lambda: V.tensor_scalar(flat(h_all[:, :, :]), flat(h_all[:, :, :]), 0.0, None, ALU.max))
        col = sb("col", [P, 4, D])
        sums = sums_of(HEADS, 2)
        for l in range(L2_LAYERS):
            W2 = 4 * D
            cols2 = stage[:, 0:T * W2].rearrange("p (t d) -> p t d", d=W2)
            skip = cols2[:, :, 3 * D:4 * D]
            We = vec[f"We_{l}"][:, :]
            wb = v_gate[:, l, :]
            gate = sm[:, 0, :]
            gate2 = sm[:, 1, :]
            project(flat(h_all[:, :, :]), w_in[:, :], b_in[:, :],
                    lambda t: stage[:, bass.ds(t * W2, W2)], W2, table=tables[2 + l], width=W2,
                    afterwards=clear_sums + (
                        lambda: V.tensor_tensor(ta[:, :, :], cols2[:, :, 2 * D:3 * D], spread(We, 1, T), ALU.mult),
                        lambda: V.tensor_reduce(qe[:, :, :], heads_of(ta[:, :, :]), X, ALU.add),
                        lambda: V.tensor_tensor(col[:, 0, :], wb[:, 0:D], wb[:, 2 * D:3 * D], ALU.add),
                        lambda: V.tensor_tensor(col[:, 1, :], wb[:, D:2 * D], wb[:, 2 * D:3 * D], ALU.subtract),
                        lambda: V.tensor_tensor(tb[:, :, :], skip, spread(col[:, 1, :], 1, T), ALU.mult),
                        lambda: V.tensor_reduce(gate2, tb[:, :, :], X, ALU.add)))
            attention(tables[2 + l], W2, HEADS, "weighted",
                      into_L2(l + 1) if l + 1 < L2_LAYERS else into_L3(0))
            vector_block(
                lambda: V.tensor_scalar(qe[:, :, :], sums[:, :, :, C], 1e-30, None, ALU.max),
                lambda: V.reciprocal(qe[:, :, :], qe[:, :, :]),
                lambda: V.tensor_tensor(heads_of(tb[:, :, :]), spread(We.rearrange("p (h c) -> p h c", h=HEADS), 1, T),
                                        spread(sums[:, :, :, C + 1], 3, C), ALU.mult),
                lambda: V.tensor_tensor(heads_of(tb[:, :, :]), heads_of(tb[:, :, :]), sums[:, :, :, 0:C], ALU.add),
                lambda: V.tensor_tensor(heads_of(ta[:, :, :]), heads_of(tb[:, :, :]), spread(qe[:, :, :], 3, C), ALU.mult),
                lambda: V.tensor_tensor(tb[:, :, :], ta[:, :, :], spread(col[:, 0, :], 1, T), ALU.mult),
                lambda: V.tensor_reduce(gate, tb[:, :, :], X, ALU.add),
                lambda: V.tensor_tensor(gate, gate, gate2, ALU.add))
            with nc.Block() as block:
                @block.scalar
                def _(act):
                    scalar_did.did(A.activation(gate, gate, ACT.Exp, scale=-1.0))
            vector_block(
                lambda: V.tensor_scalar(gate, gate, 1.0, None, ALU.add),
                lambda: V.reciprocal(gate, gate),
                lambda: V.tensor_tensor(tb[:, :, :], skip, ta[:, :, :], ALU.subtract),
                lambda: V.tensor_tensor(tb[:, :, :], tb[:, :, :], spread(gate, 2, D), ALU.mult),
                lambda: V.tensor_tensor(tb[:, :, :], tb[:, :, :], ta[:, :, :], ALU.add))
            node_sum(tb[:, :, :])
            vector_block(
                lambda: V.tensor_scalar(col[:, 2, :], ps[:, 0, 0:D], 1.0 / N, None, ALU.mult),
                lambda: V.tensor_tensor(ta[:, :, :], tb[:, :, :], spread(col[:, 2, :], 1, T), ALU.subtract),
                lambda: V.tensor_tensor(tb[:, :, :], ta[:, :, :], ta[:, :, :], ALU.mult))
            node_sum(tb[:, :, :])
            with nc.Block() as block:
                @block.scalar
                def _(act):
                    scalar_did.did(A.activation(col[:, 3, :], ps[:, 0, 0:D], ACT.Sqrt, bias=eps_ln[:, 0:1], scale=1.0 / N))
            vector_block(
                lambda: V.reciprocal(col[:, 3, :], col[:, 3, :]),
                lambda: V.tensor_tensor(col[:, 3, :], col[:, 3, :], v_gate[:, l, 3 * D:4 * D], ALU.mult),
                lambda: V.tensor_tensor(ta[:, :, :], ta[:, :, :], spread(col[:, 3, :], 1, T), ALU.mult),
                lambda: V.tensor_tensor(ta[:, :, :], ta[:, :, :], spread(v_gate[:, l, 4 * D:5 * D], 1, T), ALU.add),
                lambda: V.scalar_tensor_tensor(out=h_all[:, :, :], in0=ta[:, :, :], scalar=0.0, in1=h_all[:, :, :],
                                               op0=ALU.max, op1=ALU.add))
        add_to_x(h_all[:, :, :])

        layer_norm(h_all[:, :, :], x_all[:, :, :], relu=True)
        project(flat(h_all[:, :, :]), w["Wn"][:, :], vec["bn"][:, :], h_tile, D)
        sums = sums_of(1, 1)
        for l in range(L3_LAYERS):
            W3 = 3 * D
            n_table = 2 + L2_LAYERS + l
            project(flat(h_all[:, :, :]), w_in[:, 0:3 * D], b_in[:, 0:3 * D],
                    lambda t: stage[:, bass.ds(t * W3, W3)], W3, table=tables[n_table], width=W3,
                    afterwards=clear_sums)
            attention(tables[n_table], W3, 1, "plain", out_of_L3(l) + (into_L3(l + 1) if l + 1 < L3_LAYERS else []))
            vector_block(
                lambda: V.tensor_scalar(sm[:, 0, :], sums[:, :, 0, D], 1e-30, None, ALU.max),
                lambda: V.reciprocal(sm[:, 0, :], sm[:, 0, :]),
                lambda: V.tensor_tensor(ta[:, :, :], sums[:, :, 0, 0:D], spread(sm[:, 0, :], 2, D), ALU.mult))
            project(flat(ta[:, :, :]), w_out[:, :], v_out[:, 0:D], a_tile, D,
                    plus=flat(h_all[:, :, :]), dst=flat(ta[:, :, :]), stats=True)
            layer_norm(h_all[:, :, :], h_all[:, :, :], gamma=v_out[:, D:2 * D], beta=v_out[:, 2 * D:3 * D],
                       stats_at=(l + 1) * T)
        project(flat(h_all[:, :, :]), w["Wout"][:, :], vec["bout"][:, :], a_tile, D, table=out,
                plus=flat(x_all[:, :, :]), dst=flat(ta[:, :, :]))


_INS = ["x", "src", "dst", "edge_weight1"] + [f"L1_gnn_{n}" for n in ("W", "att_src", "att_dst", "bias", "gamma", "beta")] + [
    f"L2_gnn_{n}" for n in ("W_in", "b_in", "Wq", "bq", "Wk", "bk", "Wv", "bv", "We", "Wskip", "bskip", "Wbeta",
                            "bn_gamma", "bn_beta")] + [
    f"L3_gnn_{n}" for n in ("Wn", "bn", "WQ", "bQ", "WK", "bK", "WV", "bV", "WO", "bO", "ln_g", "ln_b", "Wout", "bout")]


def kernel(**inputs):
    import numpy as _np
    import concourse.bacc as _bacc
    from concourse import mybir as _mybir
    from concourse.bass_utils import run_bass_kernel_spmd as _run

    nc = _bacc.Bacc("TRN2", target_bir_lowering=False, num_devices=1)
    arrays, args = {}, {}
    for name in _INS:
        arr = _np.ascontiguousarray(inputs[name])
        arrays[f"in_{name}"] = arr
        args[name] = nc.dram_tensor(f"in_{name}", arr.shape, _mybir.dt.from_np(arr.dtype), kind="ExternalInput").ap()
    shape = tuple(inputs["x"].shape)
    out = nc.dram_tensor("out_x", shape, _mybir.dt.float32, kind="ExternalOutput").ap()
    program(nc, args, out)
    r = _run(nc, [arrays], core_ids=[0])
    return r.results[0]["out_x"]
```
